# Optimizing a Trainium2 kernel written in Bass

```python
import numpy as np
import jax
import jax.numpy as jnp

def _softmax(x, axis=-1):
    return jax.nn.softmax(x, axis=axis)

def _gelu(x):
    return jax.nn.gelu(x, approximate=True)

def _silu(x):
    return jax.nn.silu(x)

def _sigmoid(x):
    return jax.nn.sigmoid(x)

def _layernorm(x, axis=-1, eps=1e-05):
    m = jnp.mean(x, axis=axis, keepdims=True)
    v = jnp.var(x, axis=axis, keepdims=True)
    return (x - m) / jnp.sqrt(v + eps)

def _scatter_add(tgt, idx, src, axis=0):
    return tgt.at[idx].add(src)

def _segment_sum(src, seg, n):
    return jax.ops.segment_sum(src, seg, n)
kernel_name = 'mk_sandwich_d1_jaxref_r8_a65bbf'

def setup_inputs(seed: int=0):
    np.random.seed(seed)
    _w = jnp.asarray

    def _L0_attn_setup():
        import math
        import jax, jax.numpy as jnp
        import numpy as np
        D_MODEL = 256
        NUM_HEADS = 16
        D_HEAD = D_MODEL // NUM_HEADS
        THETA = 10000.0

        def _rope_tables(seq_len, d_head):
            idx = jnp.arange(0, d_head, 2, dtype=jnp.float32)
            inv_freq = THETA ** (-idx / d_head)
            angles = jnp.arange(seq_len, dtype=jnp.float32)[:, None] * inv_freq[None, :]
            return (jnp.cos(angles), jnp.sin(angles))

        def _apply_rope(x, cos, sin):
            B, H, S, d = x.shape
            xp = x.reshape(B, H, S, d // 2, 2)
            xe, xo = (xp[..., 0], xp[..., 1])
            rot = jnp.stack([xe * cos - xo * sin, xe * sin + xo * cos], axis=-1)
            return rot.reshape(B, H, S, d)
        key = jax.random.key(seed)
        k_x, k_q, k_k, k_v, k_o = jax.random.split(key, 5)
        std = math.sqrt(2.0 / (D_MODEL + D_MODEL))
        x = jax.random.normal(k_x, (4, 256, D_MODEL), dtype=jnp.float32)
        Wq = jax.random.normal(k_q, (D_MODEL, D_MODEL), dtype=jnp.float32) * std
        Wk = jax.random.normal(k_k, (D_MODEL, D_MODEL), dtype=jnp.float32) * std
        Wv = jax.random.normal(k_v, (D_MODEL, D_MODEL), dtype=jnp.float32) * std
        Wo = jax.random.normal(k_o, (D_MODEL, D_MODEL), dtype=jnp.float32) * std
        return {'x': x, 'Wq': Wq, 'Wk': Wk, 'Wv': Wv, 'Wo': Wo}
    _L0_attn_in = _L0_attn_setup()

    def _L0_ffn_setup():
        import jax, jax.numpy as jnp
        import numpy as np
        B, S, H = (4, 128, 256)
        E, K, I, SI = (16, 4, 176, 704)

        def _silu_mul(gu, inter):
            return jax.nn.silu(gu[:, :inter]) * gu[:, inter:]
        key = jax.random.key(seed)
        ks = jax.random.split(key, 7)
        s = 0.02
        return {'hidden_states': jax.random.normal(ks[0], (B, S, H), jnp.float32), 'gate_w': jax.random.normal(ks[1], (E, H), jnp.float32) * s, 'expert_gate_up': jax.random.normal(ks[2], (E, 2 * I, H), jnp.float32) * s, 'expert_down': jax.random.normal(ks[3], (E, H, I), jnp.float32) * s, 'shared_gate_up': jax.random.normal(ks[4], (2 * SI, H), jnp.float32) * s, 'shared_down': jax.random.normal(ks[5], (H, SI), jnp.float32) * s, 'shared_gate_vec': jax.random.normal(ks[6], (1, H), jnp.float32) * s}
    _L0_ffn_in = _L0_ffn_setup()
    _d = {'L0_attn_x': _L0_attn_in['x'], 'L0_attn_Wq': _L0_attn_in['Wq'], 'L0_attn_Wk': _L0_attn_in['Wk'], 'L0_attn_Wv': _L0_attn_in['Wv'], 'L0_attn_Wo': _L0_attn_in['Wo'], 'L0_ffn_gate_w': _L0_ffn_in['gate_w'], 'L0_ffn_expert_gate_up': _L0_ffn_in['expert_gate_up'], 'L0_ffn_expert_down': _L0_ffn_in['expert_down'], 'L0_ffn_shared_gate_up': _L0_ffn_in['shared_gate_up'], 'L0_ffn_shared_down': _L0_ffn_in['shared_down'], 'L0_ffn_shared_gate_vec': _L0_ffn_in['shared_gate_vec']}
    _x0 = _d['L0_attn_x']
    _d['L0_attn_x'] = jax.random.normal(jax.random.fold_in(jax.random.key(seed), 1), (4, 512, 256), dtype=_x0.dtype)
    del _x0
    return _d

def reference(L0_attn_x, L0_attn_Wq, L0_attn_Wk, L0_attn_Wv, L0_attn_Wo, L0_ffn_gate_w, L0_ffn_expert_gate_up, L0_ffn_expert_down, L0_ffn_shared_gate_up, L0_ffn_shared_down, L0_ffn_shared_gate_vec):

    def _L0_attn_ref(x, Wq, Wk, Wv, Wo):
        import math
        import jax, jax.numpy as jnp
        import numpy as np
        D_MODEL = 256
        NUM_HEADS = 16
        D_HEAD = D_MODEL // NUM_HEADS
        THETA = 10000.0

        def _rope_tables(seq_len, d_head):
            idx = jnp.arange(0, d_head, 2, dtype=jnp.float32)
            inv_freq = THETA ** (-idx / d_head)
            angles = jnp.arange(seq_len, dtype=jnp.float32)[:, None] * inv_freq[None, :]
            return (jnp.cos(angles), jnp.sin(angles))

        def _apply_rope(x, cos, sin):
            B, H, S, d = x.shape
            xp = x.reshape(B, H, S, d // 2, 2)
            xe, xo = (xp[..., 0], xp[..., 1])
            rot = jnp.stack([xe * cos - xo * sin, xe * sin + xo * cos], axis=-1)
            return rot.reshape(B, H, S, d)
        B, S, D = x.shape
        H, dh = (NUM_HEADS, D_HEAD)

        def proj(W):
            y = jnp.einsum('bsi,oi->bso', x, W)
            return y.reshape(B, S, H, dh).transpose(0, 2, 1, 3)
        q, k, v = (proj(Wq), proj(Wk), proj(Wv))
        cos, sin = _rope_tables(S, dh)
        q = _apply_rope(q, cos, sin)
        k = _apply_rope(k, cos, sin)
        scores = jnp.einsum('bhqd,bhkd->bhqk', q.astype(jnp.float32), k.astype(jnp.float32)) / math.sqrt(dh)
        causal = jnp.tril(jnp.ones((S, S), dtype=bool))
        scores = jnp.where(causal, scores, jnp.finfo(jnp.float32).min)
        probs = jax.nn.softmax(scores, axis=-1).astype(v.dtype)
        attn = jnp.einsum('bhqk,bhkd->bhqd', probs, v)
        attn = attn.transpose(0, 2, 1, 3).reshape(B, S, D)
        return jnp.einsum('bsi,oi->bso', attn, Wo)

    def _L0_ffn_ref(hidden_states, gate_w, expert_gate_up, expert_down, shared_gate_up, shared_down, shared_gate_vec):
        import jax, jax.numpy as jnp
        import numpy as np
        B, S, H = (4, 128, 256)
        E, K, I, SI = (16, 4, 176, 704)

        def _silu_mul(gu, inter):
            return jax.nn.silu(gu[:, :inter]) * gu[:, inter:]
        orig_shape = hidden_states.shape
        x = hidden_states.reshape(-1, H)
        router_logits = x @ gate_w.T
        routing_probs = jax.nn.softmax(router_logits.astype(jnp.float32), axis=-1)
        topk_w, topk_idx = jax.lax.top_k(routing_probs, K)
        topk_w = topk_w / topk_w.sum(axis=-1, keepdims=True)
        topk_w = topk_w.astype(x.dtype)
        combine = (jax.nn.one_hot(topk_idx, E, dtype=x.dtype) * topk_w[..., None]).sum(1)
        shared = _silu_mul(x @ shared_gate_up.T, SI) @ shared_down.T
        shared = shared * jax.nn.sigmoid(x @ shared_gate_vec.T)

        def step(acc, ew):
            w_gu, w_d, cw = ew
            h = _silu_mul(x @ w_gu.T, I)
            return (acc + h @ w_d.T * cw[:, None], None)
        acc0 = jnp.zeros_like(x)
        sparse, _ = jax.lax.scan(step, acc0, (expert_gate_up, expert_down, combine.T))
        return (shared + sparse).reshape(orig_shape)
    x = L0_attn_x
    x = x + _layernorm(_L0_attn_ref(_layernorm(x, axis=-1), L0_attn_Wq, L0_attn_Wk, L0_attn_Wv, L0_attn_Wo), axis=-1)
    x = x + _layernorm(_L0_ffn_ref(_layernorm(x, axis=-1), L0_ffn_gate_w, L0_ffn_expert_gate_up, L0_ffn_expert_down, L0_ffn_shared_gate_up, L0_ffn_shared_down, L0_ffn_shared_gate_vec), axis=-1)
    return x

_drawn_inputs = setup_inputs


def setup_inputs(seed=0):
    import zlib

    import numpy as np

    out = dict(_drawn_inputs(seed))
    spreads = {}
    factors = {}
    for name, (base, spread) in spreads.items():
        noise = np.random.default_rng([zlib.crc32(name.encode()), seed]).standard_normal(out[name].shape)
        drawn = base * np.exp(spread * noise) if base else spread * noise
        out[name] = jnp.asarray(drawn.astype(out[name].dtype))
    for name, factor in factors.items():
        out[name] = (out[name] * factor).astype(out[name].dtype)
    return out
```

```python
from contextlib import ExitStack

import concourse.bass as bass
from concourse import mybir

P = 128
B, S, D = 4, 512, 256
H, DH = 16, 16
TB = S // P
NT = B * TB
KT = D // P
E, K, I, SI = 16, 4, 176, 704
EPS = 1e-5
SLOTS = 6
SR = SLOTS * DH
MR = 3
QR = SR + MR
OCT = 8
QUAD = 4
FT = -(-(E * I + SI) // P)
CH = 7
NCH = FT // CH
GC = E + 1
NEG = -1e30

ALU = mybir.AluOpType
ACT = mybir.ActivationFunctionType
AX = mybir.AxisListType
F32 = mybir.dt.float32
F32R = mybir.dt.float32r
BF16 = mybir.dt.bfloat16

Q_HI, Q_MID, Q_LOW = slice(0, 3), slice(3, 6, 2), 4
K_HI, K_MID, K_LOW = slice(2, 5), slice(0, 6, 5), 1
SLOT_HI, SLOT_MID = 2, 5

ORDER = [("turn", 0), ("turn", 1), ("qkv", 0), ("turn", 2), ("qkv", 1), ("split", 0), ("stack", 0),
         ("turn", 3), ("qkv", 2), ("split", 1), ("stack", 1), ("qkv", 3), ("split", 2), ("stack", 2),
         ("split", 3), ("stack", 3),
         ("max", 0), ("max", 1), ("mturn", 0), ("attend", 0), ("mturn", 1), ("attend", 1),
         ("norm", 0), ("attend", 2), ("norm", 1), ("attend", 3), ("norm", 2), ("norm", 3), ("turn1", 0)]
TAIL = ["wo", "turn2", "router", "lturn", "cturn"]
MAXU = [(0, 0, 8, 4), (1, 0, 4, 2), (1, 4, 4, 2)] + [(i, h, 2, 1) for i in (2, 3) for h in range(0, OCT, 2)]
SCU = [(0, 0, 2), (0, 2, 2), (1, 0, 2), (1, 2, 2), (2, 0, 4), (3, 0, 4)]
SC_LAST = [1, 3, 4, 5]
USERS = {"turn": ["AD"], "qkv": ["AD"], "stack": ["A", "D"], "max": ["D"] * len(MAXU), "mturn": ["A"],
         "attend": ["A"] * len(SCU), "wo": ["D", "D"], "turn2": ["AD"], "router": ["A"], "lturn": ["D"],
         "cturn": ["A"], "split": [], "norm": ["D"], "turn1": ["AD"]}
RING = 3


def plan_units():
    first, act, dve = {}, [], []
    a = d = 0
    for stage in ORDER + [(name, 0) for name in TAIL]:
        first[stage] = len(act)
        for who in USERS[stage[0]]:
            a += "A" in who
            d += "D" in who
            act.append(a)
            dve.append(d)
    users = [who for stage in ORDER + [(name, 0) for name in TAIL] for who in USERS[stage[0]]]
    return first, act, dve, users


FIRST, ACT_UPTO, DVE_UPTO, UNIT_USERS = plan_units()
UNITS = len(UNIT_USERS)
ACT_UNITS, DVE_UNITS = ACT_UPTO[-1], DVE_UPTO[-1]
assert UNITS % RING == 0


def apart(eng):
    eng.nop(nofuse=True)


class Steps:

    def __init__(self, engine, sem, per_turn, turn):
        self.engine, self.sem, self.per_turn, self.turn, self.n = engine, sem, per_turn, turn, 0

    def add(self, ins):
        self.n += 1
        ins.then_inc(self.sem, 1)

    def wait(self):
        self.engine.wait_ge(self.sem, self.turn * self.per_turn + self.n)


DVE_STEPS = 52


def attention_block(nc, t, x_in, wqkv_in, wo_in, gw_in, rope_in):
    with ExitStack() as ctx:
        def sb(name, shape, dt=F32):
            return ctx.enter_context(nc.sbuf_tensor(name, shape, dt))

        def sem(name):
            return ctx.enter_context(nc.semaphore(name))

        ring = ctx.enter_context(nc.psum_tensor("ring", [P, RING, 2, 512], F32))
        ring16 = ring[:].rearrange("p r b n -> p r (b n)").bitcast(BF16)
        att_ps = ctx.enter_context(nc.psum_tensor("att_ps", [P, 2, 512], F32))

        ident = sb("ident", [P, P])
        ident16 = sb("ident16", [P, P], BF16)
        causal = sb("causal", [P, P], BF16)
        lower = sb("lower", [P, E, E], BF16)
        rope = sb("rope", [P, TB, 2, DH])
        wqkv_hi = sb("wqkv_hi", [P, KT, 3 * D], F32R)
        wqkv_lo = sb("wqkv_lo", [P, KT, 3 * D], F32R)
        wo_hi = sb("wo_hi", [P, KT, D], F32R)
        wo_lo = sb("wo_lo", [P, KT, D], F32R)
        gw_hi = sb("gw_hi", [P, KT, P], F32R)
        gw_lo = sb("gw_lo", [P, KT, P], F32R)
        probs = sb("probs", [P, 4, 1024])
        QT = sb("QT", [P, H, S], BF16)
        KTt = sb("KTt", [P, H, S], BF16)
        V = sb("V", [P, TB, H, 2 * DH])
        xn = sb("xn", [P, TB, D])
        xT_hi = sb("xT_hi", [P, 2, KT, P], F32R)
        xT_lo = sb("xT_lo", [P, 2, KT, P], F32R)
        cosd = sb("cosd", [P, 2, 2 * D])
        sind = sb("sind", [P, 2, 2 * D])
        rot = sb("rot", [P, 2, 2 * D])
        rest = sb("rest", [P, 2, 2 * D])
        stack = sb("stack", [P, 2, 2 * H, SR], BF16)
        nmax = sb("nmax", [P, TB, H])
        nrest = sb("nrest", [P, TB, H])
        nparts = sb("nparts", [P, TB, H // OCT, MR, OCT], BF16)
        nT = sb("nT", [MR * OCT, 2, S], BF16)
        att = sb("att", [P, 2, S])
        rsum = sb("rsum", [P, 2, TB, QUAD])
        attn = sb("attn", [P, TB, D])
        attT_hi = sb("attT_hi", [P, KT, S], F32R)
        attT_lo = sb("attT_lo", [P, KT, S], F32R)
        stats = sb("stats", [P, TB, 6])
        mv = sb("mv", [P, TB, 2])
        ve = sb("ve", [P, TB])
        rs = sb("rs", [P, TB])
        nw = sb("nw", [P, TB])
        logT = sb("logT", [P, S])
        logit = sb("logit", [P, TB, GC])
        eprob = sb("eprob", [P, TB, GC])
        prob = sb("prob", [P, TB, E])
        small = sb("small", [P, 4, TB])
        above = sb("above", [P, TB * E * E], BF16)
        equal = sb("equal", [P, TB * E * E], BF16)
        rank = sb("rank", [P, TB, E])
        comb = sb("comb", [P, TB, GC])
        crest = sb("crest", [P, TB, GC])
        cparts = sb("cparts", [P, TB, P], BF16)

        x_in_sem = sem("x_in_sem")
        const_in = sem("const_in")
        wstage_in = sem("wstage_in")
        pool_const = sem("pool_const")
        ones_set = sem("ones_set")
        w_hi = sem("w_hi")
        w_lo = sem("w_lo")
        dve_step = sem("dve_step")
        norm_var = sem("norm_var")
        norm_ln = sem("norm_ln")
        norm_y = sem("norm_y")
        xn_ready = sem("xn_ready")
        unit_ready = sem("unit_ready")
        act_units = sem("act_units")
        dve_units = sem("dve_units")
        roped = sem("roped")
        q_hi_ready = sem("q_hi_ready")
        q_mid_ready = sem("q_mid_ready")
        stack_ready = sem("stack_ready")
        nparts_ready = sem("nparts_ready")
        nrows_in = [sem(f"nrows_in{g}") for g in range(2)]
        masked = sem("masked")
        pv_done = sem("pv_done")
        att_copied = sem("att_copied")
        xn2_ready = sem("xn2_ready")
        logT_ready = sem("logT_ready")
        logit_ready = sem("logit_ready")
        lcent = sem("lcent")
        exp_ready = sem("exp_ready")
        cparts_ready = sem("cparts_ready")

        block = ctx.enter_context(nc.Block())
        wstage = probs[:].rearrange("p a n -> p (a n)")
        ws_qkv = wstage[:, 0:KT * 3 * D].rearrange("p (k n) -> p k n", k=KT)
        ws_wo = wstage[:, KT * 3 * D:KT * 4 * D].rearrange("p (k n) -> p k n", k=KT)
        ws_gw = wstage[:, KT * 4 * D:KT * 4 * D + KT * P].rearrange("p (k n) -> p k n", k=KT)

        def unit(stage, n=0):
            return (FIRST[stage] + n) % RING

        def wait_unit(eng, b, stage, n=0):
            eng.wait_ge(unit_ready, b * UNITS + FIRST[stage] + n + 1)

        def head_pairs(ap):
            return ap.rearrange("p (h i e) -> p h i e", i=DH // 2, e=2)

        @block.sync
        def _(sp):
            sp.dma_start(t["x"][:, 0:TB, :], x_in[:, 0:TB, :]).then_inc(x_in_sem, 16)
            sp.dma_start(ws_qkv, wqkv_in).then_inc(wstage_in, 16)
            sp.dma_start(rope[:], rope_in).then_inc(const_in, 16)
            sp.dma_start(ws_wo, wo_in).then_inc(wstage_in, 16)
            sp.dma_start(ws_gw, gw_in).then_inc(wstage_in, 16)
            for c in range(1, B):
                sp.wait_ge(x_in_sem, c * 16)
                sp.dma_start(t["x"][:, c * TB:(c + 1) * TB, :],
                             x_in[:, c * TB:(c + 1) * TB, :]).then_inc(x_in_sem, 16)
            with sp.Fori(0, B) as b:
                for g in range(2):
                    sp.wait_ge(act_units, b * ACT_UNITS + ACT_UPTO[FIRST[("mturn", g)]])
                    for part in range(MR):
                        sp.dma_start(QT[SR + part:SR + part + 1, g * OCT:(g + 1) * OCT, :],
                                     nT[part * OCT:(part + 1) * OCT, g, :]).then_inc(nrows_in[g], 16)

        @block.gpsimd
        def _(pool):
            pool.memset(ident[:], 1.0).then_inc(pool_const, 1)
            pool.memset(causal[:], 0.0).then_inc(pool_const, 1)
            pool.memset(lower[:], 1.0).then_inc(pool_const, 1)
            pool.memset(V[:, :, :, DH:2 * DH], 1.0).then_inc(ones_set, 1)
            pool.memset(cparts[:], 0.0).then_inc(ones_set, 1)
            pool.wait_ge(ones_set, 2)
            pool.memset(KTt[SR:P, :, :], 1.0).then_inc(ones_set, 1)
            pool.wait_ge(ones_set, 3)
            pool.wait_ge(pool_const, 3)
            pool.affine_select(out=ident[:], in_=ident[:], pattern=[[1, P]], compare_op=ALU.is_equal, fill=0.0,
                               base=0, channel_multiplier=-1).then_inc(pool_const, 1)
            pool.affine_select(out=causal[:], in_=causal[:], pattern=[[-1, P]], compare_op=ALU.is_ge, fill=NEG,
                               base=0, channel_multiplier=1).then_inc(pool_const, 1)
            pool.affine_select(out=lower[:], in_=lower[:], pattern=[[1, E], [-1, E]], compare_op=ALU.is_gt, fill=0.0,
                               base=0, channel_multiplier=0).then_inc(pool_const, 1)
            pool.wait_ge(pool_const, 6)
            pool.tensor_copy(ident16[:], ident[:]).then_inc(pool_const, 1)

            with pool.Fori(0, B) as b:
                for kind, n in ORDER:
                    if kind == "qkv":
                        pool.wait_ge(dve_units, b * DVE_UNITS + DVE_UPTO[FIRST[(kind, n)]])
                        pool.tensor_tensor(rot[:, n % 2, :], cosd[:, n % 2, :], sind[:, n % 2, :],
                                           ALU.add).then_inc(roped, 1)
                    elif kind == "split":
                        pool.wait_ge(q_mid_ready, 2 * (b * TB + n + 1))
                        r = rest[:, n % 2, :].rearrange("p (h d) -> p h d", d=DH)
                        sk = stack[:, n % 2].rearrange("p h (s d) -> p h s d", d=DH)
                        pool.tensor_tensor(sk[:, 0:H, Q_LOW, :], r[:, 0:H, :], sk[:, 0:H, SLOT_MID, :],
                                           ALU.subtract).then_inc(stack_ready, 1)
                        pool.tensor_tensor(sk[:, H:2 * H, K_LOW, :], r[:, H:2 * H, :], sk[:, H:2 * H, SLOT_MID, :],
                                           ALU.subtract).then_inc(stack_ready, 1)
                    elif kind == "attend":
                        for u, (j, h0, nh) in enumerate(SCU):
                            pool.wait_ge(act_units, b * ACT_UNITS + ACT_UPTO[FIRST[(kind, n)] + u])
                            apart(pool)
                            w = S - j * P
                            slot = (n * len(SCU) + u) % 4
                            stride = 512 if j == 0 else w
                            p = probs[:, slot, 0:nh * stride].rearrange("p (h n) -> p h n", h=nh)[:, :, 0:P]
                            pool.affine_select(out=p, in_=p, pattern=[[0, nh], [1, P]], compare_op=ALU.is_ge,
                                               fill=0.0, base=0, channel_multiplier=-1).then_inc(masked, 1)

        @block.scalar
        def _(act):
            act.wait_ge(wstage_in, 48)
            nc.scalar.copy(wqkv_hi[:], ws_qkv).then_inc(w_hi, 1)
            nc.scalar.copy(wo_hi[:], ws_wo).then_inc(w_hi, 1)
            nc.scalar.copy(gw_hi[:], ws_gw).then_inc(w_hi, 1)
            act.wait_ge(w_lo, 3)
            act.wait_ge(ones_set, 3)

            def norm_root(b, k):
                act.wait_ge(norm_var, b * 3 + k + 1)
                nc.scalar.activation(nw[:], ve[:], ACT.Ln).then_inc(norm_ln, 1)
                act.wait_ge(norm_ln, b * 3 + k + 1)
                nc.scalar.activation(rs[:], nw[:], ACT.Exp, scale=-0.5).then_inc(norm_y, 1)

            def copy_att(b, n):
                act.wait_ge(pv_done, (b * QUAD + n + 1) * TB)
                if n >= 2:
                    wait_unit(act, b, ("norm", n - 2))
                nc.scalar.copy(att[:, n % 2, :], att_ps[:, n % 2, :]).then_inc(att_copied, 1)

            with act.Fori(0, B) as b:
                norm_root(b, 0)
                for kind, n in ORDER:
                    st = (kind, n)
                    if kind == "turn":
                        wait_unit(act, b, st)
                        nc.scalar.copy(xT_hi[:, n % 2], ring[:, unit(st), 0, 0:KT * P].rearrange(
                            "p (k n) -> p k n", k=KT)).then_inc(act_units, 1)
                    elif kind == "qkv":
                        wait_unit(act, b, st)
                        nc.scalar.copy(V[:, n, :, 0:DH], ring[:, unit(st), 1, 0:D].rearrange(
                            "p (h d) -> p h d", d=DH)).then_inc(act_units, 1)
                        act.wait_ge(roped, b * TB + n + 1)
                        if n >= 2:
                            wait_unit(act, b, ("stack", n - 2), 1)
                        r = rot[:, n % 2, :].rearrange("p (h d) -> p h d", d=DH)
                        sk = stack[:, n % 2].rearrange("p h (s d) -> p h s d", d=DH)
                        for a, where in ((0, Q_HI), (H, K_HI)):
                            src = r[:, a:a + H, :].unsqueeze(2).to_broadcast([P, H, 3, DH])
                            nc.scalar.copy(sk[:, a:a + H, where, :], src).then_inc(q_hi_ready, 1)
                    elif kind == "stack":
                        wait_unit(act, b, st)
                        nc.scalar.copy(QT[0:SR, :, n * P:(n + 1) * P], ring16[0:SR, unit(st), :].rearrange(
                            "p (h n) -> p h n", h=H)).then_inc(act_units, 1)
                    elif kind == "mturn":
                        wait_unit(act, b, st)
                        nc.scalar.copy(nT[:, n, :], ring16[0:MR * OCT, unit(st), 0:S]).then_inc(act_units, 1)
                    elif kind == "attend":
                        for u, (j, h0, nh) in enumerate(SCU):
                            wait_unit(act, b, st, u)
                            w = S - j * P
                            m = n * len(SCU) + u
                            old = m - 4
                            if old >= 0:
                                act.wait_ge(pv_done, b * QUAD * TB + (old // len(SCU)) * TB
                                            + SCU[old % len(SCU)][0] + 1)
                            src = ring[:, unit(st, u)]
                            if j == 1:
                                src = src[:, :, 0:w]
                                dst = probs[:, m % 4, 0:nh * w].rearrange("p (h n) -> p h n", h=nh)
                            else:
                                src = src.rearrange("p b n -> p (b n)")[:, 0:nh * w]
                                dst = probs[:, m % 4, 0:nh * w]
                            nc.scalar.activation(dst, src, ACT.Exp, scale=float(DH) ** -0.5).then_inc(act_units, 1)
                            if u == 2 and n > 0:
                                copy_att(b, n - 1)
                    elif kind == "norm" and n == QUAD - 1:
                        copy_att(b, n)
                    elif kind == "turn1":
                        wait_unit(act, b, st)
                        nc.scalar.copy(attT_hi[:], ring[:, unit(st)]).then_inc(act_units, 1)
                norm_root(b, 1)
                norm_root(b, 2)
                st = ("turn2", 0)
                wait_unit(act, b, st)
                nc.scalar.copy(t["x2T_hi"][:, :, bass.ds(b * S, S)], ring[:, unit(st)]).then_inc(act_units, 1)
                st = ("router", 0)
                wait_unit(act, b, st)
                nc.scalar.copy(logT[:], ring[:, unit(st), 0, :]).then_inc(act_units, 1)
                act.wait_ge(lcent, b + 1)
                nc.scalar.activation(eprob[:, :, 0:E], eprob[:, :, 0:E], ACT.Exp).then_inc(exp_ready, 1)
                nc.scalar.activation(eprob[:, :, E:GC], logit[:, :, E:GC], ACT.Exp, scale=-1.0).then_inc(exp_ready, 1)
                st = ("cturn", 0)
                wait_unit(act, b, st)
                nc.scalar.copy(t["combT"][:, bass.ds(b * S, S)], ring16[:, unit(st), 0:S]).then_inc(act_units, 1)

        @block.vector
        def _(dve):
            dve.wait_ge(w_hi, 3)
            nc.vector.tensor_tensor(wqkv_lo[:], ws_qkv, wqkv_hi[:].bitcast(F32), ALU.subtract).then_inc(w_lo, 1)
            nc.vector.tensor_tensor(wo_lo[:], ws_wo, wo_hi[:].bitcast(F32), ALU.subtract).then_inc(w_lo, 1)
            nc.vector.tensor_tensor(gw_lo[:], ws_gw, gw_hi[:].bitcast(F32), ALU.subtract).then_inc(w_lo, 1)
            dve.wait_ge(const_in, 16)
            dve.wait_ge(pool_const, 7)
            dve.wait_ge(ones_set, 3)
            x_all = t["x"]

            with dve.Fori(0, B) as b:
                step = Steps(dve, dve_step, DVE_STEPS, b)

                def norm_scale(k, sources):
                    apart(dve)
                    for s in range(TB):
                        ins = nc.vector.bn_stats(stats[:, s, :], sources[s])
                    step.add(ins)
                    step.wait()
                    apart(dve)
                    for s in range(TB):
                        ins = nc.vector.bn_aggr(mv[:, s, :], stats[:, s, :])
                    step.add(ins)
                    step.wait()
                    nc.vector.tensor_scalar(ve[:], mv[:, :, 1], EPS, None, ALU.add).then_inc(norm_var, 1)
                    dve.wait_ge(norm_y, b * 3 + k + 1)
                    step.add(nc.vector.tensor_tensor(nw[:], rs[:], rs[:], ALU.mult))
                    step.wait()
                    step.add(nc.vector.tensor_tensor(nw[:], nw[:], ve[:], ALU.mult))
                    step.wait()
                    step.add(nc.vector.tensor_scalar(nw[:], nw[:], -0.5, 1.5, ALU.mult, ALU.add))
                    step.wait()
                    step.add(nc.vector.tensor_tensor(rs[:], rs[:], nw[:], ALU.mult))
                    step.wait()

                dve.wait_ge(x_in_sem, (b + 1) * 16)
                norm_scale(0, [x_all[:, bass.ds(b * TB + s, 1), :].rearrange("p o n -> p (o n)") for s in range(TB)])
                for s in range(TB):
                    nc.vector.tensor_scalar(xn[:, s, :],
                                            x_all[:, bass.ds(b * TB + s, 1), :].rearrange("p o n -> p (o n)"),
                                            mv[:, s, 0:1], rs[:, s:s + 1], ALU.subtract,
                                            ALU.mult).then_inc(xn_ready, 1)
                for kind, n in ORDER:
                    st = (kind, n)
                    if kind == "turn":
                        dve.wait_ge(act_units, b * ACT_UNITS + ACT_UPTO[FIRST[st]])
                        nc.vector.tensor_tensor(xT_lo[:, n % 2], ring[:, unit(st), 0, 0:KT * P].rearrange(
                            "p (k n) -> p k n", k=KT), xT_hi[:, n % 2].bitcast(F32), ALU.subtract
                        ).then_inc(dve_units, 1)
                    elif kind == "qkv":
                        wait_unit(dve, b, st)
                        if n >= 2:
                            dve.wait_ge(roped, b * TB + n - 1)
                        qk = head_pairs(ring[:, unit(st), 0, :])
                        cos = head_pairs(rope[:, n, 0, :])
                        sin = head_pairs(rope[:, n, 1, :])
                        wide = [P, 2 * H, DH // 2]
                        nc.vector.tensor_tensor(
                            cosd[:, n % 2, :].rearrange("p (h d) -> p h d", d=DH),
                            ring[:, unit(st), 0, :].rearrange("p (h d) -> p h d", d=DH),
                            rope[:, n, 0, :].unsqueeze(1).to_broadcast([P, 2 * H, DH]), ALU.mult)
                        sd = head_pairs(sind[:, n % 2, :])
                        for e in range(2):
                            ins = nc.vector.tensor_tensor(sd[:, :, :, e], qk[:, :, :, 1 - e],
                                                          sin[:, :, :, e].to_broadcast(wide), ALU.mult)
                        ins.then_inc(dve_units, 1)
                    elif kind == "split":
                        dve.wait_ge(q_hi_ready, 2 * (b * TB + n + 1))
                        r = rest[:, n % 2, :].rearrange("p (h d) -> p h d", d=DH)
                        sk = stack[:, n % 2].rearrange("p h (s d) -> p h s d", d=DH)
                        step.add(nc.vector.tensor_tensor(r, rot[:, n % 2, :].rearrange("p (h d) -> p h d", d=DH),
                                                         sk[:, :, SLOT_HI, :], ALU.subtract))
                        step.wait()
                        for a, where in ((0, Q_MID), (H, K_MID)):
                            src = r[:, a:a + H, :].unsqueeze(2).to_broadcast([P, H, 2, DH])
                            nc.vector.tensor_copy(sk[:, a:a + H, where, :], src).then_inc(q_mid_ready, 1)
                    elif kind == "stack":
                        wait_unit(dve, b, st, 1)
                        nc.vector.tensor_copy(KTt[0:SR, :, n * P:(n + 1) * P], ring16[0:SR, unit(st, 1), :].rearrange(
                            "p (h n) -> p h n", h=H)).then_inc(dve_units, 1)
                    elif kind == "max":
                        for u, (i, h0, nh, hb) in enumerate(MAXU):
                            wait_unit(dve, b, st, u)
                            w = (i + 1) * P
                            src = ring[:, unit(st, u), :, 0:hb * w].rearrange("p b (h n) -> p b h n", h=hb)
                            h = n * OCT + h0
                            nc.vector.tensor_reduce(nmax[:, i, h:h + nh].rearrange("p (b h) -> p b h", h=hb), src,
                                                    AX.X, ALU.max, negate=True).then_inc(dve_units, 1)
                        o = slice(n * OCT, (n + 1) * OCT)
                        dve.wait_ge(dve_units, b * DVE_UNITS + DVE_UPTO[FIRST[st] + len(MAXU) - 1])
                        step.add(nc.vector.tensor_copy(nparts[:, :, n, 0, :], nmax[:, :, o]))
                        step.wait()
                        step.add(nc.vector.tensor_tensor(nrest[:, :, o], nmax[:, :, o], nparts[:, :, n, 0, :],
                                                         ALU.subtract))
                        step.wait()
                        step.add(nc.vector.tensor_copy(nparts[:, :, n, 1, :], nrest[:, :, o]))
                        step.wait()
                        nc.vector.tensor_tensor(nparts[:, :, n, 2, :], nrest[:, :, o], nparts[:, :, n, 1, :],
                                                ALU.subtract).then_inc(nparts_ready, 1)
                    elif kind == "norm":
                        wait_unit(dve, b, st)
                        o = ring[:, unit(st), 0, :].rearrange("p (s a d) -> p s a d", s=TB, a=QUAD)
                        step.add(nc.vector.reciprocal(rsum[:, n % 2], o[:, :, :, DH]))
                        step.wait()
                        nc.vector.tensor_tensor(
                            attn[:, :, n * QUAD * DH:(n + 1) * QUAD * DH].rearrange("p s (a d) -> p s a d", a=QUAD),
                            o[:, :, :, 0:DH], rsum[:, n % 2].unsqueeze(3).to_broadcast([P, TB, QUAD, DH]),
                            ALU.mult).then_inc(dve_units, 1)
                    elif kind == "turn1":
                        dve.wait_ge(act_units, b * ACT_UNITS + ACT_UPTO[FIRST[st]])
                        nc.vector.tensor_tensor(attT_lo[:], ring[:, unit(st)], attT_hi[:].bitcast(F32),
                                                ALU.subtract).then_inc(dve_units, 1)
                st = ("wo", 0)
                wait_unit(dve, b, st, 1)
                o_ps = [ring[:, unit(st, s // 2), s % 2, 0:D] for s in range(TB)]
                norm_scale(1, o_ps)
                step.add(nc.vector.scalar_tensor_tensor(out=small[:, 0, :], in0=mv[:, :, 0], scalar=-1.0, in1=rs[:],
                                                        op0=ALU.mult, op1=ALU.mult))
                for s in range(TB):
                    ins = nc.vector.scalar_tensor_tensor(
                        out=xn[:, s, :], in0=o_ps[s], scalar=rs[:, s:s + 1],
                        in1=x_all[:, bass.ds(b * TB + s, 1), :].rearrange("p o n -> p (o n)"),
                        op0=ALU.mult, op1=ALU.add)
                    if s % 2:
                        ins.then_inc(dve_units, 1)
                dve.wait_ge(dve_units, b * DVE_UNITS + DVE_UPTO[FIRST[st] + 1])
                step.wait()
                for s in range(TB):
                    ins = nc.vector.tensor_scalar(x_all[:, bass.ds(b * TB + s, 1), :].rearrange("p o n -> p (o n)"),
                                                  xn[:, s, :], small[:, 0, s:s + 1], None, ALU.add)
                step.add(ins)
                step.wait()
                norm_scale(2, [x_all[:, bass.ds(b * TB + s, 1), :].rearrange("p o n -> p (o n)") for s in range(TB)])
                for s in range(TB):
                    nc.vector.tensor_scalar(xn[:, s, :],
                                            x_all[:, bass.ds(b * TB + s, 1), :].rearrange("p o n -> p (o n)"),
                                            mv[:, s, 0:1], rs[:, s:s + 1], ALU.subtract,
                                            ALU.mult).then_inc(xn2_ready, 1)
                st = ("turn2", 0)
                dve.wait_ge(act_units, b * ACT_UNITS + ACT_UPTO[FIRST[st]])
                nc.vector.tensor_tensor(t["x2T_lo"][:, :, bass.ds(b * S, S)], ring[:, unit(st)],
                                        t["x2T_hi"][:, :, bass.ds(b * S, S)].bitcast(F32),
                                        ALU.subtract).then_inc(dve_units, 1)
                st = ("lturn", 0)
                wait_unit(dve, b, st)
                nc.vector.tensor_copy(logit[:], ring[:, unit(st), 0, :].rearrange(
                    "p (s n) -> p s n", s=TB)[:, :, 0:GC]).then_inc(dve_units, 1)
                dve.wait_ge(dve_units, b * DVE_UNITS + DVE_UPTO[FIRST[st]])
                wide = [P, TB, E]
                step.add(nc.vector.tensor_reduce(small[:, 1, :], logit[:, :, 0:E], AX.X, ALU.max))
                step.wait()
                nc.vector.tensor_tensor(eprob[:, :, 0:E], logit[:, :, 0:E], small[:, 1, :].unsqueeze(2).to_broadcast(
                    wide), ALU.subtract).then_inc(lcent, 1)
                dve.wait_ge(exp_ready, 2 * (b + 1))
                step.add(nc.vector.tensor_reduce(small[:, 2, :], eprob[:, :, 0:E], AX.X, ALU.add))
                step.add(nc.vector.tensor_scalar(crest[:, :, E], eprob[:, :, E], 1.0, None, ALU.add))
                step.wait()
                step.add(nc.vector.reciprocal(small[:, 1, :], small[:, 2, :]))
                step.add(nc.vector.reciprocal(comb[:, :, E], crest[:, :, E]))
                step.wait()
                step.add(nc.vector.tensor_tensor(prob[:], eprob[:, :, 0:E], small[:, 1, :].unsqueeze(2).to_broadcast(
                    wide), ALU.mult))
                step.wait()
                cube = [P, TB, E, E]
                ab = above[:].rearrange("p (s e f) -> p s e f", s=TB, e=E)
                eq = equal[:].rearrange("p (s e f) -> p s e f", s=TB, e=E)
                other = prob[:].unsqueeze(2).to_broadcast(cube)
                own = prob[:].unsqueeze(3).to_broadcast(cube)
                step.add(nc.vector.tensor_tensor(eq, other, own, ALU.is_equal))
                step.add(nc.vector.tensor_tensor(ab, other, own, ALU.is_gt))
                step.wait()
                step.add(nc.vector.tensor_tensor(equal[:].rearrange("p (s n) -> p s n", s=TB),
                                                 equal[:].rearrange("p (s n) -> p s n", s=TB),
                                                 lower[:].rearrange("p e f -> p (e f)").unsqueeze(1).to_broadcast(
                                                     [P, TB, E * E]), ALU.mult))
                step.wait()
                step.add(nc.vector.tensor_tensor(above[:], above[:], equal[:], ALU.add))
                step.wait()
                step.add(nc.vector.tensor_reduce(rank[:], ab, AX.X, ALU.add))
                step.wait()
                step.add(nc.vector.scalar_tensor_tensor(out=crest[:, :, 0:E], in0=rank[:], scalar=K - 0.5, in1=prob[:],
                                                        op0=ALU.is_lt, op1=ALU.mult))
                step.wait()
                step.add(nc.vector.tensor_reduce(small[:, 2, :], crest[:, :, 0:E], AX.X, ALU.add))
                step.wait()
                step.add(nc.vector.reciprocal(small[:, 3, :], small[:, 2, :]))
                step.wait()
                step.add(nc.vector.tensor_tensor(comb[:, :, 0:E], crest[:, :, 0:E],
                                                 small[:, 3, :].unsqueeze(2).to_broadcast(wide), ALU.mult))
                step.wait()
                step.add(nc.vector.tensor_copy(cparts[:, :, 0 * GC:1 * GC], comb[:]))
                step.wait()
                step.add(nc.vector.tensor_tensor(crest[:], comb[:], cparts[:, :, 0 * GC:1 * GC], ALU.subtract))
                step.wait()
                step.add(nc.vector.tensor_copy(cparts[:, :, 1 * GC:2 * GC], crest[:]))
                step.wait()
                nc.vector.tensor_tensor(cparts[:, :, 2 * GC:3 * GC], crest[:], cparts[:, :, 1 * GC:2 * GC],
                                        ALU.subtract).then_inc(cparts_ready, 1)
                assert step.n == DVE_STEPS, step.n

        @block.tensor
        def _(pe):
            pe.wait_ge(pool_const, 7)
            pe.wait_ge(ones_set, 3)
            pe.wait_ge(w_lo, 3)

            def values(b, n, j):
                pe.wait_ge(masked, b * QUAD * len(SCU) + n * len(SCU) + SC_LAST[j] + 1)
                if j == 0 and n >= 2:
                    pe.wait_ge(att_copied, b * QUAD + n - 1)
                w = S - j * P
                for a in range(QUAD):
                    u = next(u for u, (jj, h0, nh) in enumerate(SCU) if jj == j and h0 <= a < h0 + nh)
                    slot = (n * len(SCU) + u) % 4
                    o = (a - SCU[u][1]) * w
                    ins = nc.tensor.matmul(att_ps[32 * a:32 * a + 32, n % 2, j * P:S], V[:, j, n * QUAD + a, :],
                                           probs[:, slot, o:o + w], start=(j == 0), stop=(j == TB - 1))
                ins.then_inc(pv_done, 1)

            with pe.Fori(0, B) as b:
                def take(stage, n=0):
                    u = FIRST[stage] + n
                    v = u - RING
                    if v >= 0:
                        who, a, d = UNIT_USERS[v], ACT_UPTO[v], DVE_UPTO[v]
                        if "A" in who:
                            pe.wait_ge(act_units, b * ACT_UNITS + a)
                        if "D" in who:
                            pe.wait_ge(dve_units, b * DVE_UNITS + d)
                    return u % RING

                def products(out, left, right, first, last):
                    for i, (l, r) in enumerate(((0, 0), (0, 1), (1, 0))):
                        ins = nc.tensor.matmul(out, left[l], right[r], start=first and i == 0, stop=last and i == 2)
                    return ins

                for kind, n in ORDER:
                    st = (kind, n)
                    if kind == "turn":
                        pe.wait_ge(xn_ready, b * TB + n + 1)
                        r = take(st)
                        for k in range(KT):
                            ins = nc.tensor.transpose(ring[:, r, 0, k * P:(k + 1) * P], xn[:, n, k * P:(k + 1) * P],
                                                      ident[:])
                        ins.then_inc(unit_ready, 1)
                    elif kind == "qkv":
                        pe.wait_ge(act_units, b * ACT_UNITS + ACT_UPTO[FIRST[("turn", n)]])
                        pe.wait_ge(dve_units, b * DVE_UNITS + DVE_UPTO[FIRST[("turn", n)]])
                        r = take(st)
                        for bank, cols in ((0, slice(0, 2 * D)), (1, slice(2 * D, 3 * D))):
                            for k in range(KT):
                                ins = products(ring[:, r, bank, 0:cols.stop - cols.start],
                                               (xT_hi[:, n % 2, k, :], xT_lo[:, n % 2, k, :]),
                                               (wqkv_hi[:, k, cols], wqkv_lo[:, k, cols]), k == 0, k == KT - 1)
                        ins.then_inc(unit_ready, 1)
                    elif kind == "stack":
                        pe.wait_ge(stack_ready, 2 * (b * TB + n + 1))
                        for half in range(2):
                            r = take(st, half)
                            for h in range(H):
                                ins = nc.tensor.transpose(ring16[0:SR, r, h * P:(h + 1) * P],
                                                          stack[:, n % 2, half * H + h, :], ident16[:])
                            ins.then_inc(unit_ready, 1)
                    elif kind == "max":
                        if n == 0:
                            pe.wait_ge(act_units, b * ACT_UNITS + ACT_UPTO[FIRST[("stack", TB - 1)] + 1])
                            pe.wait_ge(dve_units, b * DVE_UNITS + DVE_UPTO[FIRST[("stack", TB - 1)] + 1])
                        for u, (i, h0, nh, hb) in enumerate(MAXU):
                            r = take(st, u)
                            w = (i + 1) * P
                            for a in range(nh):
                                h = n * OCT + h0 + a
                                o = (a % hb) * w
                                nc.tensor.matmul(ring[:, r, a // hb, o:o + w], QT[0:SR, h, i * P:(i + 1) * P],
                                                 KTt[0:SR, h, 0:w], start=True, stop=False, skip_group_check=True)
                                ins = nc.tensor.matmul(ring[:, r, a // hb, o + w - P:o + w], ident16[:], causal[:],
                                                       start=False, stop=True, skip_group_check=True)
                            ins.then_inc(unit_ready, 1)
                    elif kind == "mturn":
                        pe.wait_ge(nparts_ready, b * 2 + n + 1)
                        r = take(st)
                        for s in range(TB):
                            ins = nc.tensor.transpose(ring16[0:MR * OCT, r, s * P:(s + 1) * P],
                                                      nparts[:, s, n].rearrange("p m h -> p (m h)"), ident16[:])
                        ins.then_inc(unit_ready, 1)
                    elif kind == "attend":
                        pe.wait_ge(nrows_in[n * QUAD // OCT], (b + 1) * 16 * MR)
                        todo = list(enumerate(SC_LAST))
                        for u, (j, h0, nh) in enumerate(SCU):
                            r = take(st, u)
                            w = S - j * P
                            for a in range(nh):
                                h = n * QUAD + h0 + a
                                out = ring[:, r, a, 0:w] if j < 2 else ring[:, r, a * w // 512, a * w % 512:a * w % 512 + w]
                                ins = nc.tensor.matmul(out, KTt[0:QR, h, j * P:(j + 1) * P], QT[0:QR, h, j * P:S],
                                                       start=True, stop=True)
                            ins.then_inc(unit_ready, 1)
                            while todo and todo[0][1] <= u - 2:
                                values(b, n, todo.pop(0)[0])
                        for j, _ in todo:
                            values(b, n, j)
                    elif kind == "norm":
                        pe.wait_ge(att_copied, b * QUAD + n + 1)
                        r = take(st)
                        for s in range(TB):
                            ins = nc.tensor.transpose(ring[:, r, 0, s * P:(s + 1) * P], att[:, n % 2, s * P:(s + 1) * P],
                                                      ident[:])
                        ins.then_inc(unit_ready, 1)
                    elif kind == "turn1":
                        pe.wait_ge(dve_units, b * DVE_UNITS + DVE_UPTO[FIRST[("norm", QUAD - 1)]])
                        r = take(st)
                        for s in range(TB):
                            for k in range(KT):
                                ins = nc.tensor.transpose(ring[:, r, k, s * P:(s + 1) * P],
                                                          attn[:, s, k * P:(k + 1) * P], ident[:])
                        ins.then_inc(unit_ready, 1)

                st = ("wo", 0)
                pe.wait_ge(act_units, b * ACT_UNITS + ACT_UPTO[FIRST[("turn1", 0)]])
                pe.wait_ge(dve_units, b * DVE_UNITS + DVE_UPTO[FIRST[("turn1", 0)]])
                for s in range(TB):
                    if s % 2 == 0:
                        r = take(st, s // 2)
                    for k in range(KT):
                        cols = slice(s * P, (s + 1) * P)
                        ins = products(ring[:, r, s % 2, 0:D],
                                       (attT_hi[:, k, cols], attT_lo[:, k, cols]), (wo_hi[:, k, :], wo_lo[:, k, :]),
                                       k == 0, k == KT - 1)
                    if s % 2:
                        ins.then_inc(unit_ready, 1)
                st = ("turn2", 0)
                r = take(st)
                for s in range(TB):
                    pe.wait_ge(xn2_ready, b * TB + s + 1)
                    for k in range(KT):
                        ins = nc.tensor.transpose(ring[:, r, k, s * P:(s + 1) * P], xn[:, s, k * P:(k + 1) * P],
                                                  ident[:])
                ins.then_inc(unit_ready, 1)
                st = ("router", 0)
                pe.wait_ge(act_units, b * ACT_UNITS + ACT_UPTO[FIRST[("turn2", 0)]])
                pe.wait_ge(dve_units, b * DVE_UNITS + DVE_UPTO[FIRST[("turn2", 0)]])
                r = take(st)
                for k in range(KT):
                    ins = products(ring[:, r, 0, :], (gw_hi[:, k, :], gw_lo[:, k, :]),
                                   (t["x2T_hi"][:, k, bass.ds(b * S, S)], t["x2T_lo"][:, k, bass.ds(b * S, S)]),
                                   k == 0, k == KT - 1)
                ins.then_inc(unit_ready, 1)
                st = ("lturn", 0)
                pe.wait_ge(act_units, b * ACT_UNITS + ACT_UPTO[FIRST[("router", 0)]])
                r = take(st)
                for s in range(TB):
                    ins = nc.tensor.transpose(ring[:, r, 0, s * P:(s + 1) * P], logT[:, s * P:(s + 1) * P], ident[:])
                ins.then_inc(unit_ready, 1)
                st = ("cturn", 0)
                pe.wait_ge(cparts_ready, b + 1)
                r = take(st)
                for s in range(TB):
                    ins = nc.tensor.transpose(ring16[:, r, s * P:(s + 1) * P], cparts[:, s, :], ident16[:])
                ins.then_inc(unit_ready, 1)
                pe.wait_ge(act_units, (b + 1) * ACT_UNITS)
                pe.wait_ge(dve_units, (b + 1) * DVE_UNITS)


def experts_block(nc, t, w_in, sel_in, out):
    with ExitStack() as ctx:
        def sb(name, shape, dt=F32):
            return ctx.enter_context(nc.sbuf_tensor(name, shape, dt))

        def sem(name):
            return ctx.enter_context(nc.semaphore(name))

        def pb(name, shape):
            return ctx.enter_context(nc.psum_tensor(name, shape, F32))

        GU = 2 * KT * P
        gate_ps = pb("gate_ps", [P, 2, S])
        up_ps = pb("up_ps", [P, 2, S])
        comb_ps = pb("comb_ps", [P, 2, S])
        y_ps = pb("y_ps", [P, TB, D])

        w_stage = sb("w_stage", [P, 2, GU + D])
        w_hi = sb("w_hi_sb", [P, 2, CH, GU + D], F32R)
        w_lo = sb("w_lo_sb", [P, 2, CH, GU + D], F32R)
        select = sb("select", [P, FT, P], BF16)
        silu = sb("silu", [P, 2, S])
        weighted = sb("weighted", [P, 2, S])
        hid = sb("hid", [P, 2, S])
        hid_hi = sb("hid_hi", [P, 2, S], F32R)
        hid_lo = sb("hid_lo", [P, 2, S], F32R)
        ysum = sb("ysum", [P, NT, D])
        stats = sb("ystats", [P, NT, 6])
        mv = sb("ymv", [P, NT, 2])
        rs = sb("yrs", [P, NT])
        shift = sb("yshift", [P, NT])

        stage_in = [sem(f"stage_in{i}") for i in range(2)]
        select_in = sem("select_in")
        whi_done = sem("whi_done")
        wlo_done = sem("wlo_done")
        gate_ready = sem("gate_ready")
        up_ready = sem("up_ready")
        silu_done = sem("silu_done")
        weighted_done = sem("weighted_done")
        hid_done = sem("hid_done")
        hid_hi_done = sem("hid_hi_done")
        hid_lo_done = sem("hid_lo_done")
        down_done = sem("down_done")
        y_added = sem("y_added")
        y_step = sem("y_step")
        y_var = sem("y_var")
        y_root = sem("y_root")
        y_out = sem("y_out")
        out_stored = sem("out_stored")

        PAIR = 2 * CH
        assert NCH % 2 == 0 and B % 2 == 0

        block = ctx.enter_context(nc.Block())

        def turns(eng):
            with eng.Fori(0, NCH // 2) as cc:
                for par in range(2):
                    chunk = cc * 2 + par
                    with eng.Fori(0, B // 2) as gp:
                        yield par, chunk, chunk * (B // 2) + gp, gp

        @block.sync
        def _(sp):
            sp.dma_start(select[:], sel_in).then_inc(select_in, 16)
            for a in range(2):
                sp.dma_start(w_stage[:, a, :], w_in[a]).then_inc(stage_in[a], 16)
            with sp.Fori(1, FT // 2) as i:
                for a in range(2):
                    sp.wait_ge(wlo_done, i * 2 + a - 1)
                    sp.dma_start(w_stage[:, a, :], w_in[bass.ds(i * 2 + a, 1), :, :].rearrange(
                        "o p n -> (o p) n")).then_inc(stage_in[a], 16)
            for b in range(B):
                sp.wait_ge(y_out, b + 1)
                sp.dma_start(out[:, b * TB:(b + 1) * TB, :], ysum[:, b * TB:(b + 1) * TB, :]).then_inc(out_stored, 16)
            sp.wait_ge(out_stored, 16 * B)

        @block.gpsimd
        def _(pool):
            pool.memset(ysum[:], 0.0).then_inc(y_added, 1)
            with pool.Fori(0, NCH // 2) as cc:
                for k in range(PAIR):
                    par, j = k // CH, k % CH
                    tile = cc * PAIR + k
                    pool.wait_ge(stage_in[k % 2], (cc * CH + k // 2 + 1) * 16)
                    if k == CH:
                        pool.wait_ge(y_added, cc * 2 * B + 1)
                    apart(pool)
                    pool.tensor_copy(w_hi[:, par, j, :], w_stage[:, k % 2, :]).then_inc(whi_done, 1)
                    pool.wait_ge(whi_done, tile + 1)
                    pool.tensor_tensor(w_lo[:, par, j, :], w_stage[:, k % 2, :], w_hi[:, par, j, :].bitcast(F32),
                                       ALU.subtract).then_inc(wlo_done, 1)
                pool.wait_ge(down_done, (cc * 2 + 1) * B * CH)

        @block.scalar
        def _(act):
            for par, chunk, turn, gp in turns(act):
                def high(k):
                    n = turn * PAIR + k
                    act.wait_ge(hid_done, n + 1)
                    if k >= 2:
                        act.wait_ge(down_done, n - 1)
                    nc.scalar.copy(hid_hi[:, k % 2, :], hid[:, k % 2, :]).then_inc(hid_hi_done, 1)

                for k in range(PAIR):
                    n = turn * PAIR + k
                    if k:
                        high(k - 1)
                    act.wait_ge(gate_ready, n + 1)
                    if k >= 2:
                        act.wait_ge(weighted_done, n - 1)
                    nc.scalar.activation(silu[:, k % 2, :], gate_ps[:, k % 2, :], ACT.Silu).then_inc(silu_done, 1)
                high(PAIR - 1)
            act.wait_ge(y_var, 1)
            nc.scalar.activation(rs[:], rs[:], ACT.Sqrt).then_inc(y_root, 1)

        @block.vector
        def _(dve):
            dve.wait_ge(y_added, 1)
            for par, chunk, turn, gp in turns(dve):
                def low(k):
                    n = turn * PAIR + k
                    dve.wait_ge(hid_hi_done, n + 1)
                    nc.vector.tensor_tensor(hid_lo[:, k % 2, :], hid[:, k % 2, :], hid_hi[:, k % 2, :].bitcast(F32),
                                            ALU.subtract).then_inc(hid_lo_done, 1)

                def add_y(gi):
                    n = turn * PAIR + gi * CH + CH
                    dve.wait_ge(down_done, n)
                    ys = ysum[:, bass.ds((gp * 2 + gi) * TB, TB), :]
                    nc.vector.tensor_tensor(ys, ys, y_ps[:], ALU.add).then_inc(y_added, 1)

                for k in range(PAIR):
                    n = turn * PAIR + k
                    if k:
                        low(k - 1)
                    dve.wait_ge(silu_done, n + 1)
                    nc.vector.tensor_tensor(weighted[:, k % 2, :], silu[:, k % 2, :], comb_ps[:, k % 2, :],
                                            ALU.mult).then_inc(weighted_done, 1)
                    if k == CH:
                        add_y(0)
                    dve.wait_ge(up_ready, n + 1)
                    dve.wait_ge(weighted_done, n + 1)
                    nc.vector.tensor_tensor(hid[:, k % 2, :], weighted[:, k % 2, :], up_ps[:, k % 2, :],
                                            ALU.mult).then_inc(hid_done, 1)
                low(PAIR - 1)
                add_y(1)
            count = 0

            def link(ins):
                nonlocal count
                count += 1
                ins.then_inc(y_step, 1)
                dve.wait_ge(y_step, count)

            dve.wait_ge(y_added, NCH * B + 1)
            for i in range(NT):
                ins = nc.vector.bn_stats(stats[:, i, :], ysum[:, i, :])
            link(ins)
            for i in range(NT):
                ins = nc.vector.bn_aggr(mv[:, i, :], stats[:, i, :])
            link(ins)
            nc.vector.tensor_scalar(rs[:], mv[:, :, 1], EPS, None, ALU.add).then_inc(y_var, 1)
            dve.wait_ge(y_root, 1)
            link(nc.vector.reciprocal(rs[:], rs[:]))
            link(nc.vector.scalar_tensor_tensor(out=shift[:], in0=mv[:, :, 0], scalar=-1.0, in1=rs[:], op0=ALU.mult,
                                                op1=ALU.mult))
            for b in range(B):
                for i in range(b * TB, (b + 1) * TB):
                    ins = nc.vector.scalar_tensor_tensor(out=ysum[:, i, :], in0=ysum[:, i, :], scalar=rs[:, i:i + 1],
                                                         in1=t["x"][:, i, :], op0=ALU.mult, op1=ALU.add)
                link(ins)
                for i in range(b * TB, (b + 1) * TB):
                    ins = nc.vector.tensor_scalar(ysum[:, i, :], ysum[:, i, :], shift[:, i:i + 1], None, ALU.add)
                ins.then_inc(y_out, 1)

        @block.tensor
        def _(pe):
            pe.wait_ge(select_in, 16)
            for par, chunk, turn, gp in turns(pe):
                def down(k):
                    n = turn * PAIR + k
                    j = k % CH
                    pe.wait_ge(hid_lo_done, n + 1)
                    if j == 0:
                        pe.wait_ge(y_added, turn * 2 + k // CH + 1)
                    for s in range(TB):
                        cols = slice(s * P, (s + 1) * P)
                        for i, (l, r) in enumerate(((hid_hi, w_hi), (hid_hi, w_lo), (hid_lo, w_hi))):
                            ins = nc.tensor.matmul(y_ps[:, s, :], l[:, k % 2, cols], r[:, par, j, GU:GU + D],
                                                   start=(j == 0 and i == 0 and s % 2 == 0), stop=(j == CH - 1 and i == 2),
                                                   skip_group_check=True)
                    ins.then_inc(down_done, 1)

                for k in range(PAIR):
                    n = turn * PAIR + k
                    j, gi = k % CH, k // CH
                    batch = bass.ds((gp * 2 + gi) * S, S)
                    pe.wait_ge(wlo_done, chunk * CH + j + 1)
                    if k >= 2:
                        pe.wait_ge(weighted_done, n - 1)
                    nc.tensor.matmul(comb_ps[:, k % 2, :], select[:, bass.ds(chunk * CH + j, 1), :].rearrange(
                        "p o n -> p (o n)"), t["combT"][:, batch], start=True, stop=True)
                    for half, ps in ((0, gate_ps), (1, up_ps)):
                        if half and k >= 2:
                            pe.wait_ge(hid_done, n - 1)
                        for c in range(KT):
                            cols = slice((half * KT + c) * P, (half * KT + c + 1) * P)
                            for i, (l, r) in enumerate(((w_hi, "x2T_hi"), (w_hi, "x2T_lo"), (w_lo, "x2T_hi"))):
                                ins = nc.tensor.matmul(ps[:, k % 2, :], l[:, par, j, cols], t[r][:, c, batch],
                                                       start=(c == 0 and i == 0), stop=(c == KT - 1 and i == 2))
                        ins.then_inc(up_ready if half else gate_ready, 1)
                    if k:
                        down(k - 1)
                down(PAIR - 1)


def build(nc, x, wqkv, wo, gw, rope, w, sel, out):
    with ExitStack() as ctx:
        t = {
            "x": ctx.enter_context(nc.sbuf_tensor("x_all", [P, NT, D], F32)),
            "x2T_hi": ctx.enter_context(nc.sbuf_tensor("x2T_hi", [P, KT, B * S], F32R)),
            "x2T_lo": ctx.enter_context(nc.sbuf_tensor("x2T_lo", [P, KT, B * S], F32R)),
            "combT": ctx.enter_context(nc.sbuf_tensor("combT", [P, B * S], BF16)),
        }
        attention_block(nc, t, x, wqkv, wo, gw, rope)
        experts_block(nc, t, w, sel, out)


def kernel(L0_attn_x, L0_attn_Wq, L0_attn_Wk, L0_attn_Wv, L0_attn_Wo, L0_ffn_gate_w, L0_ffn_expert_gate_up,
           L0_ffn_expert_down, L0_ffn_shared_gate_up, L0_ffn_shared_down, L0_ffn_shared_gate_vec):
    import numpy as np
    import concourse.bacc as bacc
    from concourse.bass_utils import run_bass_kernel_spmd

    def tiles_of_rows(a, n):
        return np.ascontiguousarray(a.reshape(n, P, -1).transpose(1, 0, 2))

    x = tiles_of_rows(np.asarray(L0_attn_x).reshape(B * S, D), NT)
    wqkv = tiles_of_rows(np.concatenate([np.asarray(L0_attn_Wq).T, np.asarray(L0_attn_Wk).T,
                                         np.asarray(L0_attn_Wv).T], axis=1), KT)
    wo = tiles_of_rows(np.asarray(L0_attn_Wo).T, KT)
    gw = np.zeros((D, P), np.float32)
    gw[:, 0:E] = np.asarray(L0_ffn_gate_w).T
    gw[:, E:GC] = np.asarray(L0_ffn_shared_gate_vec).T
    gw = tiles_of_rows(gw, KT)

    inv = np.float32(10000.0) ** (-np.arange(0, DH, 2, dtype=np.float32) / np.float32(DH))
    angle = np.arange(S, dtype=np.float32)[:, None] * inv[None, :]
    cos = np.repeat(np.cos(angle), 2, axis=1)
    sin = np.repeat(np.sin(angle), 2, axis=1)
    sin[:, 0::2] = -sin[:, 0::2]
    rope = np.ascontiguousarray(np.stack([cos, sin], 1).reshape(TB, P, 2, DH).transpose(1, 0, 2, 3)).astype(np.float32)

    def inner(gate_up, n):
        return gate_up.reshape(-1, 2, n, D)
    eg = inner(np.asarray(L0_ffn_expert_gate_up), I)
    sg = inner(np.asarray(L0_ffn_shared_gate_up), SI)
    fill = np.zeros((FT * P - E * I - SI, D), np.float32)
    w = []
    for part in range(2):
        rows = np.concatenate([eg[:, part].reshape(E * I, D), sg[:, part].reshape(SI, D), fill])
        w.append(rows.reshape(FT, P, KT, P).transpose(0, 3, 2, 1).reshape(FT, P, KT * P))
    down = np.concatenate([np.asarray(L0_ffn_expert_down).transpose(0, 2, 1).reshape(E * I, D),
                           np.asarray(L0_ffn_shared_down).T, fill])
    w.append(down.reshape(FT, P, D))
    w = np.ascontiguousarray(np.concatenate(w, axis=2))

    owner = np.minimum(np.arange(FT * P) // I, E)
    sel = np.zeros((P, FT * P), np.float32)
    for m in range(MR):
        sel[m * GC + owner, np.arange(FT * P)] = 1.0
    sel = sel.reshape(P, FT, P).astype(np.dtype("bfloat16"))

    nc = bacc.Bacc("TRN2", target_bir_lowering=False, num_devices=1)
    arrays, args = {}, {}
    for name, a in (("x", x), ("wqkv", wqkv), ("wo", wo), ("gw", gw), ("rope", rope), ("w", w), ("sel", sel)):
        arrays[f"in_{name}_dram"] = a
        args[name] = nc.dram_tensor(f"in_{name}_dram", a.shape, mybir.dt.from_np(a.dtype), kind="ExternalInput").ap()
    out = nc.dram_tensor("out_dram", (P, NT, D), F32, kind="ExternalOutput").ap()
    build(nc, out=out, **args)
    r = run_bass_kernel_spmd(nc, [arrays], core_ids=[0])
    got = np.asarray(r.results[0]["out_dram"])
    return np.ascontiguousarray(got.transpose(1, 0, 2)).reshape(B, S, D)
```

```python
from contextlib import ExitStack

import concourse.bass as bass
from concourse import mybir

P = 128
B, S, D = 4, 512, 256
H, DH = 16, 16
TB = S // P
NT = B * TB
KT = D // P
E, K, I, SI = 16, 4, 176, 704
EPS = 1e-5
SLOTS = 6
SR = SLOTS * DH
MR = 3
QR = SR + MR
OCT = 8
QUAD = 4
FT = -(-(E * I + SI) // P)
CH = 7
NCH = FT // CH
GC = E + 1
NEG = -1e30

ALU = mybir.AluOpType
ACT = mybir.ActivationFunctionType
AX = mybir.AxisListType
F32 = mybir.dt.float32
F32R = mybir.dt.float32r
BF16 = mybir.dt.bfloat16

Q_HI, Q_MID, Q_LOW = slice(0, 3), slice(3, 6, 2), 4
K_HI, K_MID, K_LOW = slice(2, 5), slice(0, 6, 5), 1
SLOT_HI, SLOT_MID = 2, 5

MAXU = [(0, 0, 8, 4), (1, 0, 4, 2), (1, 4, 4, 2)] + [(i, h, 2, 1) for i in (2, 3) for h in range(0, OCT, 2)]
SCU = [(0, 0, 2), (0, 2, 2), (1, 0, 2), (1, 2, 2), (2, 0, 4), (3, 0, 4)]
SC_LAST = [1, 3, 4, 5]
A_USERS = {"max": "D", "mturn": "A", "score": "A", "norm": "D", "turn1": "AD"}
P_USERS = {"turn": "AD", "qk": "D", "v": "A", "stack": "A"}
M_USERS = {"wo": "A", "turn2": "AD", "logit": "A", "lturn": "D"}
P_KINDS = {"xn", "turn", "qk", "v", "rot", "high", "split", "stack"}
M_KINDS = {"wo", "stat", "add", "xn2", "turn2", "logit", "lturn"}


def users_of(item):
    if item[0] == "stack" and item[2] == 3:
        return "D"
    return A_USERS.get(item[0]) or M_USERS.get(item[0]) or P_USERS.get(item[0], "")


def apart(eng):
    eng.nop(nofuse=True)


ORDER = [
    ("xn", 0), ("max", 0, 0), ("turn", 0), ("vmove",), ("xn", 1), ("max", 0, 1), ("max", 0, 2), ("qk", 0),
    ("max", 0, 3), ("max", 0, 4), ("turn", 1), ("max", 0, 5), ("max", 0, 6), ("rot", 0), ("max", 0, 7), ("high", 0),
    ("max", 0, 8), ("max", 0, 9), ("max", 0, 10), ("wo",), ("split", 0), ("msplit", 0), ("max", 1, 0), ("xn", 2),
    ("mturn", 0), ("stack", 0, 0), ("v", 0), ("stat",), ("max", 1, 1), ("qk", 1), ("turn", 2), ("score", 0, 0),
    ("score", 0, 1), ("score", 0, 2), ("score", 0, 3), ("pv", 0, 0), ("score", 0, 4), ("pv", 0, 1), ("rot", 1),
    ("add",), ("score", 0, 5), ("score", 1, 0), ("qk", 2), ("high", 1), ("score", 1, 1), ("max", 1, 2), ("rot", 2),
    ("stack", 0, 1), ("xn", 3), ("v", 1), ("max", 1, 3), ("split", 1), ("pv", 0, 2), ("pv", 0, 3), ("stack", 0, 2),
    ("pv", 1, 0), ("score", 1, 2), ("max", 1, 4), ("stack", 0, 3), ("max", 1, 5), ("high", 2), ("max", 1, 6),
    ("stack", 1, 0), ("max", 1, 7), ("stack", 1, 1), ("split", 2), ("score", 1, 3), ("score", 1, 4), ("v", 2),
    ("max", 1, 8), ("max", 1, 9), ("copy", 0), ("stack", 1, 2), ("max", 1, 10), ("turn", 3), ("msplit", 1),
    ("stack", 1, 3), ("score", 1, 5), ("xn2",), ("stack", 2, 0), ("pv", 1, 1), ("mturn", 1), ("stack", 2, 1),
    ("norm", 0), ("turn2",), ("pv", 1, 2), ("stack", 2, 2), ("v", 3), ("pv", 1, 3), ("score", 2, 0), ("score", 2, 1),
    ("copy", 1), ("stack", 2, 3), ("qk", 3), ("rot", 3), ("score", 2, 2), ("score", 2, 3), ("pv", 2, 0),
    ("score", 2, 4), ("score", 2, 5), ("pv", 2, 1), ("norm", 1), ("pv", 2, 2), ("high", 3), ("score", 3, 0),
    ("split", 3), ("score", 3, 1), ("score", 3, 2), ("turn1", 0), ("pv", 2, 3), ("score", 3, 3), ("stack", 3, 0),
    ("pv", 3, 0), ("copy", 2), ("score", 3, 4), ("score", 3, 5), ("stack", 3, 1), ("pv", 3, 1), ("stack", 3, 2),
    ("norm", 2), ("logit",), ("stack", 3, 3), ("pv", 3, 2), ("pv", 3, 3), ("copy", 3), ("lturn",), ("norm", 3),
    ("turn1", 1),
]


class Segment:

    def __init__(self, items, start, turn=0):
        self.items, self.start, self.turn = items, start, turn
        n = {k: 0 for k in ("a", "aA", "aD", "p", "pA", "pD")}
        self.index, self.upto, self.order = {}, {}, {"a": [], "p": []}
        for item in items:
            who = users_of(item)
            if not who:
                continue
            ring = "p" if item[0] in P_USERS else "a"
            self.index[item] = (ring, n[ring])
            n[ring] += 1
            for w in who:
                n[ring + w] += 1
            self.upto[item] = dict(n)
            self.order[ring].append(item)
        self.total = n

    def at(self, kind, item):
        return self.start[kind] + self.turn * self.total[kind] + self.upto[item][kind]

    def after(self):
        return {k: self.start[k] + self.total[k] for k in self.total}


FREE = {"a": 0, "aA": 1, "aD": 1, "p": 0, "pA": 0, "pD": 0}
A_RING, P_RING = 2, 2


def segments(turn):
    def chosen(a, p, m):
        return [item for item in ORDER
                if (p if item[0] in P_KINDS else m if item[0] in M_KINDS else a)]

    parts = [(chosen(0, 1, 0), 1), (chosen(1, 1, 0), 1), (ORDER, B - 2), (chosen(1, 0, 1), 1), (chosen(0, 0, 1), 1)]
    start, out = FREE, []
    for n, (items, turns) in enumerate(parts):
        seg = Segment(items, start, turn if n == 2 else 0)
        assert seg.total["a"] % A_RING == 0 and seg.total["p"] % P_RING == 0
        start = {k: start[k] + turns * seg.total[k] for k in start}
        out.append(seg)
    return out


def attention_block(nc, t, x_in, wqkv_in, wo_in, gw_in, rope_in):
    with ExitStack() as ctx:
        def sb(name, shape, dt=F32):
            return ctx.enter_context(nc.sbuf_tensor(name, shape, dt))

        def sem(name):
            return ctx.enter_context(nc.semaphore(name))

        a_ps = ctx.enter_context(nc.psum_tensor("a_ps", [P, A_RING, 2, 512], F32))
        a16 = a_ps[:].rearrange("p r b n -> p r (b n)").bitcast(BF16)
        p_ps = ctx.enter_context(nc.psum_tensor("p_ps", [P, P_RING, 512], F32))
        p16 = p_ps[:].bitcast(BF16)
        att_ps = ctx.enter_context(nc.psum_tensor("att_ps", [P, 2, 512], F32))

        ident16 = t["ident16"]
        ident = sb("ident", [P, P])
        causal = sb("causal", [P, P], BF16)
        rope = sb("rope", [P, TB, 2, DH])
        wqkv_hi = sb("wqkv_hi", [P, KT, 3 * D], F32R)
        wqkv_lo = sb("wqkv_lo", [P, KT, 3 * D], F32R)
        probs = sb("probs", [P, 4, 1024])
        QT = sb("QT", [P, H, S], BF16)
        KTt = sb("KTt", [P, H, S], BF16)
        QTn = sb("QTn", [P, H, S], BF16)
        KTn = sb("KTn", [P, H, S], BF16)
        V = sb("V", [P, TB, H, 2 * DH])
        Vn = sb("Vn", [P, TB, H, DH])
        xn = sb("xn", [P, 2, D])
        xT_hi = sb("xT_hi", [P, 2, KT, P], F32R)
        xT_lo = sb("xT_lo", [P, 2, KT, P], F32R)
        rot = sb("rot", [P, 2, 2 * D])
        rest = sb("rest", [P, 2, 2 * D])
        stack = sb("stack", [P, 2, 2 * H, SR], BF16)
        nmax = sb("nmax", [P, TB, H])
        nrest = sb("nrest", [P, TB, H])
        nparts = sb("nparts", [P, TB, H // OCT, MR, OCT], BF16)
        nT = sb("nT", [MR * OCT, S], BF16)
        att = sb("att", [P, S])
        rsum = sb("rsum", [P, 2, TB, QUAD])
        attn = sb("attn", [P, TB, P])
        stats = sb("stats", [P, NT, 6])
        mv = sb("mv", [P, NT, 2])
        rs = sb("rs", [P, NT])
        attT_hi = sb("attT_hi", [P, KT, S], F32R)
        attT_lo = sb("attT_lo", [P, KT, S], F32R)
        wo_hi = sb("wo_hi", [P, KT, D], F32R)
        wo_lo = sb("wo_lo", [P, KT, D], F32R)
        gw_hi = sb("gw_hi", [P, KT, P], F32R)
        gw_lo = sb("gw_lo", [P, KT, P], F32R)
        mix = sb("mix", [P, TB, D])
        mstats = sb("mstats", [P, TB, 6])
        mmv = sb("mmv", [P, TB, 2])
        mrs = sb("mrs", [P, TB])
        mshift = sb("mshift", [P, TB])
        power = sb("power", [P, NT])
        logT = sb("logT", [P, S])

        x_in_sem = [sem(f"x_in{c}") for c in range(B)]
        rope_in_sem = sem("rope_in_sem")
        wqkv_in_sem = sem("wqkv_in_sem")
        pool_const = sem("pool_const")
        ones_set = sem("ones_set")
        w_hi = sem("w_hi")
        w_lo = sem("w_lo")
        stat_step = sem("stat_step")
        var_ready = sem("var_ready")
        root_ready = sem("root_ready")
        mstep = sem("mstep")
        mvar_ready = sem("mvar_ready")
        eps_added = sem("eps_added")
        meps_added = sem("meps_added")
        mroot_ready = sem("mroot_ready")
        x1_ready = sem("x1_ready")
        mix_ready = sem("mix_ready")
        xn_ready = sem("xn_ready")
        a_ready = sem("a_ready")
        a_act = sem("a_act")
        a_dve = sem("a_dve")
        p_ready = sem("p_ready")
        p_act = sem("p_act")
        p_dve = sem("p_dve")
        roped = sem("roped")
        high_ready = sem("high_ready")
        rest_ready = sem("rest_ready")
        mid_ready = sem("mid_ready")
        low_ready = sem("low_ready")
        nparts_step = sem("nparts_step")
        nparts_ready = sem("nparts_ready")
        qk_moved = [sem(f"qk_moved{g}") for g in range(2)]
        v_moved = sem("v_moved")
        nrows_in = [sem(f"nrows_in{g}") for g in range(2)]
        masked = sem("masked")
        pv_done = sem("pv_done")
        att_copied = sem("att_copied")
        rsum_ready = sem("rsum_ready")

        block = ctx.enter_context(nc.Block())
        staged = probs[:].rearrange("p a n -> p (a n)")
        ws_qkv = staged[:, 0:KT * 3 * D].rearrange("p (k n) -> p k n", k=KT)
        ws_wo = staged[:, KT * 3 * D:KT * 4 * D].rearrange("p (k n) -> p k n", k=KT)
        ws_gw = staged[:, KT * 4 * D:KT * (4 * D + P)].rearrange("p (k n) -> p k n", k=KT)
        ready = {"a": a_ready, "p": p_ready}

        def unit(seg, item):
            ring, n = seg.index[item]
            return (seg.start[ring] + n) % (A_RING if ring == "a" else P_RING)

        def wait_unit(eng, seg, item):
            ring = seg.index[item][0]
            eng.wait_ge(ready[ring], seg.at(ring, item))

        def run(eng, emit):
            project, begin, _, end, finish = segments(0)
            for item in project.items:
                emit(project, item, None, 0, None)
            for item in begin.items:
                emit(begin, item, 0, 1, None)
            with eng.Fori(1, B - 1) as b:
                body = segments(b - 1)[2]
                for item in body.items:
                    emit(body, item, b, b + 1, b - 1)
            for item in end.items:
                emit(end, item, B - 1, None, B - 2)
            for item in finish.items:
                emit(finish, item, None, None, B - 1)

        def heads(ap):
            return ap.rearrange("p (h d) -> p h d", d=DH)

        def pairs(ap):
            return ap.rearrange("p (h i e) -> p h i e", i=DH // 2, e=2)

        def slots(ap):
            return ap.rearrange("p h (s d) -> p h s d", d=DH)

        def move_stack(eng, copy, sem_used, seg, item, a):
            s, c = item[1:]
            wait_unit(eng, seg, item)
            if s == 0 and a is not None:
                for g in range(2):
                    eng.wait_ge(qk_moved[g], (a + 1) * 32)
            dst = (QTn if c < 2 else KTn)[0:SR, (c % 2) * OCT:(c % 2 + 1) * OCT, s * P:(s + 1) * P]
            copy(dst, p16[0:SR, unit(seg, item), :].rearrange("p (h n) -> p h n", h=OCT)).then_inc(sem_used, 1)

        @block.sync
        def _(sp):
            sp.dma_start(t["x"][:, 0:TB, :], x_in[:, 0:TB, :]).then_inc(x_in_sem[0], 16)
            sp.dma_start(ws_qkv, wqkv_in).then_inc(wqkv_in_sem, 16)
            sp.dma_start(rope[:], rope_in).then_inc(rope_in_sem, 16)
            sp.dma_start(ws_wo, wo_in).then_inc(wqkv_in_sem, 16)
            sp.dma_start(ws_gw, gw_in).then_inc(wqkv_in_sem, 16)
            for c in range(1, B):
                sp.dma_start(t["x"][:, c * TB:(c + 1) * TB, :], x_in[:, c * TB:(c + 1) * TB, :]
                             ).then_inc(x_in_sem[c], 16)

            def move_qk(seg, item, g):
                sp.wait_ge(p_act, seg.at("pA", item))
                sp.wait_ge(p_dve, seg.at("pD", item))
                o = slice(g * OCT, (g + 1) * OCT)
                sp.dma_start(QT[0:SR, o, :], QTn[0:SR, o, :]).then_inc(qk_moved[g], 16)
                sp.dma_start(KTt[0:SR, o, :], KTn[0:SR, o, :]).then_inc(qk_moved[g], 16)

            def emit(seg, item, a, p, m):
                kind = item[0]
                if kind == "mturn":
                    g = item[1]
                    sp.wait_ge(a_act, seg.at("aA", item))
                    for part in range(MR):
                        sp.dma_start(QT[SR + part:SR + part + 1, g * OCT:(g + 1) * OCT, :],
                                     nT[part * OCT:(part + 1) * OCT, :]).then_inc(nrows_in[g], 16)
                elif item == ("stack", TB - 1, 3):
                    if a is None:
                        move_qk(seg, item, 0)
                        move_qk(seg, item, 1)
                elif p is not None and kind == "pv" and item[2] == TB - 1 and item[1] == QUAD - 1:
                    for g in range(2):
                        sp.wait_ge(a_ready, seg.at("a", ("score", 2 * g + 1, len(SCU) - 1)))
                        move_qk(seg, ("stack", TB - 1, 3), g)

            run(sp, emit)

        @block.gpsimd
        def _(pool):
            pool.memset(ident[:], 1.0).then_inc(pool_const, 1)
            pool.memset(causal[:], 0.0).then_inc(pool_const, 1)
            pool.wait_ge(pool_const, 2)
            pool.affine_select(out=ident[:], in_=ident[:], pattern=[[1, P]], compare_op=ALU.is_equal, fill=0.0,
                               base=0, channel_multiplier=-1).then_inc(pool_const, 1)
            pool.affine_select(out=causal[:], in_=causal[:], pattern=[[-1, P]], compare_op=ALU.is_ge, fill=NEG,
                               base=0, channel_multiplier=1).then_inc(pool_const, 1)
            pool.wait_ge(pool_const, 4)
            pool.tensor_copy(ident16[:], ident[:]).then_inc(pool_const, 1)
            pool.memset(power[:], -0.5).then_inc(pool_const, 1)
            pool.wait_ge(pool_const, 6)
            pool.memset(V[:, :, :, DH:2 * DH], 1.0).then_inc(ones_set, 1)
            pool.wait_ge(ones_set, 1)
            pool.wait_ge(pool_const, 5)
            pool.memset(KTt[SR:P, :, :], 1.0).then_inc(ones_set, 1)
            pool.wait_ge(ones_set, 2)

            def emit(seg, item, a, p, m):
                kind = item[0]
                if kind == "rot":
                    s = item[1]
                    pool.wait_ge(p_dve, seg.at("pD", ("qk", s)))
                    pool.tensor_tensor(rot[:, s % 2, :], rot[:, s % 2, :], rest[:, s % 2, :],
                                       ALU.add).then_inc(roped, 1)
                elif kind == "split":
                    s = item[1]
                    pool.wait_ge(mid_ready, 2 * (p * TB + s + 1))
                    r, sk = heads(rest[:, s % 2, :]), slots(stack[:, s % 2])
                    for h, low in ((0, Q_LOW), (H, K_LOW)):
                        pool.tensor_tensor(sk[:, h:h + H, low, :], r[:, h:h + H, :], sk[:, h:h + H, SLOT_MID, :],
                                           ALU.subtract).then_inc(low_ready, 1)
                elif kind in ("stat", "add"):
                    n = m * 2 + (kind == "add") + 1
                    pool.wait_ge(mvar_ready, n)
                    apart(pool)
                    pool.tensor_scalar(mrs[:], mmv[:, :, 1], EPS, None, ALU.add).then_inc(meps_added, 1)
                    pool.wait_ge(meps_added, n)
                    pool.tensor_tensor(mrs[:], mrs[:], power[:, 0:TB], ALU.pow).then_inc(mroot_ready, 1)
                elif kind == "score":
                    q, u = item[1:]
                    j, h0, nh = SCU[u]
                    pool.wait_ge(a_act, seg.at("aA", item))
                    apart(pool)
                    w = S - j * P
                    pr = probs[:, (q * len(SCU) + u) % 4, 0:nh * w].rearrange("p (h n) -> p h n", h=nh)[:, :, 0:P]
                    pool.affine_select(out=pr, in_=pr, pattern=[[0, nh], [1, P]], compare_op=ALU.is_ge,
                                       fill=0.0, base=0, channel_multiplier=-1).then_inc(masked, 1)

            for n in (0, 1):
                c = slice(0, TB) if n == 0 else slice(TB, NT)
                pool.wait_ge(var_ready, n + 1)
                pool.tensor_scalar(rs[:, c], mv[:, c, 1], EPS, None, ALU.add).then_inc(eps_added, 1)
                pool.wait_ge(eps_added, n + 1)
                pool.tensor_tensor(rs[:, c], rs[:, c], power[:, 0:c.stop - c.start], ALU.pow).then_inc(root_ready, 1)
            run(pool, emit)

        @block.scalar
        def _(act):
            act.nop(nofuse=True).then_inc(a_act, 1)
            act.wait_ge(wqkv_in_sem, 48)
            nc.scalar.copy(wqkv_hi[:], ws_qkv).then_inc(w_hi, 1)
            nc.scalar.copy(wo_hi[:], ws_wo).then_inc(w_hi, 1)
            nc.scalar.copy(gw_hi[:], ws_gw).then_inc(w_hi, 1)
            act.wait_ge(w_lo, 3)
            act.wait_ge(ones_set, 2)

            def emit(seg, item, a, p, m):
                kind = item[0]
                if kind == "turn":
                    wait_unit(act, seg, item)
                    nc.scalar.copy(xT_hi[:, item[1] % 2], p_ps[:, unit(seg, item), 0:KT * P].rearrange(
                        "p (k n) -> p k n", k=KT)).then_inc(p_act, 1)
                elif kind == "v":
                    wait_unit(act, seg, item)
                    if item[1] == 0 and a is not None:
                        act.wait_ge(v_moved, a + 1)
                    nc.scalar.copy(Vn[:, item[1]], heads(p_ps[:, unit(seg, item), 0:D])).then_inc(p_act, 1)
                elif kind == "high":
                    s = item[1]
                    act.wait_ge(roped, p * TB + s + 1)
                    if s >= 2:
                        wait_unit(act, seg, ("stack", s - 2, 3))
                    r, sk = heads(rot[:, s % 2, :]), slots(stack[:, s % 2])
                    for h, where in ((0, Q_HI), (H, K_HI)):
                        src = r[:, h:h + H, :].unsqueeze(2).to_broadcast([P, H, 3, DH])
                        nc.scalar.copy(sk[:, h:h + H, where, :], src).then_inc(high_ready, 1)
                elif kind == "stack" and "A" in users_of(item):
                    move_stack(act, nc.scalar.copy, p_act, seg, item, a)
                elif kind == "vmove":
                    nc.scalar.copy(V[:, :, :, 0:DH], Vn[:]).then_inc(v_moved, 1)
                elif kind == "mturn":
                    wait_unit(act, seg, item)
                    if item[1]:
                        act.wait_ge(nrows_in[0], (a + 1) * 16 * MR)
                    nc.scalar.copy(nT[:], a16[0:MR * OCT, unit(seg, item), 0:S]).then_inc(a_act, 1)
                elif kind == "score":
                    q, u = item[1:]
                    wait_unit(act, seg, item)
                    j, h0, nh = SCU[u]
                    w = S - j * P
                    old = q * len(SCU) + u - 4
                    if old >= 0:
                        act.wait_ge(pv_done, (a * QUAD + old // len(SCU)) * TB + SCU[old % len(SCU)][0] + 1)
                    src = a_ps[:, unit(seg, item)]
                    dst = probs[:, (q * len(SCU) + u) % 4, 0:nh * w]
                    if j == 1:
                        src, dst = src[:, :, 0:w], dst.rearrange("p (h n) -> p h n", h=nh)
                    else:
                        src = src.rearrange("p b n -> p (b n)")[:, 0:nh * w]
                    nc.scalar.activation(dst, src, ACT.Exp, scale=float(DH) ** -0.5).then_inc(a_act, 1)
                elif kind == "copy":
                    n = item[1]
                    act.wait_ge(pv_done, (a * QUAD + n + 1) * TB)
                    if n:
                        wait_unit(act, seg, ("norm", n - 1))
                    nc.scalar.copy(att[:], att_ps[:, n % 2, :]).then_inc(att_copied, 1)
                elif kind == "turn1":
                    wait_unit(act, seg, item)
                    nc.scalar.copy(attT_hi[:, item[1], :], a_ps[:, unit(seg, item), 0, :]).then_inc(a_act, 1)
                elif kind == "wo":
                    wait_unit(act, seg, item)
                    nc.scalar.copy(mix[:], a_ps[:, unit(seg, item)].rearrange("p b (s n) -> p (b s) n", n=D)
                                   ).then_inc(a_act, 1)
                elif kind == "turn2":
                    wait_unit(act, seg, item)
                    nc.scalar.copy(t["x2T_hi"][:, :, bass.ds(m * S, S)], a_ps[:, unit(seg, item)]).then_inc(a_act, 1)
                elif kind == "logit":
                    wait_unit(act, seg, item)
                    nc.scalar.copy(logT[:], a_ps[:, unit(seg, item), 0, :]).then_inc(a_act, 1)

            run(act, emit)

        @block.vector
        def _(dve):
            x_all = t["x"]
            dve.nop(nofuse=True).then_inc(a_dve, 1)
            steps = 0
            for n in (0, 1):
                tiles = range(0, TB) if n == 0 else range(TB, NT)
                for i in tiles:
                    if i % TB == 0:
                        dve.wait_ge(x_in_sem[i // TB], 16)
                    ins = nc.vector.bn_stats(stats[:, i, :], x_all[:, i, :])
                ins.then_inc(stat_step, 1)
                steps += 1
                dve.wait_ge(stat_step, steps)
                for i in tiles:
                    ins = nc.vector.bn_aggr(mv[:, i, :], stats[:, i, :])
                ins.then_inc(var_ready, 1)
            dve.wait_ge(w_hi, 3)
            for lo, staging, hi in ((wqkv_lo, ws_qkv, wqkv_hi), (wo_lo, ws_wo, wo_hi), (gw_lo, ws_gw, gw_hi)):
                nc.vector.tensor_tensor(lo[:], staging, hi[:].bitcast(F32), ALU.subtract).then_inc(w_lo, 1)
            dve.wait_ge(root_ready, 1)
            dve.wait_ge(rope_in_sem, 16)

            def x_row(row):
                if isinstance(row, int):
                    return x_all[:, row, :]
                return x_all[:, bass.ds(row, 1), :].rearrange("p o n -> p (o n)")

            def moments(before):
                apart(dve)
                for s in range(TB):
                    ins = nc.vector.bn_stats(mstats[:, s, :], mix[:, s, :])
                ins.then_inc(mstep, 1)
                dve.wait_ge(mstep, before + 1)
                apart(dve)
                for s in range(TB):
                    ins = nc.vector.bn_aggr(mmv[:, s, :], mstats[:, s, :])
                ins.then_inc(mvar_ready, 1)

            def emit(seg, item, a, p, m):
                kind = item[0]
                if kind == "xn":
                    s = item[1]
                    if s >= 2:
                        wait_unit(dve, seg, ("turn", s - 2))
                    row = p * TB + s
                    if s == 0 and a is not None:
                        dve.wait_ge(root_ready, 2)
                    if isinstance(row, int):
                        xr, mean, scale = x_all[:, row, :], mv[:, row, 0:1], rs[:, row:row + 1]
                    else:
                        xr = x_all[:, bass.ds(row, 1), :].rearrange("p o n -> p (o n)")
                        mean, scale = mv[:, bass.ds(row, 1), 0], rs[:, bass.ds(row, 1)]
                    nc.vector.tensor_scalar(xn[:, s % 2, :], xr, mean, scale, ALU.subtract,
                                            ALU.mult).then_inc(xn_ready, 1)
                elif kind == "turn":
                    s = item[1]
                    dve.wait_ge(p_act, seg.at("pA", item))
                    nc.vector.tensor_tensor(xT_lo[:, s % 2], p_ps[:, unit(seg, item), 0:KT * P].rearrange(
                        "p (k n) -> p k n", k=KT), xT_hi[:, s % 2].bitcast(F32), ALU.subtract).then_inc(p_dve, 1)
                elif kind == "qk":
                    s = item[1]
                    wait_unit(dve, seg, item)
                    if s >= 2:
                        dve.wait_ge(rest_ready, p * TB + s - 1)
                        dve.wait_ge(low_ready, 2 * (p * TB + s - 1))
                        dve.wait_ge(mid_ready, 2 * (p * TB + s - 1))
                    ps = p_ps[:, unit(seg, item), :]
                    sin = pairs(rope[:, s, 1, :])
                    nc.vector.tensor_tensor(heads(rot[:, s % 2, :]), heads(ps),
                                            rope[:, s, 0, :].unsqueeze(1).to_broadcast([P, 2 * H, DH]), ALU.mult)
                    sd = pairs(rest[:, s % 2, :])
                    for e in range(2):
                        ins = nc.vector.tensor_tensor(sd[:, :, :, e], pairs(ps)[:, :, :, 1 - e],
                                                      sin[:, :, :, e].to_broadcast([P, 2 * H, DH // 2]), ALU.mult)
                    ins.then_inc(p_dve, 1)
                elif kind == "split":
                    s = item[1]
                    dve.wait_ge(high_ready, 2 * (p * TB + s + 1))
                    r, sk = heads(rest[:, s % 2, :]), slots(stack[:, s % 2])
                    nc.vector.tensor_tensor(r, heads(rot[:, s % 2, :]), sk[:, :, SLOT_HI, :],
                                            ALU.subtract).then_inc(rest_ready, 1)
                    dve.wait_ge(rest_ready, p * TB + s + 1)
                    for h, where in ((0, Q_MID), (H, K_MID)):
                        src = r[:, h:h + H, :].unsqueeze(2).to_broadcast([P, H, 2, DH])
                        nc.vector.tensor_copy(sk[:, h:h + H, where, :], src).then_inc(mid_ready, 1)
                elif kind == "stack" and "D" in users_of(item):
                    move_stack(dve, nc.vector.tensor_copy, p_dve, seg, item, a)
                elif kind == "max":
                    g, u = item[1:]
                    wait_unit(dve, seg, item)
                    i, h0, nh, hb = MAXU[u]
                    src = a_ps[:, unit(seg, item), :, 0:hb * (i + 1) * P].rearrange("p b (h n) -> p b h n", h=hb)
                    h = g * OCT + h0
                    nc.vector.tensor_reduce(nmax[:, i, h:h + nh].rearrange("p (b h) -> p b h", h=hb), src,
                                            AX.X, ALU.max, negate=True).then_inc(a_dve, 1)
                elif kind == "msplit":
                    g = item[1]
                    o = slice(g * OCT, (g + 1) * OCT)
                    base = (a * 2 + g) * 3
                    dve.wait_ge(a_dve, seg.at("aD", ("max", g, len(MAXU) - 1)))
                    nc.vector.tensor_copy(nparts[:, :, g, 0, :], nmax[:, :, o]).then_inc(nparts_step, 1)
                    dve.wait_ge(nparts_step, base + 1)
                    nc.vector.tensor_tensor(nrest[:, :, o], nmax[:, :, o], nparts[:, :, g, 0, :],
                                            ALU.subtract).then_inc(nparts_step, 1)
                    dve.wait_ge(nparts_step, base + 2)
                    nc.vector.tensor_copy(nparts[:, :, g, 1, :], nrest[:, :, o]).then_inc(nparts_step, 1)
                    dve.wait_ge(nparts_step, base + 3)
                    nc.vector.tensor_tensor(nparts[:, :, g, 2, :], nrest[:, :, o], nparts[:, :, g, 1, :],
                                            ALU.subtract).then_inc(nparts_ready, 1)
                elif kind == "norm":
                    n = item[1]
                    wait_unit(dve, seg, item)
                    if n == 2:
                        wait_unit(dve, seg, ("turn1", 0))
                    o = a_ps[:, unit(seg, item), 0, :].rearrange("p (s a d) -> p s a d", s=TB, a=QUAD)
                    nc.vector.reciprocal(rsum[:, n % 2], o[:, :, :, DH]).then_inc(rsum_ready, 1)
                    dve.wait_ge(rsum_ready, a * QUAD + n + 1)
                    nc.vector.tensor_tensor(
                        attn[:, :, n % 2 * QUAD * DH:(n % 2 + 1) * QUAD * DH].rearrange("p s (a d) -> p s a d", a=QUAD),
                        o[:, :, :, 0:DH], rsum[:, n % 2].unsqueeze(3).to_broadcast([P, TB, QUAD, DH]),
                        ALU.mult).then_inc(a_dve, 1)
                elif kind == "turn1":
                    dve.wait_ge(a_act, seg.at("aA", item))
                    k = item[1]
                    nc.vector.tensor_tensor(attT_lo[:, k, :], a_ps[:, unit(seg, item), 0, :],
                                            attT_hi[:, k, :].bitcast(F32), ALU.subtract).then_inc(a_dve, 1)
                elif kind == "stat":
                    dve.wait_ge(a_act, seg.at("aA", ("wo",)))
                    moments(m * 5)
                elif kind == "add":
                    dve.wait_ge(mroot_ready, m * 2 + 1)
                    nc.vector.scalar_tensor_tensor(out=mshift[:], in0=mmv[:, :, 0], scalar=-1.0, in1=mrs[:],
                                                   op0=ALU.mult, op1=ALU.mult).then_inc(mstep, 1)
                    for s in range(TB):
                        ins = nc.vector.scalar_tensor_tensor(out=mix[:, s, :], in0=mix[:, s, :], scalar=mrs[:, s:s + 1],
                                                             in1=x_row(m * TB + s), op0=ALU.mult, op1=ALU.add)
                    ins.then_inc(mstep, 1)
                    dve.wait_ge(mstep, m * 5 + 3)
                    for s in range(TB):
                        ins = nc.vector.tensor_scalar(mix[:, s, :], mix[:, s, :], mshift[:, s:s + 1], None, ALU.add)
                    ins.then_inc(mstep, 1)
                    dve.wait_ge(mstep, m * 5 + 4)
                    apart(dve)
                    nc.vector.tensor_copy(x_all[:, bass.ds(m * TB, TB), :], mix[:]).then_inc(x1_ready, 1)
                    moments(m * 5 + 4)
                elif kind == "xn2":
                    dve.wait_ge(mroot_ready, m * 2 + 2)
                    dve.wait_ge(x1_ready, m + 1)
                    for s in range(TB):
                        ins = nc.vector.tensor_scalar(mix[:, s, :], mix[:, s, :], mmv[:, s, 0:1], mrs[:, s:s + 1],
                                                      ALU.subtract, ALU.mult)
                    ins.then_inc(mix_ready, 1)
                elif kind == "turn2":
                    dve.wait_ge(a_act, seg.at("aA", item))
                    cols = bass.ds(m * S, S)
                    nc.vector.tensor_tensor(t["x2T_lo"][:, :, cols], a_ps[:, unit(seg, item)],
                                            t["x2T_hi"][:, :, cols].bitcast(F32), ALU.subtract).then_inc(a_dve, 1)
                elif kind == "lturn":
                    wait_unit(dve, seg, item)
                    apart(dve)
                    nc.vector.tensor_copy(t["logit"][:, bass.ds(m * TB, TB), :], a_ps[:, unit(seg, item), 0, :].rearrange(
                        "p (s n) -> p s n", s=TB)[:, :, 0:GC]).then_inc(a_dve, 1)

            run(dve, emit)

        @block.tensor
        def _(pe):
            pe.wait_ge(pool_const, 5)
            pe.wait_ge(ones_set, 2)
            pe.wait_ge(w_lo, 3)

            def take(seg, item):
                ring, n = seg.index[item]
                size = A_RING if ring == "a" else P_RING
                used = {"A": a_act if ring == "a" else p_act, "D": a_dve if ring == "a" else p_dve}
                if n >= size:
                    old = seg.order[ring][n - size]
                    for who in users_of(old):
                        pe.wait_ge(used[who], seg.at(ring + who, old))
                else:
                    for who in "AD":
                        kind = ring + who
                        if seg.start[kind]:
                            pe.wait_ge(used[who], seg.start[kind] + seg.turn * seg.total[kind])
                return unit(seg, item)

            def emit(seg, item, a, p, m):
                kind = item[0]
                if kind == "turn":
                    s = item[1]
                    pe.wait_ge(xn_ready, p * TB + s + 1)
                    r = take(seg, item)
                    for k in range(KT):
                        ins = nc.tensor.transpose(p_ps[:, r, k * P:(k + 1) * P], xn[:, s % 2, k * P:(k + 1) * P],
                                                  ident[:])
                    ins.then_inc(p_ready, 1)
                elif kind in ("qk", "v"):
                    s = item[1]
                    if kind == "qk":
                        pe.wait_ge(p_act, seg.at("pA", ("turn", s)))
                        pe.wait_ge(p_dve, seg.at("pD", ("turn", s)))
                    r = take(seg, item)
                    cols = slice(0, 2 * D) if kind == "qk" else slice(2 * D, 3 * D)
                    for k in range(KT):
                        ins = products(nc, p_ps[:, r, 0:cols.stop - cols.start],
                                       (xT_hi[:, s % 2, k, :], xT_lo[:, s % 2, k, :]),
                                       (wqkv_hi[:, k, cols], wqkv_lo[:, k, cols]), k == 0, k == KT - 1)
                    ins.then_inc(p_ready, 1)
                elif kind == "stack":
                    s, c = item[1:]
                    pe.wait_ge(low_ready, 2 * (p * TB + s) + 1 + c // 2)
                    r = take(seg, item)
                    for h in range(OCT):
                        ins = nc.tensor.transpose(p16[0:SR, r, h * P:(h + 1) * P], stack[:, s % 2, c * OCT + h, :],
                                                  ident16[:])
                    ins.then_inc(p_ready, 1)
                elif kind == "max":
                    g, u = item[1:]
                    if u == 0:
                        pe.wait_ge(qk_moved[g], (a + 1) * 32)
                    r = take(seg, item)
                    i, h0, nh, hb = MAXU[u]
                    w = (i + 1) * P
                    for n in range(nh):
                        h = g * OCT + h0 + n
                        o = (n % hb) * w
                        nc.tensor.matmul(a_ps[:, r, n // hb, o:o + w], QT[0:SR, h, i * P:(i + 1) * P],
                                         KTt[0:SR, h, 0:w], start=True, stop=False, skip_group_check=True)
                        ins = nc.tensor.matmul(a_ps[:, r, n // hb, o + w - P:o + w], ident16[:], causal[:],
                                               start=False, stop=True, skip_group_check=True)
                    ins.then_inc(a_ready, 1)
                elif kind == "mturn":
                    g = item[1]
                    pe.wait_ge(nparts_ready, a * 2 + g + 1)
                    r = take(seg, item)
                    for s in range(TB):
                        ins = nc.tensor.transpose(a16[0:MR * OCT, r, s * P:(s + 1) * P],
                                                  nparts[:, s, g].rearrange("p m h -> p (m h)"), ident16[:])
                    ins.then_inc(a_ready, 1)
                elif kind == "score":
                    q, u = item[1:]
                    if u == 0:
                        pe.wait_ge(nrows_in[q * QUAD // OCT], (a + 1) * 16 * MR)
                    r = take(seg, item)
                    j, h0, nh = SCU[u]
                    w = S - j * P
                    for n in range(nh):
                        h = q * QUAD + h0 + n
                        bank, o = (n, 0) if j < 2 else (n * w // 512, n * w % 512)
                        ins = nc.tensor.matmul(a_ps[:, r, bank, o:o + w], KTt[0:QR, h, j * P:(j + 1) * P],
                                               QT[0:QR, h, j * P:S], start=True, stop=True)
                    ins.then_inc(a_ready, 1)
                elif kind == "pv":
                    q, j = item[1:]
                    pe.wait_ge(masked, (a * QUAD + q) * len(SCU) + SC_LAST[j] + 1)
                    if j == 0:
                        if q == 0:
                            pe.wait_ge(v_moved, a + 1)
                        if q >= 2:
                            pe.wait_ge(att_copied, a * QUAD + q - 1)
                    w = S - j * P
                    for n in range(QUAD):
                        u = next(u for u, (jj, h0, nh) in enumerate(SCU) if jj == j and h0 <= n < h0 + nh)
                        o = (n - SCU[u][1]) * w
                        ins = nc.tensor.matmul(att_ps[32 * n:32 * n + 32, q % 2, j * P:S], V[:, j, q * QUAD + n, :],
                                               probs[:, (q * len(SCU) + u) % 4, o:o + w],
                                               start=(j == 0), stop=(j == TB - 1))
                    ins.then_inc(pv_done, 1)
                elif kind == "norm":
                    n = item[1]
                    pe.wait_ge(att_copied, a * QUAD + n + 1)
                    r = take(seg, item)
                    for s in range(TB):
                        ins = nc.tensor.transpose(a_ps[:, r, 0, s * P:(s + 1) * P], att[:, s * P:(s + 1) * P],
                                                  ident[:])
                    ins.then_inc(a_ready, 1)
                elif kind == "turn1":
                    k = item[1]
                    pe.wait_ge(a_dve, seg.at("aD", ("norm", 2 * k + 1)))
                    r = take(seg, item)
                    for s in range(TB):
                        ins = nc.tensor.transpose(a_ps[:, r, 0, s * P:(s + 1) * P], attn[:, s, :],
                                                  ident[:])
                    ins.then_inc(a_ready, 1)
                elif kind == "wo":
                    pe.wait_ge(a_dve, seg.start["aD"] + seg.turn * seg.total["aD"])
                    r = take(seg, item)
                    for s in range(TB):
                        cols = slice(s * P, (s + 1) * P)
                        o = a_ps[:, r, s // 2, s % 2 * D:(s % 2 + 1) * D]
                        for k in range(KT):
                            ins = products(nc, o, (attT_hi[:, k, cols], attT_lo[:, k, cols]),
                                           (wo_hi[:, k, :], wo_lo[:, k, :]), k == 0, k == KT - 1)
                    ins.then_inc(a_ready, 1)
                elif kind == "turn2":
                    pe.wait_ge(mix_ready, m + 1)
                    r = take(seg, item)
                    for s in range(TB):
                        for k in range(KT):
                            ins = nc.tensor.transpose(a_ps[:, r, k, s * P:(s + 1) * P], mix[:, s, k * P:(k + 1) * P],
                                                      ident[:])
                    ins.then_inc(a_ready, 1)
                elif kind == "logit":
                    pe.wait_ge(a_dve, seg.at("aD", ("turn2",)))
                    r = take(seg, item)
                    cols = bass.ds(m * S, S)
                    for k in range(KT):
                        ins = products(nc, a_ps[:, r, 0, :], (gw_hi[:, k, :], gw_lo[:, k, :]),
                                       (t["x2T_hi"][:, k, cols], t["x2T_lo"][:, k, cols]), k == 0, k == KT - 1)
                    ins.then_inc(a_ready, 1)
                elif kind == "lturn":
                    pe.wait_ge(a_act, seg.at("aA", ("logit",)))
                    r = take(seg, item)
                    for s in range(TB):
                        ins = nc.tensor.transpose(a_ps[:, r, 0, s * P:(s + 1) * P], logT[:, s * P:(s + 1) * P],
                                                  ident[:])
                    ins.then_inc(a_ready, 1)

            run(pe, emit)


def products(nc, out, left, right, first, last):
    for i, (l, r) in enumerate(((0, 0), (0, 1), (1, 0))):
        ins = nc.tensor.matmul(out, left[l], right[r], start=first and i == 0, stop=last and i == 2)
    return ins


def route_block(nc, t):
    with ExitStack() as ctx:
        def sb(name, shape, dt=F32):
            return ctx.enter_context(nc.sbuf_tensor(name, shape, dt))

        def sem(name):
            return ctx.enter_context(nc.semaphore(name))

        c_ps = ctx.enter_context(nc.psum_tensor("c_ps", [P, B, 512], F32))
        c16 = c_ps[:].bitcast(BF16)
        logit, ident16 = t["logit"], t["ident16"]
        wide = [P, NT, E]
        eprob = sb("eprob", [P, NT, GC])
        prob = sb("prob", wide)
        big = sb("big", [P, 3, NT])
        top = sb("top", [P, NT, 8])
        more = sb("more", wide)
        same = sb("same", wide)
        count = sb("count", [P, 2, NT, E + E // 2])
        comb = sb("comb", [P, NT, GC])
        crest = sb("crest", [P, NT, GC])
        cparts = sb("cparts", [P, NT, P], BF16)

        const_set = sem("mconst_set")
        step_done = sem("mstep_done")
        centred = sem("centred")
        exp_ready = sem("exp_ready")
        cparts_ready = sem("cparts_ready")
        c_ready = sem("c_ready")
        comb_copied = sem("comb_copied")

        block = ctx.enter_context(nc.Block())

        @block.gpsimd
        def _(pool):
            pool.memset(cparts[:], 0.0).then_inc(const_set, 1)
            pool.memset(count[:], 0.0).then_inc(const_set, 1)

        @block.scalar
        def _(act):
            nc.scalar.activation(eprob[:, :, E:GC], logit[:, :, E:GC], ACT.Exp, scale=-1.0).then_inc(exp_ready, 1)
            act.wait_ge(centred, 1)
            nc.scalar.activation(eprob[:, :, 0:E], eprob[:, :, 0:E], ACT.Exp).then_inc(exp_ready, 1)
            for b in range(0, B, 2):
                act.wait_ge(c_ready, b + 1)
                nc.scalar.copy(t["combT"][:, b * S:(b + 1) * S], c16[:, b, 0:S]).then_inc(comb_copied, 1)

        @block.vector
        def _(dve):
            steps = 0

            def link(ins):
                nonlocal steps
                steps += 1
                ins.then_inc(step_done, 1)
                dve.wait_ge(step_done, steps)

            def over(ap):
                return ap.unsqueeze(2).to_broadcast(wide)

            link(nc.vector.tensor_reduce(big[:, 0, :], logit[:, :, 0:E], AX.X, ALU.max))
            nc.vector.tensor_tensor(eprob[:, :, 0:E], logit[:, :, 0:E], over(big[:, 0, :]),
                                    ALU.subtract).then_inc(centred, 1)
            dve.wait_ge(exp_ready, 2)
            nc.vector.tensor_reduce(big[:, 1, :], eprob[:, :, 0:E], AX.X, ALU.add)
            link(nc.vector.tensor_scalar(crest[:, :, E], eprob[:, :, E], 1.0, None, ALU.add))
            nc.vector.reciprocal(big[:, 2, :], big[:, 1, :])
            link(nc.vector.reciprocal(comb[:, :, E], crest[:, :, E]))
            link(nc.vector.tensor_tensor(prob[:], eprob[:, :, 0:E], over(big[:, 2, :]), ALU.mult))
            for i in range(NT):
                ins = nc.vector.max(top[:, i, :], prob[:, i, :])
            link(ins)
            fourth = over(top[:, :, K - 1])
            nc.vector.tensor_tensor(more[:], prob[:], fourth, ALU.is_gt)
            dve.wait_ge(const_set, 2)
            z = E // 2
            nc.vector.tensor_tensor(same[:], prob[:], fourth, ALU.is_equal)
            link(nc.vector.tensor_tensor(count[:, 0, :, z:], prob[:], fourth, ALU.is_equal))
            nc.vector.tensor_reduce(big[:, 0, :], more[:], AX.X, ALU.add)
            for i in range(4):
                old, new = count[:, i % 2], count[:, 1 - i % 2]
                link(nc.vector.tensor_tensor(new[:, :, z:], old[:, :, z:], old[:, :, z - 2 ** i:z + E - 2 ** i],
                                             ALU.add))
            link(nc.vector.tensor_tensor(crest[:, :, 0:E], count[:, 0, :, z:], over(big[:, 0, :]), ALU.add))
            link(nc.vector.scalar_tensor_tensor(out=same[:], in0=crest[:, :, 0:E], scalar=K + 0.5, in1=same[:],
                                                op0=ALU.is_lt, op1=ALU.mult))
            link(nc.vector.tensor_tensor(more[:], more[:], same[:], ALU.add))
            link(nc.vector.tensor_tensor(crest[:, :, 0:E], more[:], prob[:], ALU.mult))
            link(nc.vector.tensor_reduce(big[:, 0, :], crest[:, :, 0:E], AX.X, ALU.add))
            link(nc.vector.reciprocal(big[:, 1, :], big[:, 0, :]))
            link(nc.vector.tensor_tensor(comb[:, :, 0:E], crest[:, :, 0:E], over(big[:, 1, :]), ALU.mult))
            link(nc.vector.tensor_copy(cparts[:, :, 0:GC], comb[:]))
            link(nc.vector.tensor_tensor(crest[:], comb[:], cparts[:, :, 0:GC], ALU.subtract))
            link(nc.vector.tensor_copy(cparts[:, :, GC:2 * GC], crest[:]))
            nc.vector.tensor_tensor(cparts[:, :, 2 * GC:3 * GC], crest[:], cparts[:, :, GC:2 * GC],
                                    ALU.subtract).then_inc(cparts_ready, 1)
            for b in range(1, B, 2):
                dve.wait_ge(c_ready, b + 1)
                nc.vector.tensor_copy(t["combT"][:, b * S:(b + 1) * S], c16[:, b, 0:S]).then_inc(comb_copied, 1)

        @block.tensor
        def _(pe):
            pe.wait_ge(cparts_ready, 1)
            for b in range(B):
                for s in range(TB):
                    ins = nc.tensor.transpose(c16[:, b, s * P:(s + 1) * P], cparts[:, b * TB + s, :], ident16[:])
                ins.then_inc(c_ready, 1)


def experts_block(nc, t, w_in, sel_in, out):
    with ExitStack() as ctx:
        def sb(name, shape, dt=F32):
            return ctx.enter_context(nc.sbuf_tensor(name, shape, dt))

        def sem(name):
            return ctx.enter_context(nc.semaphore(name))

        def pb(name, shape):
            return ctx.enter_context(nc.psum_tensor(name, shape, F32))

        GU = 2 * KT * P
        gate_ps = pb("gate_ps", [P, 2, S])
        up_ps = pb("up_ps", [P, 2, S])
        comb_ps = pb("comb_ps", [P, 2, S])
        y_ps = pb("y_ps", [P, TB, D])

        w_stage = sb("w_stage", [P, 2, GU + D])
        w_hi = sb("w_hi_sb", [P, 2, CH, GU + D], F32R)
        w_lo = sb("w_lo_sb", [P, 2, CH, GU + D], F32R)
        select = sb("select", [P, FT, P], BF16)
        silu = sb("silu", [P, 2, S])
        weighted = sb("weighted", [P, 2, S])
        hid = sb("hid", [P, 2, S])
        hid_hi = sb("hid_hi", [P, 2, S], F32R)
        hid_lo = sb("hid_lo", [P, 2, S], F32R)
        ysum = sb("ysum", [P, NT, D])
        stats = sb("ystats", [P, NT, 6])
        mv = sb("ymv", [P, NT, 2])
        rs = sb("yrs", [P, NT])
        shift = sb("yshift", [P, NT])

        stage_in = [sem(f"stage_in{i}") for i in range(2)]
        select_in = sem("select_in")
        whi_done = sem("whi_done")
        wlo_done = sem("wlo_done")
        gate_ready = sem("gate_ready")
        up_ready = sem("up_ready")
        silu_done = sem("silu_done")
        weighted_done = sem("weighted_done")
        hid_done = sem("hid_done")
        hid_hi_done = sem("hid_hi_done")
        hid_lo_done = sem("hid_lo_done")
        down_done = sem("down_done")
        y_added = sem("y_added")
        y_step = sem("y_step")
        y_var = sem("y_var")
        y_root = sem("y_root")
        y_out = sem("y_out")
        out_stored = sem("out_stored")

        PAIR = 2 * CH
        assert NCH % 2 == 0 and B % 2 == 0

        block = ctx.enter_context(nc.Block())

        def turns(eng):
            with eng.Fori(0, NCH // 2) as cc:
                for par in range(2):
                    chunk = cc * 2 + par
                    with eng.Fori(0, B // 2) as gp:
                        yield par, chunk, chunk * (B // 2) + gp, gp

        @block.sync
        def _(sp):
            sp.dma_start(select[:], sel_in).then_inc(select_in, 16)
            for a in range(2):
                sp.dma_start(w_stage[:, a, :], w_in[a]).then_inc(stage_in[a], 16)
            with sp.Fori(1, FT // 2) as i:
                for a in range(2):
                    sp.wait_ge(wlo_done, i * 2 + a - 1)
                    sp.dma_start(w_stage[:, a, :], w_in[bass.ds(i * 2 + a, 1), :, :].rearrange(
                        "o p n -> (o p) n")).then_inc(stage_in[a], 16)
            for b in range(B):
                sp.wait_ge(y_out, b + 1)
                sp.dma_start(out[:, b * TB:(b + 1) * TB, :], ysum[:, b * TB:(b + 1) * TB, :]).then_inc(out_stored, 16)
            sp.wait_ge(out_stored, 16 * B)

        @block.gpsimd
        def _(pool):
            pool.memset(ysum[:], 0.0).then_inc(y_added, 1)
            with pool.Fori(0, NCH // 2) as cc:
                for k in range(PAIR):
                    par, j = k // CH, k % CH
                    tile = cc * PAIR + k
                    pool.wait_ge(stage_in[k % 2], (cc * CH + k // 2 + 1) * 16)
                    if k == CH:
                        pool.wait_ge(y_added, cc * 2 * B + 1)
                    apart(pool)
                    pool.tensor_copy(w_hi[:, par, j, :], w_stage[:, k % 2, :]).then_inc(whi_done, 1)
                    pool.wait_ge(whi_done, tile + 1)
                    pool.tensor_tensor(w_lo[:, par, j, :], w_stage[:, k % 2, :], w_hi[:, par, j, :].bitcast(F32),
                                       ALU.subtract).then_inc(wlo_done, 1)
                pool.wait_ge(down_done, (cc * 2 + 1) * B * CH)

        @block.scalar
        def _(act):
            for par, chunk, turn, gp in turns(act):
                def high(k):
                    n = turn * PAIR + k
                    act.wait_ge(hid_done, n + 1)
                    if k >= 2:
                        act.wait_ge(down_done, n - 1)
                    nc.scalar.copy(hid_hi[:, k % 2, :], hid[:, k % 2, :]).then_inc(hid_hi_done, 1)

                for k in range(PAIR):
                    n = turn * PAIR + k
                    if k:
                        high(k - 1)
                    act.wait_ge(gate_ready, n + 1)
                    if k >= 2:
                        act.wait_ge(weighted_done, n - 1)
                    nc.scalar.activation(silu[:, k % 2, :], gate_ps[:, k % 2, :], ACT.Silu).then_inc(silu_done, 1)
                high(PAIR - 1)
            act.wait_ge(y_var, 1)
            nc.scalar.activation(rs[:], rs[:], ACT.Sqrt).then_inc(y_root, 1)

        @block.vector
        def _(dve):
            dve.wait_ge(y_added, 1)
            for par, chunk, turn, gp in turns(dve):
                def low(k):
                    n = turn * PAIR + k
                    dve.wait_ge(hid_hi_done, n + 1)
                    nc.vector.tensor_tensor(hid_lo[:, k % 2, :], hid[:, k % 2, :], hid_hi[:, k % 2, :].bitcast(F32),
                                            ALU.subtract).then_inc(hid_lo_done, 1)

                def add_y(gi):
                    n = turn * PAIR + gi * CH + CH
                    dve.wait_ge(down_done, n)
                    ys = ysum[:, bass.ds((gp * 2 + gi) * TB, TB), :]
                    nc.vector.tensor_tensor(ys, ys, y_ps[:], ALU.add).then_inc(y_added, 1)

                for k in range(PAIR):
                    n = turn * PAIR + k
                    if k:
                        low(k - 1)
                    dve.wait_ge(silu_done, n + 1)
                    nc.vector.tensor_tensor(weighted[:, k % 2, :], silu[:, k % 2, :], comb_ps[:, k % 2, :],
                                            ALU.mult).then_inc(weighted_done, 1)
                    if k == CH:
                        add_y(0)
                    dve.wait_ge(up_ready, n + 1)
                    dve.wait_ge(weighted_done, n + 1)
                    nc.vector.tensor_tensor(hid[:, k % 2, :], weighted[:, k % 2, :], up_ps[:, k % 2, :],
                                            ALU.mult).then_inc(hid_done, 1)
                low(PAIR - 1)
                add_y(1)
            count = 0

            def link(ins):
                nonlocal count
                count += 1
                ins.then_inc(y_step, 1)
                dve.wait_ge(y_step, count)

            dve.wait_ge(y_added, NCH * B + 1)
            for i in range(NT):
                ins = nc.vector.bn_stats(stats[:, i, :], ysum[:, i, :])
            link(ins)
            for i in range(NT):
                ins = nc.vector.bn_aggr(mv[:, i, :], stats[:, i, :])
            link(ins)
            nc.vector.tensor_scalar(rs[:], mv[:, :, 1], EPS, None, ALU.add).then_inc(y_var, 1)
            dve.wait_ge(y_root, 1)
            link(nc.vector.reciprocal(rs[:], rs[:]))
            link(nc.vector.scalar_tensor_tensor(out=shift[:], in0=mv[:, :, 0], scalar=-1.0, in1=rs[:], op0=ALU.mult,
                                                op1=ALU.mult))
            for b in range(B):
                for i in range(b * TB, (b + 1) * TB):
                    ins = nc.vector.scalar_tensor_tensor(out=ysum[:, i, :], in0=ysum[:, i, :], scalar=rs[:, i:i + 1],
                                                         in1=t["x"][:, i, :], op0=ALU.mult, op1=ALU.add)
                link(ins)
                for i in range(b * TB, (b + 1) * TB):
                    ins = nc.vector.tensor_scalar(ysum[:, i, :], ysum[:, i, :], shift[:, i:i + 1], None, ALU.add)
                ins.then_inc(y_out, 1)

        @block.tensor
        def _(pe):
            pe.wait_ge(select_in, 16)
            for par, chunk, turn, gp in turns(pe):
                def down(k):
                    n = turn * PAIR + k
                    j = k % CH
                    pe.wait_ge(hid_lo_done, n + 1)
                    if j == 0:
                        pe.wait_ge(y_added, turn * 2 + k // CH + 1)
                    for s in range(TB):
                        cols = slice(s * P, (s + 1) * P)
                        for i, (l, r) in enumerate(((hid_hi, w_hi), (hid_hi, w_lo), (hid_lo, w_hi))):
                            ins = nc.tensor.matmul(y_ps[:, s, :], l[:, k % 2, cols], r[:, par, j, GU:GU + D],
                                                   start=(j == 0 and i == 0 and s % 2 == 0), stop=(j == CH - 1 and i == 2),
                                                   skip_group_check=True)
                    ins.then_inc(down_done, 1)

                for k in range(PAIR):
                    n = turn * PAIR + k
                    j, gi = k % CH, k // CH
                    batch = bass.ds((gp * 2 + gi) * S, S)
                    pe.wait_ge(wlo_done, chunk * CH + j + 1)
                    if k >= 2:
                        pe.wait_ge(weighted_done, n - 1)
                    nc.tensor.matmul(comb_ps[:, k % 2, :], select[:, bass.ds(chunk * CH + j, 1), :].rearrange(
                        "p o n -> p (o n)"), t["combT"][:, batch], start=True, stop=True)
                    for half, ps in ((0, gate_ps), (1, up_ps)):
                        if half and k >= 2:
                            pe.wait_ge(hid_done, n - 1)
                        for c in range(KT):
                            cols = slice((half * KT + c) * P, (half * KT + c + 1) * P)
                            for i, (l, r) in enumerate(((w_hi, "x2T_hi"), (w_hi, "x2T_lo"), (w_lo, "x2T_hi"))):
                                ins = nc.tensor.matmul(ps[:, k % 2, :], l[:, par, j, cols], t[r][:, c, batch],
                                                       start=(c == 0 and i == 0), stop=(c == KT - 1 and i == 2))
                        ins.then_inc(up_ready if half else gate_ready, 1)
                    if k:
                        down(k - 1)
                down(PAIR - 1)


def build(nc, x, wqkv, wo, gw, rope, w, sel, out):
    with ExitStack() as ctx:
        t = {
            "x": ctx.enter_context(nc.sbuf_tensor("x_all", [P, NT, D], F32)),
            "x2T_hi": ctx.enter_context(nc.sbuf_tensor("x2T_hi", [P, KT, B * S], F32R)),
            "x2T_lo": ctx.enter_context(nc.sbuf_tensor("x2T_lo", [P, KT, B * S], F32R)),
            "ident16": ctx.enter_context(nc.sbuf_tensor("ident16", [P, P], BF16)),
            "logit": ctx.enter_context(nc.sbuf_tensor("logit", [P, NT, GC], F32)),
        }
        attention_block(nc, t, x, wqkv, wo, gw, rope)
        t["combT"] = ctx.enter_context(nc.sbuf_tensor("combT", [P, B * S], BF16))
        route_block(nc, t)
        experts_block(nc, t, w, sel, out)


def kernel(L0_attn_x, L0_attn_Wq, L0_attn_Wk, L0_attn_Wv, L0_attn_Wo, L0_ffn_gate_w, L0_ffn_expert_gate_up,
           L0_ffn_expert_down, L0_ffn_shared_gate_up, L0_ffn_shared_down, L0_ffn_shared_gate_vec):
    import numpy as np
    import concourse.bacc as bacc
    from concourse.bass_utils import run_bass_kernel_spmd

    def tiles_of_rows(a, n):
        return np.ascontiguousarray(a.reshape(n, P, -1).transpose(1, 0, 2))

    x = tiles_of_rows(np.asarray(L0_attn_x).reshape(B * S, D), NT)
    wqkv = tiles_of_rows(np.concatenate([np.asarray(L0_attn_Wq).T, np.asarray(L0_attn_Wk).T,
                                         np.asarray(L0_attn_Wv).T], axis=1), KT)
    wo = tiles_of_rows(np.asarray(L0_attn_Wo).T, KT)
    gw = np.zeros((D, P), np.float32)
    gw[:, 0:E] = np.asarray(L0_ffn_gate_w).T
    gw[:, E:GC] = np.asarray(L0_ffn_shared_gate_vec).T
    gw = tiles_of_rows(gw, KT)

    inv = np.float32(10000.0) ** (-np.arange(0, DH, 2, dtype=np.float32) / np.float32(DH))
    angle = np.arange(S, dtype=np.float32)[:, None] * inv[None, :]
    cos = np.repeat(np.cos(angle), 2, axis=1)
    sin = np.repeat(np.sin(angle), 2, axis=1)
    sin[:, 0::2] = -sin[:, 0::2]
    rope = np.ascontiguousarray(np.stack([cos, sin], 1).reshape(TB, P, 2, DH).transpose(1, 0, 2, 3)).astype(np.float32)

    def inner(gate_up, n):
        return gate_up.reshape(-1, 2, n, D)
    eg = inner(np.asarray(L0_ffn_expert_gate_up), I)
    sg = inner(np.asarray(L0_ffn_shared_gate_up), SI)
    fill = np.zeros((FT * P - E * I - SI, D), np.float32)
    w = []
    for part in range(2):
        rows = np.concatenate([eg[:, part].reshape(E * I, D), sg[:, part].reshape(SI, D), fill])
        w.append(rows.reshape(FT, P, KT, P).transpose(0, 3, 2, 1).reshape(FT, P, KT * P))
    down = np.concatenate([np.asarray(L0_ffn_expert_down).transpose(0, 2, 1).reshape(E * I, D),
                           np.asarray(L0_ffn_shared_down).T, fill])
    w.append(down.reshape(FT, P, D))
    w = np.ascontiguousarray(np.concatenate(w, axis=2))

    owner = np.minimum(np.arange(FT * P) // I, E)
    sel = np.zeros((P, FT * P), np.float32)
    for m in range(MR):
        sel[m * GC + owner, np.arange(FT * P)] = 1.0
    sel = sel.reshape(P, FT, P).astype(np.dtype("bfloat16"))

    nc = bacc.Bacc("TRN2", target_bir_lowering=False, num_devices=1)
    arrays, args = {}, {}
    for name, a in (("x", x), ("wqkv", wqkv), ("wo", wo), ("gw", gw), ("rope", rope), ("w", w), ("sel", sel)):
        arrays[f"in_{name}_dram"] = a
        args[name] = nc.dram_tensor(f"in_{name}_dram", a.shape, mybir.dt.from_np(a.dtype), kind="ExternalInput").ap()
    out = nc.dram_tensor("out_dram", (P, NT, D), F32, kind="ExternalOutput").ap()
    build(nc, out=out, **args)
    r = run_bass_kernel_spmd(nc, [arrays], core_ids=[0])
    got = np.asarray(r.results[0]["out_dram"])
    return np.ascontiguousarray(got.transpose(1, 0, 2)).reshape(B, S, D)
```

```python
from contextlib import ExitStack

import concourse.bass as bass
from concourse import mybir

P = 128
B, S, D = 4, 512, 256
H, DH = 16, 16
TB = S // P
NT = B * TB
KT = D // P
E, K, I, SI = 16, 4, 176, 704
EPS = 1e-5
SLOTS = 6
SR = SLOTS * DH
MR = 3
QR = SR + MR
OCT = 8
QUAD = 4
FT = -(-(E * I + SI) // P)
CH = 4
NCH = FT // CH
GC = E + 1
NEG = -1e30

ALU = mybir.AluOpType
ACT = mybir.ActivationFunctionType
AX = mybir.AxisListType
F32 = mybir.dt.float32
F32R = mybir.dt.float32r
BF16 = mybir.dt.bfloat16

Q_HI, Q_MID, Q_LOW = slice(0, 3), slice(3, 6, 2), 4
K_HI, K_MID, K_LOW = slice(2, 5), slice(0, 6, 5), 1
SLOT_HI, SLOT_MID = 2, 5

MAXU = [(0, 0, 8, 4), (1, 0, 4, 2), (1, 4, 4, 2)] + [(i, h, 2, 1) for i in (2, 3) for h in range(0, OCT, 2)]
SCU = [(0, 0, 2), (0, 2, 2), (1, 0, 2), (1, 2, 2), (2, 0, 4), (3, 0, 4)]
SC_LAST = [1, 3, 4, 5]
A_USERS = {"max": "D", "mturn": "A", "score": "A", "norm": "D", "turn1": "AD"}
P_USERS = {"turn": "AD", "qk": "D", "v": "A", "stack": "A"}
M_USERS = {"wo": "A", "turn2": "AD", "logit": "A", "lturn": "D"}
P_KINDS = {"xn", "turn", "qk", "v", "rot", "high", "split", "stack"}
M_KINDS = {"wo", "stat", "add", "xn2", "turn2", "logit", "lturn"}


def users_of(item):
    if item[0] == "stack" and item[2] == 3:
        return "D"
    return A_USERS.get(item[0]) or M_USERS.get(item[0]) or P_USERS.get(item[0], "")


def apart(eng):
    eng.nop(nofuse=True)


ORDER = [
    ("xn", 0), ("max", 0, 0), ("max", 0, 1), ("max", 0, 2), ("max", 0, 3), ("max", 0, 4), ("max", 0, 5), ("xn", 1),
    ("max", 0, 6), ("max", 0, 7), ("turn", 0), ("max", 0, 8), ("max", 0, 9), ("qk", 0), ("max", 0, 10), ("turn", 1),
    ("msplit", 0), ("wo",), ("max", 1, 0), ("xn", 2), ("qk", 1), ("xn", 3), ("mturn", 0), ("rot", 0), ("max", 1, 1),
    ("high", 0), ("vmove",), ("rot", 1), ("max", 1, 2), ("v", 0), ("high", 1), ("max", 1, 3), ("split", 0),
    ("turn", 2), ("score", 0, 0), ("score", 0, 1), ("stat",), ("v", 1), ("score", 0, 2), ("turn", 3),
    ("score", 0, 3), ("qk", 2), ("max", 1, 4), ("pv", 0, 0), ("stack", 0, 0), ("max", 1, 5), ("stack", 0, 1),
    ("score", 0, 4), ("pv", 0, 1), ("split", 1), ("score", 0, 5), ("v", 2), ("score", 1, 0), ("score", 1, 1),
    ("add",), ("pv", 0, 2), ("stack", 0, 2), ("score", 1, 2), ("pv", 0, 3), ("score", 1, 3), ("copy", 0),
    ("pv", 1, 0), ("rot", 2), ("stack", 0, 3), ("stack", 1, 0), ("score", 1, 4), ("max", 1, 6), ("max", 1, 7),
    ("high", 2), ("stack", 1, 1), ("max", 1, 8), ("max", 1, 9), ("pv", 1, 1), ("max", 1, 10), ("msplit", 1),
    ("stack", 1, 2), ("xn2",), ("score", 1, 5), ("qk", 3), ("pv", 1, 2), ("rot", 3), ("mturn", 1), ("pv", 1, 3),
    ("norm", 0), ("copy", 1), ("turn2",), ("v", 3), ("split", 2), ("stack", 1, 3), ("high", 3), ("score", 2, 0),
    ("logit",), ("score", 2, 1), ("score", 2, 2), ("stack", 2, 0), ("score", 2, 3), ("pv", 2, 0), ("score", 2, 4),
    ("split", 3), ("stack", 2, 1), ("norm", 1), ("pv", 2, 1), ("score", 2, 5), ("score", 3, 0), ("score", 3, 1),
    ("pv", 2, 2), ("pv", 2, 3), ("score", 3, 2), ("score", 3, 3), ("stack", 2, 2), ("pv", 3, 0), ("score", 3, 4),
    ("score", 3, 5), ("stack", 2, 3), ("copy", 2), ("pv", 3, 1), ("turn1", 0), ("stack", 3, 0), ("pv", 3, 2),
    ("pv", 3, 3), ("norm", 2), ("copy", 3), ("stack", 3, 1), ("norm", 3), ("stack", 3, 2), ("stack", 3, 3),
    ("lturn",), ("turn1", 1),
]
AP_ORDER = [
    ("xn", 0), ("xn", 1), ("max", 0, 0), ("max", 0, 1), ("max", 0, 2), ("max", 0, 3), ("max", 0, 4), ("max", 0, 5),
    ("turn", 0), ("max", 0, 6), ("max", 0, 7), ("vmove",), ("max", 0, 8), ("max", 0, 9), ("max", 0, 10),
    ("msplit", 0), ("turn", 1), ("qk", 0), ("rot", 0), ("mturn", 0), ("max", 1, 0), ("max", 1, 1), ("max", 1, 2),
    ("qk", 1), ("high", 0), ("xn", 2), ("score", 0, 0), ("max", 1, 3), ("v", 0), ("score", 0, 1), ("rot", 1),
    ("v", 1), ("score", 0, 2), ("split", 0), ("max", 1, 4), ("turn", 2), ("pv", 0, 0), ("max", 1, 5), ("max", 1, 6),
    ("high", 1), ("qk", 2), ("score", 0, 3), ("xn", 3), ("score", 0, 4), ("stack", 0, 0), ("rot", 2), ("max", 1, 7),
    ("turn", 3), ("score", 0, 5), ("pv", 0, 1), ("stack", 0, 1), ("score", 1, 0), ("split", 1), ("stack", 0, 2),
    ("max", 1, 8), ("pv", 0, 2), ("pv", 0, 3), ("score", 1, 1), ("stack", 0, 3), ("high", 2), ("max", 1, 9),
    ("max", 1, 10), ("msplit", 1), ("stack", 1, 0), ("score", 1, 2), ("pv", 1, 0), ("stack", 1, 1), ("v", 2),
    ("mturn", 1), ("score", 1, 3), ("stack", 1, 2), ("score", 1, 4), ("qk", 3), ("score", 1, 5), ("copy", 0),
    ("pv", 1, 1), ("score", 2, 0), ("rot", 3), ("score", 2, 1), ("pv", 1, 2), ("split", 2), ("stack", 1, 3),
    ("score", 2, 2), ("pv", 1, 3), ("score", 2, 3), ("norm", 0), ("copy", 1), ("pv", 2, 0), ("high", 3), ("norm", 1),
    ("score", 2, 4), ("stack", 2, 0), ("score", 2, 5), ("pv", 2, 1), ("score", 3, 0), ("pv", 2, 2), ("score", 3, 1),
    ("score", 3, 2), ("pv", 2, 3), ("split", 3), ("stack", 2, 1), ("score", 3, 3), ("pv", 3, 0), ("score", 3, 4),
    ("stack", 2, 2), ("copy", 2), ("score", 3, 5), ("pv", 3, 1), ("stack", 2, 3), ("turn1", 0), ("pv", 3, 2),
    ("stack", 3, 0), ("norm", 2), ("pv", 3, 3), ("copy", 3), ("stack", 3, 1), ("stack", 3, 2), ("norm", 3),
    ("stack", 3, 3), ("turn1", 1), ("v", 3),
]
P_ORDER = [
    ("xn", 0), ("xn", 1), ("turn", 0), ("xn", 2), ("turn", 1), ("qk", 0), ("v", 0), ("rot", 0), ("turn", 2),
    ("xn", 3), ("high", 0), ("qk", 1), ("v", 1), ("rot", 1), ("v", 2), ("split", 0), ("turn", 3), ("high", 1),
    ("qk", 2), ("rot", 2), ("split", 1), ("stack", 0, 0), ("stack", 0, 1), ("stack", 0, 2), ("stack", 0, 3),
    ("qk", 3), ("high", 2), ("rot", 3), ("stack", 1, 0), ("stack", 1, 1), ("stack", 1, 2), ("split", 2),
    ("stack", 1, 3), ("high", 3), ("stack", 2, 0), ("split", 3), ("stack", 2, 1), ("stack", 2, 2), ("v", 3),
    ("stack", 2, 3), ("stack", 3, 0), ("stack", 3, 1), ("stack", 3, 2), ("stack", 3, 3),
]
AM_ORDER = [
    ("max", 0, 0), ("max", 0, 1), ("max", 0, 2), ("max", 0, 3), ("max", 0, 4), ("max", 0, 5), ("max", 0, 6),
    ("max", 0, 7), ("max", 0, 8), ("max", 0, 9), ("max", 0, 10), ("max", 1, 0), ("max", 1, 1), ("max", 1, 2),
    ("vmove",), ("msplit", 0), ("wo",), ("max", 1, 3), ("mturn", 0), ("max", 1, 4), ("max", 1, 5), ("max", 1, 6),
    ("max", 1, 7), ("max", 1, 8), ("score", 0, 0), ("score", 0, 1), ("stat",), ("score", 0, 2), ("max", 1, 9),
    ("score", 0, 3), ("pv", 0, 0), ("max", 1, 10), ("score", 0, 4), ("pv", 0, 1), ("score", 0, 5), ("score", 1, 0),
    ("score", 1, 1), ("pv", 0, 2), ("msplit", 1), ("pv", 0, 3), ("mturn", 1), ("score", 1, 2), ("score", 1, 3),
    ("pv", 1, 0), ("copy", 0), ("score", 1, 4), ("score", 1, 5), ("pv", 1, 1), ("score", 2, 0), ("score", 2, 1),
    ("pv", 1, 2), ("score", 2, 2), ("pv", 1, 3), ("add",), ("norm", 0), ("copy", 1), ("score", 2, 3), ("pv", 2, 0),
    ("norm", 1), ("xn2",), ("score", 2, 4), ("pv", 2, 1), ("score", 2, 5), ("score", 3, 0), ("score", 3, 1),
    ("pv", 2, 2), ("score", 3, 2), ("pv", 2, 3), ("score", 3, 3), ("turn2",), ("pv", 3, 0), ("copy", 2),
    ("score", 3, 4), ("pv", 3, 1), ("score", 3, 5), ("turn1", 0), ("pv", 3, 2), ("norm", 2), ("pv", 3, 3),
    ("copy", 3), ("norm", 3), ("logit",), ("turn1", 1), ("lturn",),
]


class Segment:

    def __init__(self, items, start):
        self.items, self.start = items, start
        n = {k: 0 for k in ("a", "aA", "aD", "p", "pA", "pD")}
        self.index, self.upto, self.order = {}, {}, {"a": [], "p": []}
        for item in items:
            who = users_of(item)
            if not who:
                continue
            ring = "p" if item[0] in P_USERS else "a"
            self.index[item] = (ring, n[ring])
            n[ring] += 1
            for w in who:
                n[ring + w] += 1
            self.upto[item] = dict(n)
            self.order[ring].append(item)
        self.total = n

    def at(self, kind, item):
        return self.start[kind] + self.upto[item][kind]

    def after(self):
        return {k: self.start[k] + self.total[k] for k in self.total}


FREE = {"a": 0, "aA": 1, "aD": 1, "p": 0, "pA": 0, "pD": 0}
A_RING, P_RING = 2, 2


def segments():
    start, out = FREE, []
    for items in [P_ORDER, AP_ORDER] + [ORDER] * (B - 2) + [AM_ORDER]:
        seg = Segment(items, start)
        assert seg.total["a"] % A_RING == 0 and seg.total["p"] % P_RING == 0
        start = seg.after()
        out.append(seg)
    return out


def attention_block(nc, t, x_in, wqkv_in, wo_in, gw_in, rope_in):
    with ExitStack() as ctx:
        def sb(name, shape, dt=F32):
            return ctx.enter_context(nc.sbuf_tensor(name, shape, dt))

        def sem(name):
            return ctx.enter_context(nc.semaphore(name))

        a_ps = ctx.enter_context(nc.psum_tensor("a_ps", [P, A_RING, 2, 512], F32))
        a16 = a_ps[:].rearrange("p r b n -> p r (b n)").bitcast(BF16)
        p_ps = ctx.enter_context(nc.psum_tensor("p_ps", [P, P_RING, 512], F32))
        p16 = p_ps[:].bitcast(BF16)
        att_ps = ctx.enter_context(nc.psum_tensor("att_ps", [P, 2, 512], F32))

        ident, ident16 = t["ident"], t["ident16"]
        attT_hi, attT_lo = t["attT_hi"], t["attT_lo"]
        wo_hi, wo_lo, gw_hi, gw_lo = t["wo_hi"], t["wo_lo"], t["gw_hi"], t["gw_lo"]
        causal = sb("causal", [P, P], BF16)
        rope = sb("rope", [P, TB, 2, DH])
        wqkv_hi = sb("wqkv_hi", [P, KT, 3 * D], F32R)
        wqkv_lo = sb("wqkv_lo", [P, KT, 3 * D], F32R)
        probs = sb("probs", [P, 4, 1024])
        QT = sb("QT", [P, 2, H, S], BF16)
        KTt = sb("KTt", [P, 2, H, S], BF16)
        V = sb("V", [P, TB, H, 2 * DH])
        Vn = sb("Vn", [P, TB, H, DH])
        xn = sb("xn", [P, 2, D])
        xT_hi = sb("xT_hi", [P, 2, KT, P], F32R)
        xT_lo = sb("xT_lo", [P, 2, KT, P], F32R)
        rot = sb("rot", [P, 2, 2 * D])
        rest = sb("rest", [P, 2, 2 * D])
        stack = sb("stack", [P, 2, 2 * H, SR], BF16)
        nmax = sb("nmax", [P, TB, H])
        nrest = sb("nrest", [P, TB, H])
        nparts = sb("nparts", [P, TB, H // OCT, MR, OCT], BF16)
        nT = sb("nT", [MR * OCT, S], BF16)
        att = sb("att", [P, S])
        rsum = sb("rsum", [P, 2, TB, QUAD])
        attn = sb("attn", [P, TB, P])
        stats = sb("stats", [P, NT, 6])
        mv = sb("mv", [P, NT, 2])
        rs = sb("rs", [P, NT])
        mix = sb("mix", [P, TB, D])
        mstats = sb("mstats", [P, TB, 6])
        mmv = sb("mmv", [P, TB, 2])
        mrs = sb("mrs", [P, TB])
        mshift = sb("mshift", [P, TB])
        power = sb("power", [P, NT])
        logT = sb("logT", [P, S])

        x_in_sem = [sem(f"x_in{c}") for c in range(B)]
        rope_in_sem = sem("rope_in_sem")
        wqkv_in_sem = sem("wqkv_in_sem")
        mix_in_sem = sem("mix_in_sem")
        pool_const = sem("pool_const")
        ones_set = sem("ones_set")
        w_hi = sem("w_hi")
        w_lo = sem("w_lo")
        stat_step = sem("stat_step")
        var_ready = sem("var_ready")
        root_ready = sem("root_ready")
        mstep = sem("mstep")
        mvar_ready = sem("mvar_ready")
        eps_added = sem("eps_added")
        meps_added = sem("meps_added")
        mroot_ready = sem("mroot_ready")
        x1_ready = sem("x1_ready")
        mix_ready = sem("mix_ready")
        xn_ready = sem("xn_ready")
        a_ready = sem("a_ready")
        a_act = sem("a_act")
        a_dve = sem("a_dve")
        p_ready = sem("p_ready")
        p_act = sem("p_act")
        p_dve = sem("p_dve")
        roped = sem("roped")
        high_ready = sem("high_ready")
        rest_ready = sem("rest_ready")
        mid_ready = sem("mid_ready")
        low_ready = sem("low_ready")
        nparts_step = sem("nparts_step")
        nparts_ready = sem("nparts_ready")
        v_moved = sem("v_moved")
        nrows_in = [sem(f"nrows_in{g}") for g in range(2)]
        masked = sem("masked")
        pv_done = sem("pv_done")
        att_copied = sem("att_copied")
        rsum_ready = sem("rsum_ready")

        block = ctx.enter_context(nc.Block())
        staged = probs[:].rearrange("p a n -> p (a n)")
        ws_qkv = staged[:, 0:KT * 3 * D].rearrange("p (k n) -> p k n", k=KT)
        ws_wo = staged[:, KT * 3 * D:KT * 4 * D].rearrange("p (k n) -> p k n", k=KT)
        ws_gw = staged[:, KT * 4 * D:KT * (4 * D + P)].rearrange("p (k n) -> p k n", k=KT)
        ready = {"a": a_ready, "p": p_ready}

        def unit(seg, item):
            ring, n = seg.index[item]
            return (seg.start[ring] + n) % (A_RING if ring == "a" else P_RING)

        def wait_unit(eng, seg, item):
            ring = seg.index[item][0]
            eng.wait_ge(ready[ring], seg.at(ring, item))

        def run(eng, emit):
            for n, seg in enumerate(segments()):
                a = n - 1 if n > 0 else None
                p = n if n < B else None
                m = n - 2 if n > 1 else None
                for item in seg.items:
                    emit(seg, item, a, p, m)

        def heads(ap):
            return ap.rearrange("p (h d) -> p h d", d=DH)

        def pairs(ap):
            return ap.rearrange("p (h i e) -> p h i e", i=DH // 2, e=2)

        def slots(ap):
            return ap.rearrange("p h (s d) -> p h s d", d=DH)

        def move_stack(eng, copy, sem_used, seg, item, p):
            s, c = item[1:]
            wait_unit(eng, seg, item)
            dst = (QT if c < 2 else KTt)[0:SR, p % 2, (c % 2) * OCT:(c % 2 + 1) * OCT, s * P:(s + 1) * P]
            copy(dst, p16[0:SR, unit(seg, item), :].rearrange("p (h n) -> p h n", h=OCT)).then_inc(sem_used, 1)

        @block.sync
        def _(sp):
            sp.dma_start(t["x"][:, 0:TB, :], x_in[:, 0:TB, :]).then_inc(x_in_sem[0], 16)
            sp.dma_start(ws_qkv, wqkv_in).then_inc(wqkv_in_sem, 16)
            sp.dma_start(rope[:], rope_in).then_inc(rope_in_sem, 16)
            for c in range(1, B):
                sp.dma_start(t["x"][:, c * TB:(c + 1) * TB, :], x_in[:, c * TB:(c + 1) * TB, :]
                             ).then_inc(x_in_sem[c], 16)
            sp.dma_start(ws_wo, wo_in).then_inc(mix_in_sem, 16)
            sp.dma_start(ws_gw, gw_in).then_inc(mix_in_sem, 16)

            def emit(seg, item, a, p, m):
                kind = item[0]
                if kind == "mturn":
                    g = item[1]
                    sp.wait_ge(a_act, seg.at("aA", item))
                    for part in range(MR):
                        sp.dma_start(QT[SR + part:SR + part + 1, a % 2, g * OCT:(g + 1) * OCT, :],
                                     nT[part * OCT:(part + 1) * OCT, :]).then_inc(nrows_in[g], 16)

            run(sp, emit)

        @block.gpsimd
        def _(pool):
            def scales(n):
                c = slice(0, TB) if n == 0 else slice(TB, NT)
                pool.wait_ge(var_ready, n + 1)
                pool.tensor_scalar(rs[:, c], mv[:, c, 1], EPS, None, ALU.add).then_inc(eps_added, 1)
                pool.wait_ge(eps_added, n + 1)
                pool.tensor_tensor(rs[:, c], rs[:, c], power[:, 0:c.stop - c.start], ALU.pow).then_inc(root_ready, 1)

            pool.memset(ident[:], 1.0).then_inc(pool_const, 1)
            pool.memset(causal[:], 0.0).then_inc(pool_const, 1)
            pool.memset(power[:], -0.5).then_inc(pool_const, 1)
            pool.wait_ge(pool_const, 3)
            pool.affine_select(out=ident[:], in_=ident[:], pattern=[[1, P]], compare_op=ALU.is_equal, fill=0.0,
                               base=0, channel_multiplier=-1).then_inc(pool_const, 1)
            pool.affine_select(out=causal[:], in_=causal[:], pattern=[[-1, P]], compare_op=ALU.is_ge, fill=NEG,
                               base=0, channel_multiplier=1).then_inc(pool_const, 1)
            pool.wait_ge(pool_const, 5)
            pool.tensor_copy(ident16[:], ident[:]).then_inc(pool_const, 1)
            scales(0)
            pool.wait_ge(pool_const, 6)
            pool.memset(V[:, :, :, DH:2 * DH], 1.0).then_inc(ones_set, 1)
            pool.wait_ge(ones_set, 1)
            pool.memset(KTt[SR:P, 0, :, :], 1.0).then_inc(ones_set, 1)
            pool.wait_ge(ones_set, 2)

            def emit(seg, item, a, p, m):
                kind = item[0]
                if kind == "rot":
                    s = item[1]
                    pool.wait_ge(p_dve, seg.at("pD", ("qk", s)))
                    pool.tensor_tensor(rot[:, s % 2, :], rot[:, s % 2, :], rest[:, s % 2, :],
                                       ALU.add).then_inc(roped, 1)
                    if a is None and s == TB - 1:
                        scales(1)
                elif kind == "split":
                    s = item[1]
                    pool.wait_ge(mid_ready, 2 * (p * TB + s + 1))
                    r, sk = heads(rest[:, s % 2, :]), slots(stack[:, s % 2])
                    for h, low in ((0, Q_LOW), (H, K_LOW)):
                        pool.tensor_tensor(sk[:, h:h + H, low, :], r[:, h:h + H, :], sk[:, h:h + H, SLOT_MID, :],
                                           ALU.subtract).then_inc(low_ready, 1)
                elif kind == "vmove" and a == 0:
                    before = [it[0] for it in seg.items[:seg.items.index(item)]]
                    pool.wait_ge(roped, TB + before.count("rot"))
                    pool.wait_ge(low_ready, 2 * (TB + before.count("split")))
                    pool.memset(KTt[SR:P, 1, :, :], 1.0).then_inc(ones_set, 1)
                    pool.wait_ge(ones_set, 3)
                elif kind in ("stat", "add"):
                    n = m * 2 + (kind == "add") + 1
                    pool.wait_ge(mvar_ready, n)
                    pool.tensor_scalar(mrs[:], mmv[:, :, 1], EPS, None, ALU.add).then_inc(meps_added, 1)
                    pool.wait_ge(meps_added, n)
                    pool.tensor_tensor(mrs[:], mrs[:], power[:, 0:TB], ALU.pow).then_inc(mroot_ready, 1)
                elif kind == "score":
                    q, u = item[1:]
                    j, h0, nh = SCU[u]
                    pool.wait_ge(a_act, seg.at("aA", item))
                    w = S - j * P
                    pr = probs[:, (q * len(SCU) + u) % 4, 0:nh * w].rearrange("p (h n) -> p h n", h=nh)[:, :, 0:P]
                    pool.affine_select(out=pr, in_=pr, pattern=[[0, nh], [1, P]], compare_op=ALU.is_ge,
                                       fill=0.0, base=0, channel_multiplier=-1).then_inc(masked, 1)

            run(pool, emit)

        @block.scalar
        def _(act):
            act.nop(nofuse=True).then_inc(a_act, 1)
            act.wait_ge(wqkv_in_sem, 16)
            nc.scalar.copy(wqkv_hi[:], ws_qkv).then_inc(w_hi, 1)

            def emit(seg, item, a, p, m):
                kind = item[0]
                if kind == "turn":
                    wait_unit(act, seg, item)
                    nc.scalar.copy(xT_hi[:, item[1] % 2], p_ps[:, unit(seg, item), 0:KT * P].rearrange(
                        "p (k n) -> p k n", k=KT)).then_inc(p_act, 1)
                elif kind == "v":
                    wait_unit(act, seg, item)
                    if item[1] == 0 and a is not None:
                        act.wait_ge(v_moved, a + 1)
                    nc.scalar.copy(Vn[:, item[1]], heads(p_ps[:, unit(seg, item), 0:D])).then_inc(p_act, 1)
                elif kind == "high":
                    s = item[1]
                    act.wait_ge(roped, p * TB + s + 1)
                    if s >= 2:
                        wait_unit(act, seg, ("stack", s - 2, 3))
                    r, sk = heads(rot[:, s % 2, :]), slots(stack[:, s % 2])
                    for h, where in ((0, Q_HI), (H, K_HI)):
                        src = r[:, h:h + H, :].unsqueeze(2).to_broadcast([P, H, 3, DH])
                        nc.scalar.copy(sk[:, h:h + H, where, :], src).then_inc(high_ready, 1)
                    if a is None and s == TB - 1:
                        act.wait_ge(mix_in_sem, 32)
                        nc.scalar.copy(wo_hi[:], ws_wo).then_inc(w_hi, 1)
                        nc.scalar.copy(gw_hi[:], ws_gw).then_inc(w_hi, 1)
                elif kind == "stack" and "A" in users_of(item):
                    move_stack(act, nc.scalar.copy, p_act, seg, item, p)
                elif kind == "vmove":
                    if a == 0:
                        act.wait_ge(w_lo, 3)
                        act.wait_ge(ones_set, 2)
                    nc.scalar.copy(V[:, :, :, 0:DH], Vn[:]).then_inc(v_moved, 1)
                elif kind == "mturn":
                    wait_unit(act, seg, item)
                    if item[1]:
                        act.wait_ge(nrows_in[0], (a + 1) * 16 * MR)
                    nc.scalar.copy(nT[:], a16[0:MR * OCT, unit(seg, item), 0:S]).then_inc(a_act, 1)
                elif kind == "score":
                    q, u = item[1:]
                    wait_unit(act, seg, item)
                    j, h0, nh = SCU[u]
                    w = S - j * P
                    old = q * len(SCU) + u - 4
                    if old >= 0:
                        act.wait_ge(pv_done, (a * QUAD + old // len(SCU)) * TB + SCU[old % len(SCU)][0] + 1)
                    src = a_ps[:, unit(seg, item)]
                    dst = probs[:, (q * len(SCU) + u) % 4, 0:nh * w]
                    if j == 1:
                        src, dst = src[:, :, 0:w], dst.rearrange("p (h n) -> p h n", h=nh)
                    else:
                        src = src.rearrange("p b n -> p (b n)")[:, 0:nh * w]
                    nc.scalar.activation(dst, src, ACT.Exp, scale=float(DH) ** -0.5).then_inc(a_act, 1)
                elif kind == "copy":
                    n = item[1]
                    act.wait_ge(pv_done, (a * QUAD + n + 1) * TB)
                    if n:
                        wait_unit(act, seg, ("norm", n - 1))
                    nc.scalar.copy(att[:], att_ps[:, n % 2, :]).then_inc(att_copied, 1)
                elif kind == "turn1":
                    wait_unit(act, seg, item)
                    nc.scalar.copy(attT_hi[:, item[1], :], a_ps[:, unit(seg, item), 0, :]).then_inc(a_act, 1)
                elif kind == "wo":
                    wait_unit(act, seg, item)
                    nc.scalar.copy(mix[:], a_ps[:, unit(seg, item)].rearrange("p b (s n) -> p (b s) n", n=D)
                                   ).then_inc(a_act, 1)
                elif kind == "turn2":
                    wait_unit(act, seg, item)
                    nc.scalar.copy(t["x2T_hi"][:, :, m * S:(m + 1) * S], a_ps[:, unit(seg, item)]).then_inc(a_act, 1)
                elif kind == "logit":
                    wait_unit(act, seg, item)
                    nc.scalar.copy(logT[:], a_ps[:, unit(seg, item), 0, :]).then_inc(a_act, 1)

            run(act, emit)

        @block.vector
        def _(dve):
            x_all = t["x"]
            dve.nop(nofuse=True).then_inc(a_dve, 1)

            def statistics(n):
                tiles = range(0, TB) if n == 0 else range(TB, NT)
                for i in tiles:
                    if i % TB == 0:
                        dve.wait_ge(x_in_sem[i // TB], 16)
                    ins = nc.vector.bn_stats(stats[:, i, :], x_all[:, i, :])
                ins.then_inc(stat_step, 1)
                dve.wait_ge(stat_step, n + 1)
                for i in tiles:
                    ins = nc.vector.bn_aggr(mv[:, i, :], stats[:, i, :])
                ins.then_inc(var_ready, 1)

            def weights_low(lo, staging, hi):
                nc.vector.tensor_tensor(lo[:], staging, hi[:].bitcast(F32), ALU.subtract).then_inc(w_lo, 1)

            statistics(0)
            dve.wait_ge(root_ready, 1)

            def moments(before):
                for s in range(TB):
                    ins = nc.vector.bn_stats(mstats[:, s, :], mix[:, s, :])
                ins.then_inc(mstep, 1)
                dve.wait_ge(mstep, before + 1)
                for s in range(TB):
                    ins = nc.vector.bn_aggr(mmv[:, s, :], mstats[:, s, :])
                ins.then_inc(mvar_ready, 1)

            def emit(seg, item, a, p, m):
                kind = item[0]
                if kind == "xn":
                    s = item[1]
                    if s >= 2:
                        wait_unit(dve, seg, ("turn", s - 2))
                    row = p * TB + s
                    if s == 0 and a is not None:
                        dve.wait_ge(root_ready, 2)
                    xr, mean, scale = x_all[:, row, :], mv[:, row, 0:1], rs[:, row:row + 1]
                    nc.vector.tensor_scalar(xn[:, s % 2, :], xr, mean, scale, ALU.subtract,
                                            ALU.mult).then_inc(xn_ready, 1)
                    if a is None and s == 1:
                        dve.wait_ge(w_hi, 1)
                        weights_low(wqkv_lo, ws_qkv, wqkv_hi)
                        dve.wait_ge(rope_in_sem, 16)
                elif kind == "turn":
                    s = item[1]
                    dve.wait_ge(p_act, seg.at("pA", item))
                    nc.vector.tensor_tensor(xT_lo[:, s % 2], p_ps[:, unit(seg, item), 0:KT * P].rearrange(
                        "p (k n) -> p k n", k=KT), xT_hi[:, s % 2].bitcast(F32), ALU.subtract).then_inc(p_dve, 1)
                elif kind == "qk":
                    s = item[1]
                    wait_unit(dve, seg, item)
                    if s >= 2:
                        dve.wait_ge(rest_ready, p * TB + s - 1)
                        dve.wait_ge(low_ready, 2 * (p * TB + s - 1))
                        dve.wait_ge(mid_ready, 2 * (p * TB + s - 1))
                    ps = p_ps[:, unit(seg, item), :]
                    sin = pairs(rope[:, s, 1, :])
                    nc.vector.tensor_tensor(heads(rot[:, s % 2, :]), heads(ps),
                                            rope[:, s, 0, :].unsqueeze(1).to_broadcast([P, 2 * H, DH]), ALU.mult)
                    sd = pairs(rest[:, s % 2, :])
                    for e in range(2):
                        ins = nc.vector.tensor_tensor(sd[:, :, :, e], pairs(ps)[:, :, :, 1 - e],
                                                      sin[:, :, :, e].to_broadcast([P, 2 * H, DH // 2]), ALU.mult)
                    ins.then_inc(p_dve, 1)
                elif kind == "split":
                    s = item[1]
                    dve.wait_ge(high_ready, 2 * (p * TB + s + 1))
                    r, sk = heads(rest[:, s % 2, :]), slots(stack[:, s % 2])
                    nc.vector.tensor_tensor(r, heads(rot[:, s % 2, :]), sk[:, :, SLOT_HI, :],
                                            ALU.subtract).then_inc(rest_ready, 1)
                    dve.wait_ge(rest_ready, p * TB + s + 1)
                    for h, where in ((0, Q_MID), (H, K_MID)):
                        src = r[:, h:h + H, :].unsqueeze(2).to_broadcast([P, H, 2, DH])
                        nc.vector.tensor_copy(sk[:, h:h + H, where, :], src).then_inc(mid_ready, 1)
                    if a is None and s == 1:
                        statistics(1)
                    if a is None and s == 3:
                        dve.wait_ge(w_hi, 3)
                        weights_low(wo_lo, ws_wo, wo_hi)
                        weights_low(gw_lo, ws_gw, gw_hi)
                elif kind == "stack" and "D" in users_of(item):
                    move_stack(dve, nc.vector.tensor_copy, p_dve, seg, item, p)
                elif kind == "max":
                    g, u = item[1:]
                    wait_unit(dve, seg, item)
                    i, h0, nh, hb = MAXU[u]
                    src = a_ps[:, unit(seg, item), :, 0:hb * (i + 1) * P].rearrange("p b (h n) -> p b h n", h=hb)
                    h = g * OCT + h0
                    nc.vector.tensor_reduce(nmax[:, i, h:h + nh].rearrange("p (b h) -> p b h", h=hb), src,
                                            AX.X, ALU.max, negate=True).then_inc(a_dve, 1)
                elif kind == "msplit":
                    g = item[1]
                    o = slice(g * OCT, (g + 1) * OCT)
                    base = (a * 2 + g) * 3
                    dve.wait_ge(a_dve, seg.at("aD", ("max", g, len(MAXU) - 1)))
                    nc.vector.tensor_copy(nparts[:, :, g, 0, :], nmax[:, :, o]).then_inc(nparts_step, 1)
                    dve.wait_ge(nparts_step, base + 1)
                    nc.vector.tensor_tensor(nrest[:, :, o], nmax[:, :, o], nparts[:, :, g, 0, :],
                                            ALU.subtract).then_inc(nparts_step, 1)
                    dve.wait_ge(nparts_step, base + 2)
                    nc.vector.tensor_copy(nparts[:, :, g, 1, :], nrest[:, :, o]).then_inc(nparts_step, 1)
                    dve.wait_ge(nparts_step, base + 3)
                    nc.vector.tensor_tensor(nparts[:, :, g, 2, :], nrest[:, :, o], nparts[:, :, g, 1, :],
                                            ALU.subtract).then_inc(nparts_ready, 1)
                elif kind == "norm":
                    n = item[1]
                    wait_unit(dve, seg, item)
                    if n == 2:
                        wait_unit(dve, seg, ("turn1", 0))
                    o = a_ps[:, unit(seg, item), 0, :].rearrange("p (s a d) -> p s a d", s=TB, a=QUAD)
                    nc.vector.reciprocal(rsum[:, n % 2], o[:, :, :, DH]).then_inc(rsum_ready, 1)
                    dve.wait_ge(rsum_ready, a * QUAD + n + 1)
                    nc.vector.tensor_tensor(
                        attn[:, :, n % 2 * QUAD * DH:(n % 2 + 1) * QUAD * DH].rearrange("p s (a d) -> p s a d", a=QUAD),
                        o[:, :, :, 0:DH], rsum[:, n % 2].unsqueeze(3).to_broadcast([P, TB, QUAD, DH]),
                        ALU.mult).then_inc(a_dve, 1)
                elif kind == "turn1":
                    dve.wait_ge(a_act, seg.at("aA", item))
                    k = item[1]
                    nc.vector.tensor_tensor(attT_lo[:, k, :], a_ps[:, unit(seg, item), 0, :],
                                            attT_hi[:, k, :].bitcast(F32), ALU.subtract).then_inc(a_dve, 1)
                elif kind == "stat":
                    dve.wait_ge(a_act, seg.at("aA", ("wo",)))
                    moments(m * 5)
                elif kind == "add":
                    dve.wait_ge(mroot_ready, m * 2 + 1)
                    nc.vector.scalar_tensor_tensor(out=mshift[:], in0=mmv[:, :, 0], scalar=-1.0, in1=mrs[:],
                                                   op0=ALU.mult, op1=ALU.mult).then_inc(mstep, 1)
                    for s in range(TB):
                        ins = nc.vector.scalar_tensor_tensor(out=mix[:, s, :], in0=mix[:, s, :], scalar=mrs[:, s:s + 1],
                                                             in1=x_all[:, m * TB + s, :], op0=ALU.mult, op1=ALU.add)
                    ins.then_inc(mstep, 1)
                    dve.wait_ge(mstep, m * 5 + 3)
                    for s in range(TB):
                        ins = nc.vector.tensor_scalar(mix[:, s, :], mix[:, s, :], mshift[:, s:s + 1], None, ALU.add)
                    ins.then_inc(mstep, 1)
                    dve.wait_ge(mstep, m * 5 + 4)
                    moments(m * 5 + 4)
                    nc.vector.tensor_copy(x_all[:, m * TB:(m + 1) * TB, :], mix[:]).then_inc(x1_ready, 1)
                elif kind == "xn2":
                    dve.wait_ge(mroot_ready, m * 2 + 2)
                    dve.wait_ge(x1_ready, m + 1)
                    for s in range(TB):
                        ins = nc.vector.tensor_scalar(mix[:, s, :], mix[:, s, :], mmv[:, s, 0:1], mrs[:, s:s + 1],
                                                      ALU.subtract, ALU.mult)
                    ins.then_inc(mix_ready, 1)
                elif kind == "turn2":
                    dve.wait_ge(a_act, seg.at("aA", item))
                    cols = slice(m * S, (m + 1) * S)
                    nc.vector.tensor_tensor(t["x2T_lo"][:, :, cols], a_ps[:, unit(seg, item)],
                                            t["x2T_hi"][:, :, cols].bitcast(F32), ALU.subtract).then_inc(a_dve, 1)
                elif kind == "lturn":
                    wait_unit(dve, seg, item)
                    nc.vector.tensor_copy(t["logit"][:, m * TB:(m + 1) * TB, :], a_ps[:, unit(seg, item), 0, :].rearrange(
                        "p (s n) -> p s n", s=TB)[:, :, 0:GC]).then_inc(a_dve, 1)

            run(dve, emit)

        @block.tensor
        def _(pe):
            pe.wait_ge(pool_const, 6)

            def take(seg, item):
                ring, n = seg.index[item]
                size = A_RING if ring == "a" else P_RING
                used = {"A": a_act if ring == "a" else p_act, "D": a_dve if ring == "a" else p_dve}
                if n >= size:
                    old = seg.order[ring][n - size]
                    for who in users_of(old):
                        pe.wait_ge(used[who], seg.at(ring + who, old))
                else:
                    for who in "AD":
                        kind = ring + who
                        if seg.start[kind]:
                            pe.wait_ge(used[who], seg.start[kind])
                return unit(seg, item)

            def emit(seg, item, a, p, m):
                kind = item[0]
                if kind == "turn":
                    s = item[1]
                    pe.wait_ge(xn_ready, p * TB + s + 1)
                    r = take(seg, item)
                    for k in range(KT):
                        ins = nc.tensor.transpose(p_ps[:, r, k * P:(k + 1) * P], xn[:, s % 2, k * P:(k + 1) * P],
                                                  ident[:])
                    ins.then_inc(p_ready, 1)
                elif kind in ("qk", "v"):
                    s = item[1]
                    pe.wait_ge(p_act, seg.at("pA", ("turn", s)))
                    pe.wait_ge(p_dve, seg.at("pD", ("turn", s)))
                    if a is None and s == 0:
                        pe.wait_ge(w_lo, 1)
                    r = take(seg, item)
                    cols = slice(0, 2 * D) if kind == "qk" else slice(2 * D, 3 * D)
                    for k in range(KT):
                        ins = products(nc, p_ps[:, r, 0:cols.stop - cols.start],
                                       (xT_hi[:, s % 2, k, :], xT_lo[:, s % 2, k, :]),
                                       (wqkv_hi[:, k, cols], wqkv_lo[:, k, cols]), k == 0, k == KT - 1)
                    ins.then_inc(p_ready, 1)
                elif kind == "stack":
                    s, c = item[1:]
                    pe.wait_ge(low_ready, 2 * (p * TB + s) + 1 + c // 2)
                    r = take(seg, item)
                    for h in range(OCT):
                        ins = nc.tensor.transpose(p16[0:SR, r, h * P:(h + 1) * P], stack[:, s % 2, c * OCT + h, :],
                                                  ident16[:])
                    ins.then_inc(p_ready, 1)
                elif kind == "max":
                    g, u = item[1:]
                    if g == 0 and u == 0:
                        pe.wait_ge(p_act, seg.start["pA"])
                        pe.wait_ge(p_dve, seg.start["pD"])
                        pe.wait_ge(ones_set, 2 if a == 0 else 3)
                        pe.wait_ge(w_lo, 3)
                    r = take(seg, item)
                    i, h0, nh, hb = MAXU[u]
                    w = (i + 1) * P
                    for n in range(nh):
                        h = g * OCT + h0 + n
                        o = (n % hb) * w
                        nc.tensor.matmul(a_ps[:, r, n // hb, o:o + w], QT[0:SR, a % 2, h, i * P:(i + 1) * P],
                                         KTt[0:SR, a % 2, h, 0:w], start=True, stop=False, skip_group_check=True)
                        ins = nc.tensor.matmul(a_ps[:, r, n // hb, o + w - P:o + w], ident16[:], causal[:],
                                               start=False, stop=True, skip_group_check=True)
                    ins.then_inc(a_ready, 1)
                elif kind == "mturn":
                    g = item[1]
                    pe.wait_ge(nparts_ready, a * 2 + g + 1)
                    r = take(seg, item)
                    for s in range(TB):
                        ins = nc.tensor.transpose(a16[0:MR * OCT, r, s * P:(s + 1) * P],
                                                  nparts[:, s, g].rearrange("p m h -> p (m h)"), ident16[:])
                    ins.then_inc(a_ready, 1)
                elif kind == "score":
                    q, u = item[1:]
                    if u == 0:
                        pe.wait_ge(nrows_in[q * QUAD // OCT], (a + 1) * 16 * MR)
                    r = take(seg, item)
                    j, h0, nh = SCU[u]
                    w = S - j * P
                    for n in range(nh):
                        h = q * QUAD + h0 + n
                        bank, o = (n, 0) if j < 2 else (n * w // 512, n * w % 512)
                        ins = nc.tensor.matmul(a_ps[:, r, bank, o:o + w], KTt[0:QR, a % 2, h, j * P:(j + 1) * P],
                                               QT[0:QR, a % 2, h, j * P:S], start=True, stop=True)
                    ins.then_inc(a_ready, 1)
                elif kind == "pv":
                    q, j = item[1:]
                    pe.wait_ge(masked, (a * QUAD + q) * len(SCU) + SC_LAST[j] + 1)
                    if j == 0:
                        if q == 0:
                            pe.wait_ge(v_moved, a + 1)
                        if q >= 2:
                            pe.wait_ge(att_copied, a * QUAD + q - 1)
                    w = S - j * P
                    for n in range(QUAD):
                        u = next(u for u, (jj, h0, nh) in enumerate(SCU) if jj == j and h0 <= n < h0 + nh)
                        o = (n - SCU[u][1]) * w
                        ins = nc.tensor.matmul(att_ps[32 * n:32 * n + 32, q % 2, j * P:S], V[:, j, q * QUAD + n, :],
                                               probs[:, (q * len(SCU) + u) % 4, o:o + w],
                                               start=(j == 0), stop=(j == TB - 1))
                    ins.then_inc(pv_done, 1)
                elif kind == "norm":
                    n = item[1]
                    pe.wait_ge(att_copied, a * QUAD + n + 1)
                    r = take(seg, item)
                    for s in range(TB):
                        ins = nc.tensor.transpose(a_ps[:, r, 0, s * P:(s + 1) * P], att[:, s * P:(s + 1) * P],
                                                  ident[:])
                    ins.then_inc(a_ready, 1)
                elif kind == "turn1":
                    k = item[1]
                    pe.wait_ge(a_dve, seg.at("aD", ("norm", 2 * k + 1)))
                    r = take(seg, item)
                    for s in range(TB):
                        ins = nc.tensor.transpose(a_ps[:, r, 0, s * P:(s + 1) * P], attn[:, s, :],
                                                  ident[:])
                    ins.then_inc(a_ready, 1)
                elif kind == "wo":
                    pe.wait_ge(a_dve, seg.start["aD"])
                    r = take(seg, item)
                    for s in range(TB):
                        cols = slice(s * P, (s + 1) * P)
                        o = a_ps[:, r, s // 2, s % 2 * D:(s % 2 + 1) * D]
                        for k in range(KT):
                            ins = products(nc, o, (attT_hi[:, k, cols], attT_lo[:, k, cols]),
                                           (wo_hi[:, k, :], wo_lo[:, k, :]), k == 0, k == KT - 1)
                    ins.then_inc(a_ready, 1)
                elif kind == "turn2":
                    pe.wait_ge(mix_ready, m + 1)
                    r = take(seg, item)
                    for s in range(TB):
                        for k in range(KT):
                            ins = nc.tensor.transpose(a_ps[:, r, k, s * P:(s + 1) * P], mix[:, s, k * P:(k + 1) * P],
                                                      ident[:])
                    ins.then_inc(a_ready, 1)
                elif kind == "logit":
                    pe.wait_ge(a_dve, seg.at("aD", ("turn2",)))
                    r = take(seg, item)
                    cols = slice(m * S, (m + 1) * S)
                    for k in range(KT):
                        ins = products(nc, a_ps[:, r, 0, :], (gw_hi[:, k, :], gw_lo[:, k, :]),
                                       (t["x2T_hi"][:, k, cols], t["x2T_lo"][:, k, cols]), k == 0, k == KT - 1)
                    ins.then_inc(a_ready, 1)
                elif kind == "lturn":
                    pe.wait_ge(a_act, seg.at("aA", ("logit",)))
                    r = take(seg, item)
                    for s in range(TB):
                        ins = nc.tensor.transpose(a_ps[:, r, 0, s * P:(s + 1) * P], logT[:, s * P:(s + 1) * P],
                                                  ident[:])
                    ins.then_inc(a_ready, 1)

            run(pe, emit)


def products(nc, out, left, right, first, last):
    for i, (l, r) in enumerate(((0, 0), (0, 1), (1, 0))):
        ins = nc.tensor.matmul(out, left[l], right[r], start=first and i == 0, stop=last and i == 2)
    return ins


def ffn_block(nc, t, w_in, sel_in, out):
    with ExitStack() as ctx:
        def sb(name, shape, dt=F32):
            return ctx.enter_context(nc.sbuf_tensor(name, shape, dt))

        def sem(name):
            return ctx.enter_context(nc.semaphore(name))

        def pb(name, shape):
            return ctx.enter_context(nc.psum_tensor(name, shape, F32))

        gate_ps = pb("gate_ps", [P, 2, S])
        up_ps = pb("up_ps", [P, 2, S])
        comb_ps = pb("comb_ps", [P, 2, S])
        y_ps = pb("y_ps", [P, TB, D])

        last_rows = slice((B - 1) * TB, NT)
        last_cols = slice((B - 1) * S, B * S)
        x_all, ident, ident16, logit = t["x"], t["ident"], t["ident16"], t["logit"]
        mix = sb("fmix", [P, TB, D])
        mstats = sb("fmstats", [P, TB, 6])
        mmv = sb("fmmv", [P, TB, 2])
        mrs = sb("fmrs", [P, TB])
        mshift = sb("fmshift", [P, TB])
        logT = sb("flogT", [P, S])

        eprob = sb("eprob", [P, NT, GC])
        prob = sb("prob", [P, NT, E])
        big = sb("big", [P, 3, NT])
        top = sb("top", [P, NT, 8])
        more = sb("more", [P, NT, E])
        same = sb("same", [P, NT, E])
        count = sb("count", [P, 2, NT, E + E // 2])
        comb = sb("comb", [P, NT, GC])
        crest = sb("crest", [P, NT, GC])
        cparts = sb("cparts", [P, NT, P], BF16)
        combT = sb("combT", [P, B * S], BF16)
        turned = [ps[:].bitcast(BF16)[:, i, 0:S] for ps, i in ((gate_ps, 0), (gate_ps, 1), (up_ps, 0), (comb_ps, 0))]
        PARTS = (slice(0, (B - 1) * TB), last_rows)

        GU = 2 * KT * P
        STAGES = 4
        w_stage = sb("w_stage", [P, STAGES, GU + D])
        w_hi = sb("w_hi_sb", [P, 2, CH, GU + D], F32R)
        w_lo = sb("w_lo_sb", [P, 2, CH, GU + D], F32R)
        select = sb("select", [P, FT, P], BF16)
        silu = sb("silu", [P, 2, S])
        weighted = sb("weighted", [P, 2, S])
        hid = sb("hid", [P, 2, S])
        hid_hi = sb("hid_hi", [P, 2, S], F32R)
        hid_lo = sb("hid_lo", [P, 2, S], F32R)
        ysum = sb("ysum", [P, NT, D])
        stats = sb("ystats", [P, TB, 6])
        mv = sb("ymv", [P, TB, 2])
        rs = sb("yrs", [P, TB])
        shift = sb("yshift", [P, TB])
        power = sb("ypower", [P, TB])

        wo_ready = sem("wo_ready")
        mix_copied = sem("mix_copied")
        fm_step = sem("fm_step")
        fm_var = sem("fm_var")
        fm_eps = sem("fm_eps")
        fm_root = sem("fm_root")
        fm_normed = sem("fm_normed")
        x2_turned = sem("x2_turned")
        x2_hi = sem("x2_hi")
        x2_lo = sem("x2_lo")
        logT_ready = sem("logT_ready")
        logT_copied = sem("logT_copied")
        logit_turned = sem("logit_turned")
        logit_ready = sem("logit_ready")
        const_set = sem("mconst_set")
        step_done = sem("mstep_done")
        centred = sem("centred")
        exp_ready = sem("exp_ready")
        cparts_ready = sem("cparts_ready")
        c_ready = sem("c_ready")
        comb_copied = sem("comb_copied")
        stage_in = [sem(f"stage_in{i}") for i in range(STAGES)]
        select_in = sem("select_in")
        whi_done = sem("whi_done")
        wlo_done = sem("wlo_done")
        gate_ready = sem("gate_ready")
        up_ready = sem("up_ready")
        silu_done = sem("silu_done")
        weighted_done = sem("weighted_done")
        hid_done = sem("hid_done")
        hid_hi_done = sem("hid_hi_done")
        hid_lo_done = sem("hid_lo_done")
        down_done = sem("down_done")
        y_added = sem("y_added")
        y_step = sem("y_step")
        y_var = sem("y_var")
        y_eps = sem("y_eps")
        y_root = sem("y_root")
        y_out = sem("y_out")
        out_stored = sem("out_stored")

        BC = B * CH
        LOOPS = (NCH - 3) // 2
        assert NCH == 2 * LOOPS + 3 and CH == STAGES and B >= 3
        TURN2 = CH
        ROUTE = CH + 1
        TURN_COMB = (B - 1) * CH - 2

        block = ctx.enter_context(nc.Block())

        def steps(eng, emit):
            for k in range(BC):
                emit(0, k)
            with eng.Fori(0, LOOPS) as turn:
                for k in range(2 * BC):
                    emit(turn * 2 + 1, k)
            for k in range(2 * BC):
                emit(NCH - 2, k)

        def place(chunk, k):
            odd = 0 if isinstance(chunk, int) and chunk == 0 else 1
            return (odd + k // BC) % 2, k // CH % B, k % CH

        def first(chunk):
            return isinstance(chunk, int) and chunk == 0

        def final(chunk, k):
            return isinstance(chunk, int) and chunk > 0 and k >= BC

        def is_last(chunk, k):
            return final(chunk, k) and k == 2 * BC - 1

        @block.sync
        def _(sp):
            for a in range(STAGES):
                sp.dma_start(w_stage[:, a, :], w_in[a]).then_inc(stage_in[a], 16)
            sp.dma_start(select[:], sel_in).then_inc(select_in, 16)
            with sp.Fori(1, FT // STAGES) as i:
                for a in range(STAGES):
                    sp.wait_ge(wlo_done, (i - 1) * STAGES + a + 1)
                    sp.dma_start(w_stage[:, a, :], w_in[bass.ds(i * STAGES + a, 1), :, :].rearrange(
                        "o p n -> (o p) n")).then_inc(stage_in[a], 16)
            for b in range(B):
                sp.wait_ge(y_out, b + 1)
                sp.dma_start(out[:, b * TB:(b + 1) * TB, :], ysum[:, b * TB:(b + 1) * TB, :]).then_inc(out_stored, 16)
            sp.wait_ge(out_stored, 16 * B)

        @block.gpsimd
        def _(pool):
            pool.memset(count[:], 0.0).then_inc(const_set, 1)
            pool.memset(cparts[:], 0.0).then_inc(const_set, 1)
            pool.wait_ge(const_set, 2)
            pool.memset(power[:], -0.5).then_inc(const_set, 1)
            pool.wait_ge(const_set, 3)
            pool.memset(ysum[:], 0.0).then_inc(y_added, 1)
            pool.wait_ge(y_added, 1)

            def split(chunk, par):
                for j in range(CH):
                    tile = chunk * CH + j
                    pool.wait_ge(stage_in[j], chunk * 16 + 16)
                    apart(pool)
                    pool.tensor_copy(w_hi[:, par, j, :], w_stage[:, j, :]).then_inc(whi_done, 1)
                    pool.wait_ge(whi_done, tile + 1)
                    pool.tensor_tensor(w_lo[:, par, j, :], w_stage[:, j, :], w_hi[:, par, j, :].bitcast(F32),
                                       ALU.subtract).then_inc(wlo_done, 1)

            split(0, 0)
            for i in range(2):
                pool.wait_ge(fm_var, i + 1)
                pool.tensor_scalar(mrs[:], mmv[:, :, 1], EPS, None, ALU.add).then_inc(fm_eps, 1)
                pool.wait_ge(fm_eps, i + 1)
                pool.tensor_tensor(mrs[:], mrs[:], power[:], ALU.pow).then_inc(fm_root, 1)
            with pool.Fori(0, LOOPS) as turn:
                for half in range(2):
                    pool.wait_ge(y_added, turn * (2 * B) + half * B + 1)
                    split(turn * 2 + 1 + half, 1 - half)
            for half in range(2):
                pool.wait_ge(y_added, (NCH - 3 + half) * B + 1)
                split(NCH - 2 + half, 1 - half)
            for b in range(B):
                pool.wait_ge(y_var, b + 1)
                pool.tensor_scalar(rs[:], mv[:, :, 1], EPS, None, ALU.add).then_inc(y_eps, 1)
                pool.wait_ge(y_eps, b + 1)
                pool.tensor_tensor(rs[:], rs[:], power[:], ALU.pow).then_inc(y_root, 1)

        @block.scalar
        def _(act):
            def exponentials(part):
                o = PARTS[part]
                act.wait_ge(centred, part + 1)
                nc.scalar.activation(eprob[:, o, E:GC], logit[:, o, E:GC], ACT.Exp, scale=-1.0).then_inc(exp_ready, 1)
                nc.scalar.activation(eprob[:, o, 0:E], eprob[:, o, 0:E], ACT.Exp).then_inc(exp_ready, 1)

            def copy_comb(b):
                act.wait_ge(c_ready, b + 1)
                nc.scalar.copy(combT[:, b * S:(b + 1) * S], turned[b]).then_inc(comb_copied, 1)

            exponentials(0)
            act.wait_ge(wo_ready, 1)
            nc.scalar.copy(mix[:], y_ps[:]).then_inc(mix_copied, 1)
            for b in range(0, B - 1, 2):
                copy_comb(b)

            def activate(k, n):
                act.wait_ge(gate_ready, n + 1)
                nc.scalar.activation(silu[:, k % 2, :], gate_ps[:, k % 2, :], ACT.Silu).then_inc(silu_done, 1)

            def emit(chunk, k):
                n = chunk * BC + k
                act.wait_ge(hid_done, n + 1)
                nc.scalar.copy(hid_hi[:, k % 2, :], hid[:, k % 2, :]).then_inc(hid_hi_done, 1)
                if first(chunk) and k == TURN2:
                    act.wait_ge(x2_turned, 1)
                    nc.scalar.copy(t["x2T_hi"][:, :, last_cols], y_ps[:].rearrange("p (c s) n -> p c (s n)", c=KT)
                                   ).then_inc(x2_hi, 1)
                if not is_last(chunk, k):
                    activate(k + 1, n + 1)
                if first(chunk):
                    if k == TURN2:
                        act.wait_ge(logT_ready, 1)
                        nc.scalar.copy(logT[:], y_ps[:, 0:2, :].rearrange("p s n -> p (s n)")).then_inc(logT_copied, 1)
                    elif k == ROUTE:
                        exponentials(1)
                    elif k == TURN_COMB:
                        copy_comb(B - 1)

            activate(0, 0)
            steps(act, emit)

        @block.vector
        def _(dve):
            links = 0

            def link(ins):
                nonlocal links
                links += 1
                ins.then_inc(step_done, 1)
                dve.wait_ge(step_done, links)

            def route(part):
                o = PARTS[part]
                wide = [P, o.stop - o.start, E]

                def over(ap):
                    return ap.unsqueeze(2).to_broadcast(wide)

                link(nc.vector.tensor_reduce(big[:, 0, o], logit[:, o, 0:E], AX.X, ALU.max))
                nc.vector.tensor_tensor(eprob[:, o, 0:E], logit[:, o, 0:E], over(big[:, 0, o]),
                                        ALU.subtract).then_inc(centred, 1)
                yield
                dve.wait_ge(exp_ready, 2 * part + 2)
                nc.vector.tensor_reduce(big[:, 1, o], eprob[:, o, 0:E], AX.X, ALU.add)
                link(nc.vector.tensor_scalar(crest[:, o, E], eprob[:, o, E], 1.0, None, ALU.add))
                nc.vector.reciprocal(big[:, 2, o], big[:, 1, o])
                link(nc.vector.reciprocal(comb[:, o, E], crest[:, o, E]))
                link(nc.vector.tensor_tensor(prob[:, o], eprob[:, o, 0:E], over(big[:, 2, o]), ALU.mult))
                for i in range(o.start, o.stop):
                    ins = nc.vector.max(top[:, i, :], prob[:, i, :])
                link(ins)
                yield
                fourth = over(top[:, o, K - 1])
                nc.vector.tensor_tensor(more[:, o], prob[:, o], fourth, ALU.is_gt)
                dve.wait_ge(const_set, 3)
                z = E // 2
                nc.vector.tensor_tensor(same[:, o], prob[:, o], fourth, ALU.is_equal)
                link(nc.vector.tensor_tensor(count[:, 0, o, z:], prob[:, o], fourth, ALU.is_equal))
                nc.vector.tensor_reduce(big[:, 0, o], more[:, o], AX.X, ALU.add)
                for i in range(4):
                    old, new = count[:, i % 2, o], count[:, 1 - i % 2, o]
                    link(nc.vector.tensor_tensor(new[:, :, z:], old[:, :, z:], old[:, :, z - 2 ** i:z + E - 2 ** i],
                                                 ALU.add))
                yield
                link(nc.vector.tensor_tensor(crest[:, o, 0:E], count[:, 0, o, z:], over(big[:, 0, o]), ALU.add))
                link(nc.vector.scalar_tensor_tensor(out=same[:, o], in0=crest[:, o, 0:E], scalar=K + 0.5,
                                                    in1=same[:, o], op0=ALU.is_lt, op1=ALU.mult))
                link(nc.vector.tensor_tensor(more[:, o], more[:, o], same[:, o], ALU.add))
                link(nc.vector.tensor_tensor(crest[:, o, 0:E], more[:, o], prob[:, o], ALU.mult))
                yield
                link(nc.vector.tensor_reduce(big[:, 0, o], crest[:, o, 0:E], AX.X, ALU.add))
                link(nc.vector.reciprocal(big[:, 1, o], big[:, 0, o]))
                link(nc.vector.tensor_tensor(comb[:, o, 0:E], crest[:, o, 0:E], over(big[:, 1, o]), ALU.mult))
                link(nc.vector.tensor_copy(cparts[:, o, 0:GC], comb[:, o]))
                link(nc.vector.tensor_tensor(crest[:, o], comb[:, o], cparts[:, o, 0:GC], ALU.subtract))
                link(nc.vector.tensor_copy(cparts[:, o, GC:2 * GC], crest[:, o]))
                nc.vector.tensor_tensor(cparts[:, o, 2 * GC:3 * GC], crest[:, o], cparts[:, o, GC:2 * GC],
                                        ALU.subtract).then_inc(cparts_ready, 1)
                yield

            def after_attention():
                def moments(n):
                    for s in range(TB):
                        ins = nc.vector.bn_stats(mstats[:, s, :], mix[:, s, :])
                    ins.then_inc(fm_step, 1)
                    dve.wait_ge(fm_step, n)
                    for s in range(TB):
                        ins = nc.vector.bn_aggr(mmv[:, s, :], mstats[:, s, :])
                    ins.then_inc(fm_var, 1)

                dve.wait_ge(mix_copied, 1)
                moments(1)
                yield
                dve.wait_ge(fm_root, 1)
                nc.vector.scalar_tensor_tensor(out=mshift[:], in0=mmv[:, :, 0], scalar=-1.0, in1=mrs[:],
                                               op0=ALU.mult, op1=ALU.mult).then_inc(fm_step, 1)
                for s in range(TB):
                    ins = nc.vector.scalar_tensor_tensor(out=mix[:, s, :], in0=mix[:, s, :], scalar=mrs[:, s:s + 1],
                                                         in1=x_all[:, last_rows.start + s, :], op0=ALU.mult,
                                                         op1=ALU.add)
                ins.then_inc(fm_step, 1)
                yield
                dve.wait_ge(fm_step, 3)
                for s in range(TB):
                    ins = nc.vector.tensor_scalar(mix[:, s, :], mix[:, s, :], mshift[:, s:s + 1], None, ALU.add)
                ins.then_inc(fm_step, 1)
                dve.wait_ge(fm_step, 4)
                moments(5)
                nc.vector.tensor_copy(x_all[:, last_rows, :], mix[:]).then_inc(fm_step, 1)
                yield
                dve.wait_ge(fm_root, 2)
                dve.wait_ge(fm_step, 6)
                for s in range(TB):
                    ins = nc.vector.tensor_scalar(mix[:, s, :], mix[:, s, :], mmv[:, s, 0:1], mrs[:, s:s + 1],
                                                  ALU.subtract, ALU.mult)
                ins.then_inc(fm_normed, 1)
                yield

            for _ in route(0):
                pass
            for b in range(1, B - 1, 2):
                dve.wait_ge(c_ready, b + 1)
                nc.vector.tensor_copy(combT[:, b * S:(b + 1) * S], turned[b]).then_inc(comb_copied, 1)

            def combine(k, n):
                dve.wait_ge(silu_done, n + 1)
                nc.vector.tensor_tensor(weighted[:, k % 2, :], silu[:, k % 2, :], comb_ps[:, k % 2, :],
                                        ALU.mult).then_inc(weighted_done, 1)
                dve.wait_ge(up_ready, n + 1)
                dve.wait_ge(weighted_done, n + 1)
                nc.vector.tensor_tensor(hid[:, k % 2, :], weighted[:, k % 2, :], up_ps[:, k % 2, :],
                                        ALU.mult).then_inc(hid_done, 1)

            def add_y(b, n):
                dve.wait_ge(down_done, n)
                ys = ysum[:, b * TB:(b + 1) * TB, :]
                nc.vector.tensor_tensor(ys, ys, y_ps[:], ALU.add).then_inc(y_added, 1)

            def finish(b, part):
                tiles = [(s, b * TB + s) for s in range(TB)]
                if part == 0:
                    dve.wait_ge(y_added, (NCH - 1) * B + b + 2)
                    for s, i in tiles:
                        ins = nc.vector.bn_stats(stats[:, s, :], ysum[:, i, :])
                    ins.then_inc(y_step, 1)
                    dve.wait_ge(y_step, b * 3 + 1)
                    for s, i in tiles:
                        ins = nc.vector.bn_aggr(mv[:, s, :], stats[:, s, :])
                    ins.then_inc(y_var, 1)
                elif part == 1:
                    dve.wait_ge(y_root, b + 1)
                    nc.vector.scalar_tensor_tensor(out=shift[:], in0=mv[:, :, 0], scalar=-1.0, in1=rs[:],
                                                   op0=ALU.mult, op1=ALU.mult).then_inc(y_step, 1)
                    for s, i in tiles:
                        ins = nc.vector.scalar_tensor_tensor(out=ysum[:, i, :], in0=ysum[:, i, :],
                                                             scalar=rs[:, s:s + 1], in1=t["x"][:, i, :],
                                                             op0=ALU.mult, op1=ALU.add)
                    ins.then_inc(y_step, 1)
                else:
                    dve.wait_ge(y_step, b * 3 + 3)
                    for s, i in tiles:
                        ins = nc.vector.tensor_scalar(ysum[:, i, :], ysum[:, i, :], shift[:, s:s + 1], None, ALU.add)
                    ins.then_inc(y_out, 1)

            mixing, routing = after_attention(), route(1)

            def emit(chunk, k):
                n = chunk * BC + k
                dve.wait_ge(hid_hi_done, n + 1)
                nc.vector.tensor_tensor(hid_lo[:, k % 2, :], hid[:, k % 2, :], hid_hi[:, k % 2, :].bitcast(F32),
                                        ALU.subtract).then_inc(hid_lo_done, 1)
                _, b, j = place(chunk, k)
                if first(chunk) and k == TURN2:
                    dve.wait_ge(x2_hi, 1)
                    nc.vector.tensor_tensor(t["x2T_lo"][:, :, last_cols], y_ps[:].rearrange("p (c s) n -> p c (s n)", c=KT),
                                            t["x2T_hi"][:, :, last_cols].bitcast(F32), ALU.subtract).then_inc(x2_lo, 1)
                if not is_last(chunk, k):
                    combine(k + 1, n + 1)
                if first(chunk):
                    if k < TURN2:
                        next(mixing)
                    elif k == TURN2:
                        dve.wait_ge(logit_turned, 1)
                        nc.vector.tensor_copy(logit[:, last_rows, :], y_ps[:, 2:4, :].rearrange(
                            "p a (s n) -> p (a s) n", n=P)[:, :, 0:GC]).then_inc(logit_ready, 1)
                        dve.wait_ge(logit_ready, 1)
                    elif k < ROUTE + 5:
                        next(routing)
                if j == CH - 1:
                    add_y(b, n + 1)
                elif final(chunk, k) and b:
                    finish(b - 1, j)

            combine(0, 0)
            steps(dve, emit)
            for part in range(3):
                finish(B - 1, part)

        @block.tensor
        def _(pe):
            def turn_comb(b):
                for s in range(TB):
                    ins = nc.tensor.transpose(turned[b][:, s * P:(s + 1) * P], cparts[:, b * TB + s, :], ident16[:])
                ins.then_inc(c_ready, 1)

            for s in range(TB):
                cols = slice(s * P, (s + 1) * P)
                for k in range(KT):
                    ins = products(nc, y_ps[:, s, :], (t["attT_hi"][:, k, cols], t["attT_lo"][:, k, cols]),
                                   (t["wo_hi"][:, k, :], t["wo_lo"][:, k, :]), k == 0, k == KT - 1)
            ins.then_inc(wo_ready, 1)
            pe.wait_ge(cparts_ready, 1)
            for b in range(B - 1):
                turn_comb(b)
            pe.wait_ge(select_in, 16)
            pe.wait_ge(comb_copied, B - 1)

            def gate_up(chunk, k):
                par, b, j = place(chunk, k)
                tile = chunk * CH + k // BC * CH + j
                batch = slice(b * S, (b + 1) * S)
                if b == 0:
                    pe.wait_ge(wlo_done, tile + 1)
                if first(chunk) and k == (B - 1) * CH:
                    pe.wait_ge(comb_copied, B)
                nc.tensor.matmul(comb_ps[:, k % 2, :], select[:, bass.ds(tile, 1), :].rearrange("p o n -> p (o n)"),
                                 combT[:, batch], start=True, stop=True)
                for half, ps in ((0, gate_ps), (1, up_ps)):
                    for c in range(KT):
                        cols = slice((half * KT + c) * P, (half * KT + c + 1) * P)
                        ins = products(nc, ps[:, k % 2, :], (w_hi[:, par, j, cols], w_lo[:, par, j, cols]),
                                       (t["x2T_hi"][:, c, batch], t["x2T_lo"][:, c, batch]), c == 0, c == KT - 1)
                    ins.then_inc(up_ready if half else gate_ready, 1)

            def emit(chunk, k):
                par, b, j = place(chunk, k)
                if first(chunk) and k == TURN2:
                    pe.wait_ge(fm_normed, 1)
                    pe.wait_ge(y_added, 2)
                    x2_ps = y_ps[:].rearrange("p (c s) n -> p c (s n)", c=KT)
                    for s in range(TB):
                        for c in range(KT):
                            ins = nc.tensor.transpose(x2_ps[:, c, s * P:(s + 1) * P], mix[:, s, c * P:(c + 1) * P],
                                                      ident[:])
                    ins.then_inc(x2_turned, 1)
                if not is_last(chunk, k):
                    gate_up(chunk, k + 1)
                if first(chunk) and k == TURN2:
                    pe.wait_ge(x2_lo, 1)
                    log_ps = y_ps[:, 0:2, :].rearrange("p s n -> p (s n)")
                    for c in range(KT):
                        ins = products(nc, log_ps, (t["gw_hi"][:, c, :], t["gw_lo"][:, c, :]),
                                       (t["x2T_hi"][:, c, last_cols], t["x2T_lo"][:, c, last_cols]), c == 0, c == KT - 1)
                    ins.then_inc(logT_ready, 1)
                    pe.wait_ge(logT_copied, 1)
                    turned_ps = y_ps[:, 2:4, :].rearrange("p s n -> p (s n)")
                    for s in range(TB):
                        ins = nc.tensor.transpose(turned_ps[:, s * P:(s + 1) * P], logT[:, s * P:(s + 1) * P], ident[:])
                    ins.then_inc(logit_turned, 1)
                    pe.wait_ge(logit_ready, 1)
                pe.wait_ge(hid_lo_done, chunk * BC + k + 1)
                if first(chunk) and k == TURN_COMB:
                    pe.wait_ge(cparts_ready, 2)
                    turn_comb(B - 1)
                if j == 0:
                    pe.wait_ge(y_added, chunk * B + k // CH + 1)
                    if first(chunk) and k == 0:
                        pe.wait_ge(mix_copied, 1)
                for s in range(TB):
                    cols = slice(s * P, (s + 1) * P)
                    for i, (l, r) in enumerate(((hid_hi, w_hi), (hid_hi, w_lo), (hid_lo, w_hi))):
                        ins = nc.tensor.matmul(y_ps[:, s, :], l[:, k % 2, cols], r[:, par, j, GU:GU + D],
                                               start=(j == 0 and i == 0 and s % 2 == 0), stop=(j == CH - 1 and i == 2),
                                               skip_group_check=True)
                ins.then_inc(down_done, 1)

            gate_up(0, 0)
            steps(pe, emit)


def build(nc, x, wqkv, wo, gw, rope, w, sel, out):
    with ExitStack() as ctx:
        t = {
            "x": ctx.enter_context(nc.sbuf_tensor("x_all", [P, NT, D], F32)),
            "x2T_hi": ctx.enter_context(nc.sbuf_tensor("x2T_hi", [P, KT, B * S], F32R)),
            "x2T_lo": ctx.enter_context(nc.sbuf_tensor("x2T_lo", [P, KT, B * S], F32R)),
            "ident": ctx.enter_context(nc.sbuf_tensor("ident", [P, P], F32)),
            "ident16": ctx.enter_context(nc.sbuf_tensor("ident16", [P, P], BF16)),
            "logit": ctx.enter_context(nc.sbuf_tensor("logit", [P, NT, GC], F32)),
        }
        for name, cols in (("attT", S), ("wo", D), ("gw", P)):
            for part in ("_hi", "_lo"):
                t[name + part] = ctx.enter_context(nc.sbuf_tensor(name + part, [P, KT, cols], F32R))
        attention_block(nc, t, x, wqkv, wo, gw, rope)
        ffn_block(nc, t, w, sel, out)


def kernel(L0_attn_x, L0_attn_Wq, L0_attn_Wk, L0_attn_Wv, L0_attn_Wo, L0_ffn_gate_w, L0_ffn_expert_gate_up,
           L0_ffn_expert_down, L0_ffn_shared_gate_up, L0_ffn_shared_down, L0_ffn_shared_gate_vec):
    import numpy as np
    import concourse.bacc as bacc
    from concourse.bass_utils import run_bass_kernel_spmd

    def tiles_of_rows(a, n):
        return np.ascontiguousarray(a.reshape(n, P, -1).transpose(1, 0, 2))

    x = tiles_of_rows(np.asarray(L0_attn_x).reshape(B * S, D), NT)
    wqkv = tiles_of_rows(np.concatenate([np.asarray(L0_attn_Wq).T, np.asarray(L0_attn_Wk).T,
                                         np.asarray(L0_attn_Wv).T], axis=1), KT)
    wo = tiles_of_rows(np.asarray(L0_attn_Wo).T, KT)
    gw = np.zeros((D, P), np.float32)
    gw[:, 0:E] = np.asarray(L0_ffn_gate_w).T
    gw[:, E:GC] = np.asarray(L0_ffn_shared_gate_vec).T
    gw = tiles_of_rows(gw, KT)

    inv = np.float32(10000.0) ** (-np.arange(0, DH, 2, dtype=np.float32) / np.float32(DH))
    angle = np.arange(S, dtype=np.float32)[:, None] * inv[None, :]
    cos = np.repeat(np.cos(angle), 2, axis=1)
    sin = np.repeat(np.sin(angle), 2, axis=1)
    sin[:, 0::2] = -sin[:, 0::2]
    rope = np.ascontiguousarray(np.stack([cos, sin], 1).reshape(TB, P, 2, DH).transpose(1, 0, 2, 3)).astype(np.float32)

    def inner(gate_up, n):
        return gate_up.reshape(-1, 2, n, D)
    eg = inner(np.asarray(L0_ffn_expert_gate_up), I)
    sg = inner(np.asarray(L0_ffn_shared_gate_up), SI)
    fill = np.zeros((FT * P - E * I - SI, D), np.float32)
    w = []
    for part in range(2):
        rows = np.concatenate([eg[:, part].reshape(E * I, D), sg[:, part].reshape(SI, D), fill])
        w.append(rows.reshape(FT, P, KT, P).transpose(0, 3, 2, 1).reshape(FT, P, KT * P))
    down = np.concatenate([np.asarray(L0_ffn_expert_down).transpose(0, 2, 1).reshape(E * I, D),
                           np.asarray(L0_ffn_shared_down).T, fill])
    w.append(down.reshape(FT, P, D))
    w = np.ascontiguousarray(np.concatenate(w, axis=2))

    owner = np.minimum(np.arange(FT * P) // I, E)
    sel = np.zeros((P, FT * P), np.float32)
    for m in range(MR):
        sel[m * GC + owner, np.arange(FT * P)] = 1.0
    sel = sel.reshape(P, FT, P).astype(np.dtype("bfloat16"))

    nc = bacc.Bacc("TRN2", target_bir_lowering=False, num_devices=1)
    arrays, args = {}, {}
    for name, a in (("x", x), ("wqkv", wqkv), ("wo", wo), ("gw", gw), ("rope", rope), ("w", w), ("sel", sel)):
        arrays[f"in_{name}_dram"] = a
        args[name] = nc.dram_tensor(f"in_{name}_dram", a.shape, mybir.dt.from_np(a.dtype), kind="ExternalInput").ap()
    out = nc.dram_tensor("out_dram", (P, NT, D), F32, kind="ExternalOutput").ap()
    build(nc, out=out, **args)
    r = run_bass_kernel_spmd(nc, [arrays], core_ids=[0])
    got = np.asarray(r.results[0]["out_dram"])
    return np.ascontiguousarray(got.transpose(1, 0, 2)).reshape(B, S, D)
```
